# Optimizing a Trainium2 kernel written in Bass

```python
import numpy as np
import jax
import jax.numpy as jnp

def _softmax(x, axis=-1):
    return jax.nn.softmax(x, axis=axis)

def _gelu(x):
    return jax.nn.gelu(x, approximate=True)

def _silu(x):
    return jax.nn.silu(x)

def _sigmoid(x):
    return jax.nn.sigmoid(x)

def _layernorm(x, axis=-1, eps=1e-05):
    m = jnp.mean(x, axis=axis, keepdims=True)
    v = jnp.var(x, axis=axis, keepdims=True)
    return (x - m) / jnp.sqrt(v + eps)

def _scatter_add(tgt, idx, src, axis=0):
    return tgt.at[idx].add(src)

def _segment_sum(src, seg, n):
    return jax.ops.segment_sum(src, seg, n)
kernel_name = 'mk_decoder_postln_d2_seqx_r4_d037ef'

def setup_inputs(seed: int=0):
    np.random.seed(seed)
    _w = jnp.asarray

    def _rec_inputs():
        import jax
        import jax.numpy as jnp
        _rk = jax.random.key(seed)
        x = -0.0002928 + 1 * jax.random.normal(jax.random.fold_in(_rk, 1), (8, 512, 256), jnp.float32)
        _lenS = 512 - jax.random.randint(jax.random.fold_in(_rk, 7), (8,), 0, max(1, 512 // 4) + 1, jnp.int32)
        _lenS2 = 64 - jax.random.randint(jax.random.fold_in(_rk, 8), (8,), 0, max(1, 64 // 4) + 1, jnp.int32)
        _ctx_1024P = jax.random.normal(jax.random.fold_in(_rk, 11), (8, 16, 256), jnp.float32)
        _ctx_1024c = jax.random.dirichlet(jax.random.fold_in(_rk, 511), 0.3 * jnp.ones((16,), jnp.float32), (8, 64))
        _ctx_1024t = jnp.einsum('bsk,bkd->bsd', _ctx_1024c, _ctx_1024P)
        _ctx_1024t = _ctx_1024t * jax.lax.rsqrt(jnp.mean(jnp.square(_ctx_1024t)) + 1e-12) * 0.953939
        ctx_1024 = -1.39393e-06 + 0.999914 * (_ctx_1024t + 0.3 * jax.random.normal(jax.random.fold_in(_rk, 611), (8, 64, 256), jnp.float32))
        _validS = jnp.arange(512)[None, :] < _lenS[:, None]
        _validS2 = jnp.arange(64)[None, :] < _lenS2[:, None]
        _causal = jnp.tril(jnp.ones((512, 512), dtype=bool))
        mask_BxSxS2_ik1 = jnp.where(jnp.broadcast_to(_validS2[:, None, :], (8, 512, 64)), 1, 0).astype(jnp.int32)
        return (x, ctx_1024, mask_BxSxS2_ik1)
    x, ctx_1024, mask_BxSxS2_ik1 = _rec_inputs()

    def _L0_attn_setup():
        import jax, jax.numpy as jnp
        import numpy as np
        import math
        B, S, D = (4, 512, 256)
        H = 16
        HD = D // H
        DL = 64
        LAMBDA_DECAY = 0.01
        key = jax.random.key(seed)
        ks = jax.random.split(key, 8)
        sc = lambda fan_in: 1.0 / math.sqrt(fan_in)
        return {'x': jax.random.normal(ks[0], (B, S, D), dtype=jnp.float32), 'W_q': jax.random.normal(ks[1], (D, D), dtype=jnp.float32) * sc(D), 'W_k': jax.random.normal(ks[2], (D, D), dtype=jnp.float32) * sc(D), 'W_v': jax.random.normal(ks[3], (D, D), dtype=jnp.float32) * sc(D), 'W_o': jax.random.normal(ks[4], (D, D), dtype=jnp.float32) * sc(D), 'W_down_kv': jax.random.normal(ks[5], (D, DL), dtype=jnp.float32) * sc(D), 'W_up_k': jax.random.normal(ks[6], (DL, D), dtype=jnp.float32) * sc(DL), 'W_up_v': jax.random.normal(ks[7], (DL, D), dtype=jnp.float32) * sc(DL)}
    _L0_attn_all = _L0_attn_setup()
    _L0_attn_in = {k: v for k, v in _L0_attn_all.items() if k in ('W_q', 'W_k', 'W_v', 'W_o', 'W_down_kv', 'W_up_k', 'W_up_v')}
    del _L0_attn_all

    def _L0_xattn_setup():
        import jax, jax.numpy as jnp
        import numpy as np
        N_HEADS = 16
        NEG_BIAS = -1000000000.0

        def _split_heads(x):
            B, S, D = x.shape
            return x.reshape(B, S, N_HEADS, D // N_HEADS).transpose(0, 2, 1, 3)
        key = jax.random.key(seed)
        k1, k2, k3, k4 = jax.random.split(key, 4)
        B, S, D = (2, 512, 256)
        queries = jax.random.normal(k1, (B, S, D), dtype=jnp.float32)
        keys = jax.random.normal(k2, (B, S, D), dtype=jnp.float32)
        values = jax.random.normal(k3, (B, S, D), dtype=jnp.float32)
        mask = jax.random.randint(k4, (B, S, S), 0, 2, dtype=jnp.int32)
        return {'queries': queries, 'keys': keys, 'values': values, 'mask': mask}
    _L0_xattn_all = _L0_xattn_setup()
    _L0_xattn_in = {k: v for k, v in _L0_xattn_all.items() if k in ()}
    del _L0_xattn_all

    def _L0_ffn_setup():
        import jax, jax.numpy as jnp
        import numpy as np
        D_MODEL = 256
        EXPANSION = 4
        D_HIDDEN = D_MODEL * EXPANSION
        NUM_STAGES = int(np.log2(D_HIDDEN))

        def butterfly(y, weights, dim):
            lead = y.shape[:-1]
            for stage in range(weights.shape[0]):
                s = 2 ** stage
                nb = dim // (2 * s)
                yr = y.reshape(*lead, nb, 2, s)
                a = yr[..., 0, :]
                b = yr[..., 1, :]
                w = weights[stage].reshape(nb, s, 2, 2)
                na = w[..., 0, 0] * a + w[..., 0, 1] * b
                nb2 = w[..., 1, 0] * a + w[..., 1, 1] * b
                y = jnp.stack([na, nb2], axis=-2).reshape(*lead, dim)
            return y
        key = jax.random.key(seed)
        ks = jax.random.split(key, 6)
        B, S = (4, 512)
        x = jax.random.normal(ks[0], (B, S, D_MODEL), jnp.float32)
        W_exp = jax.random.normal(ks[1], (D_MODEL, D_HIDDEN), jnp.float32) * 0.02
        b_exp = jnp.zeros((D_HIDDEN,), jnp.float32)
        up_weights = jax.random.normal(ks[2], (NUM_STAGES, D_HIDDEN // 2, 2, 2), jnp.float32) * 0.02
        up_bias = jnp.zeros((D_HIDDEN,), jnp.float32)
        down_weights = jax.random.normal(ks[3], (NUM_STAGES, D_HIDDEN // 2, 2, 2), jnp.float32) * 0.02
        W_con = jax.random.normal(ks[4], (D_HIDDEN, D_MODEL), jnp.float32) * 0.02
        b_con = jnp.zeros((D_MODEL,), jnp.float32)
        down_bias = jnp.zeros((D_MODEL,), jnp.float32)
        return dict(x=x, W_exp=W_exp, b_exp=b_exp, up_weights=up_weights, up_bias=up_bias, down_weights=down_weights, W_con=W_con, b_con=b_con, down_bias=down_bias)
    _L0_ffn_all = _L0_ffn_setup()
    _L0_ffn_in = {k: v for k, v in _L0_ffn_all.items() if k in ('W_exp', 'b_exp', 'up_weights', 'up_bias', 'down_weights', 'W_con', 'b_con', 'down_bias')}
    del _L0_ffn_all

    def _L1_attn_setup():
        import jax, jax.numpy as jnp
        import numpy as np
        N_HEADS = 16
        HEAD_DIM = 64
        ROPE_THETA = 10000.0

        def _rope_cos_sin(seq_len, dim, theta):
            inv_freq = 1.0 / theta ** (jnp.arange(0, dim, 2, dtype=jnp.float32) / dim)
            pos = jnp.arange(seq_len, dtype=jnp.float32)
            freqs = pos[:, None] * inv_freq[None, :]
            emb = jnp.concatenate([freqs, freqs], axis=-1)
            return (jnp.cos(emb), jnp.sin(emb))

        def _rotate_half(x):
            d = x.shape[-1] // 2
            return jnp.concatenate([-x[..., d:], x[..., :d]], axis=-1)
        key = jax.random.key(seed)
        ks = jax.random.split(key, 6)
        B, S, D_MODEL, LATENT = (1, 1024, 256, 128)
        q_dim = N_HEADS * HEAD_DIM
        sd = lambda fan_in: 1.0 / np.sqrt(fan_in)
        return {'x': jax.random.normal(ks[0], (B, S, D_MODEL), jnp.float32), 'wq': jax.random.normal(ks[1], (q_dim, D_MODEL), jnp.float32) * sd(D_MODEL), 'w_kv_down': jax.random.normal(ks[2], (LATENT, D_MODEL), jnp.float32) * sd(D_MODEL), 'w_k_up': jax.random.normal(ks[3], (q_dim, LATENT), jnp.float32) * sd(LATENT), 'w_v_up': jax.random.normal(ks[4], (q_dim, LATENT), jnp.float32) * sd(LATENT), 'wo': jax.random.normal(ks[5], (D_MODEL, q_dim), jnp.float32) * sd(q_dim)}
    _L1_attn_all = _L1_attn_setup()
    _L1_attn_in = {k: v for k, v in _L1_attn_all.items() if k in ('wq', 'w_kv_down', 'w_k_up', 'w_v_up', 'wo')}
    del _L1_attn_all

    def _L1_xattn_setup():
        import jax, jax.numpy as jnp
        import numpy as np
        HEADS = 8
        DIM_HEAD = 64
        key = jax.random.key(seed)
        ks = jax.random.split(key, 9)
        B, N1, N2, D = (4, 512, 512, 256)
        inner = HEADS * DIM_HEAD
        s_in = 1.0 / np.sqrt(D)
        s_inner = 1.0 / np.sqrt(inner)
        return {'x1': jax.random.normal(ks[0], (B, N1, D), jnp.float32), 'x2': jax.random.normal(ks[1], (B, N2, D), jnp.float32), 'Wq1': jax.random.normal(ks[2], (D, inner), jnp.float32) * s_in, 'Wk1': jax.random.normal(ks[3], (D, inner), jnp.float32) * s_in, 'Wv1': jax.random.normal(ks[4], (D, inner), jnp.float32) * s_in, 'Wk2': jax.random.normal(ks[5], (D, inner), jnp.float32) * s_in, 'Wv2': jax.random.normal(ks[6], (D, inner), jnp.float32) * s_in, 'Wo': jax.random.normal(ks[7], (inner, D), jnp.float32) * s_inner, 'bo': jnp.zeros((D,), jnp.float32)}
    _L1_xattn_all = _L1_xattn_setup()
    _L1_xattn_in = {k: v for k, v in _L1_xattn_all.items() if k in ('Wq1', 'Wk1', 'Wv1', 'Wk2', 'Wv2', 'Wo', 'bo')}
    del _L1_xattn_all

    def _L1_ffn_setup():
        import jax, jax.numpy as jnp
        import numpy as np
        E = 8
        K = 2
        D = 256
        H = 4 * D
        EPS = 1e-05
        TEMP = 1.5
        key = jax.random.key(seed)
        ks = jax.random.split(key, 6)
        B, T = (2, 512)
        x = jax.random.normal(ks[0], (B, T, D), dtype=jnp.float32)
        gamma = jnp.ones((D,), dtype=jnp.float32)
        beta = jnp.zeros((D,), dtype=jnp.float32)
        router_w = jax.random.normal(ks[1], (E, D), dtype=jnp.float32) * 0.02
        W1 = jax.random.normal(ks[2], (E, D, H), dtype=jnp.float32) * 0.02
        W2 = jax.random.normal(ks[3], (E, H, D), dtype=jnp.float32) * 0.02
        return {'x': x, 'gamma': gamma, 'beta': beta, 'router_w': router_w, 'W1': W1, 'W2': W2}
    _L1_ffn_all = _L1_ffn_setup()
    _L1_ffn_in = {k: v for k, v in _L1_ffn_all.items() if k in ('gamma', 'beta', 'router_w', 'W1', 'W2')}
    del _L1_ffn_all
    return {'x': x, 'ctx_1024': ctx_1024, 'mask_BxSxS2_ik1': mask_BxSxS2_ik1, 'L0_attn_W_q': _L0_attn_in['W_q'], 'L0_attn_W_k': _L0_attn_in['W_k'], 'L0_attn_W_v': _L0_attn_in['W_v'], 'L0_attn_W_o': _L0_attn_in['W_o'], 'L0_attn_W_down_kv': _L0_attn_in['W_down_kv'], 'L0_attn_W_up_k': _L0_attn_in['W_up_k'], 'L0_attn_W_up_v': _L0_attn_in['W_up_v'], 'L0_ffn_W_exp': _L0_ffn_in['W_exp'], 'L0_ffn_b_exp': _L0_ffn_in['b_exp'], 'L0_ffn_up_weights': _L0_ffn_in['up_weights'], 'L0_ffn_up_bias': _L0_ffn_in['up_bias'], 'L0_ffn_down_weights': _L0_ffn_in['down_weights'], 'L0_ffn_W_con': _L0_ffn_in['W_con'], 'L0_ffn_b_con': _L0_ffn_in['b_con'], 'L0_ffn_down_bias': _L0_ffn_in['down_bias'], 'L1_attn_wq': _L1_attn_in['wq'], 'L1_attn_w_kv_down': _L1_attn_in['w_kv_down'], 'L1_attn_w_k_up': _L1_attn_in['w_k_up'], 'L1_attn_w_v_up': _L1_attn_in['w_v_up'], 'L1_attn_wo': _L1_attn_in['wo'], 'L1_xattn_Wq1': _L1_xattn_in['Wq1'], 'L1_xattn_Wk1': _L1_xattn_in['Wk1'], 'L1_xattn_Wv1': _L1_xattn_in['Wv1'], 'L1_xattn_Wk2': _L1_xattn_in['Wk2'], 'L1_xattn_Wv2': _L1_xattn_in['Wv2'], 'L1_xattn_Wo': _L1_xattn_in['Wo'], 'L1_xattn_bo': _L1_xattn_in['bo'], 'L1_ffn_gamma': _L1_ffn_in['gamma'], 'L1_ffn_beta': _L1_ffn_in['beta'], 'L1_ffn_router_w': _L1_ffn_in['router_w'], 'L1_ffn_W1': _L1_ffn_in['W1'], 'L1_ffn_W2': _L1_ffn_in['W2']}

def reference(x, ctx_1024, mask_BxSxS2_ik1, L0_attn_W_q, L0_attn_W_k, L0_attn_W_v, L0_attn_W_o, L0_attn_W_down_kv, L0_attn_W_up_k, L0_attn_W_up_v, L0_ffn_W_exp, L0_ffn_b_exp, L0_ffn_up_weights, L0_ffn_up_bias, L0_ffn_down_weights, L0_ffn_W_con, L0_ffn_b_con, L0_ffn_down_bias, L1_attn_wq, L1_attn_w_kv_down, L1_attn_w_k_up, L1_attn_w_v_up, L1_attn_wo, L1_xattn_Wq1, L1_xattn_Wk1, L1_xattn_Wv1, L1_xattn_Wk2, L1_xattn_Wv2, L1_xattn_Wo, L1_xattn_bo, L1_ffn_gamma, L1_ffn_beta, L1_ffn_router_w, L1_ffn_W1, L1_ffn_W2):
    import jax
    import jax.numpy as jnp

    def _L0_attn_ref(x, W_q, W_k, W_v, W_o, W_down_kv, W_up_k, W_up_v):
        import jax, jax.numpy as jnp
        import numpy as np
        import math
        B, S, D = (4, 512, 256)
        H = 16
        HD = D // H
        DL = 64
        LAMBDA_DECAY = 0.01
        b, s, d = x.shape
        q = x @ W_q
        k = x @ W_k
        v = x @ W_v
        latent_kv = (k + v) @ W_down_kv
        k_rec = (latent_kv @ W_up_k).reshape(b, s, H, HD).transpose(0, 2, 1, 3)
        v_rec = (latent_kv @ W_up_v).reshape(b, s, H, HD).transpose(0, 2, 1, 3)
        qh = q.reshape(b, s, H, HD).transpose(0, 2, 1, 3)
        scores = jnp.einsum('bhqd,bhkd->bhqk', qh, k_rec) / math.sqrt(d)
        t = jnp.arange(s, dtype=jnp.float32)
        decay = jnp.exp(-LAMBDA_DECAY * jnp.abs(t[:, None] - t[None, :]))
        scores = scores * decay[None, None, :, :]
        attn = jax.nn.softmax(scores, axis=-1)
        out = jnp.einsum('bhqk,bhkd->bhqd', attn, v_rec)
        out = out.transpose(0, 2, 1, 3).reshape(b, s, d)
        return out @ W_o

    def _L0_xattn_ref(queries, keys, values, mask):
        import jax, jax.numpy as jnp
        import numpy as np
        N_HEADS = 16
        NEG_BIAS = -1000000000.0

        def _split_heads(x):
            B, S, D = x.shape
            return x.reshape(B, S, N_HEADS, D // N_HEADS).transpose(0, 2, 1, 3)
        q = _split_heads(queries)
        k = _split_heads(keys)
        v = _split_heads(values)
        d_head = q.shape[-1]
        sim = jnp.einsum('bhqd,bhkd->bhqk', q, k) / jnp.sqrt(jnp.float32(d_head))
        bias = NEG_BIAS * (1.0 - mask.astype(sim.dtype))[:, None]
        sim = sim + bias
        weights = jax.nn.softmax(sim, axis=-1)
        out = jnp.einsum('bhqk,bhkd->bhqd', weights, v)
        B, H, Sq, d = out.shape
        return out.transpose(0, 2, 1, 3).reshape(B, Sq, H * d)

    def _L0_ffn_ref(x, W_exp, b_exp, up_weights, up_bias, down_weights, W_con, b_con, down_bias):
        import jax, jax.numpy as jnp
        import numpy as np
        D_MODEL = 256
        EXPANSION = 4
        D_HIDDEN = D_MODEL * EXPANSION
        NUM_STAGES = int(np.log2(D_HIDDEN))

        def butterfly(y, weights, dim):
            lead = y.shape[:-1]
            for stage in range(weights.shape[0]):
                s = 2 ** stage
                nb = dim // (2 * s)
                yr = y.reshape(*lead, nb, 2, s)
                a = yr[..., 0, :]
                b = yr[..., 1, :]
                w = weights[stage].reshape(nb, s, 2, 2)
                na = w[..., 0, 0] * a + w[..., 0, 1] * b
                nb2 = w[..., 1, 0] * a + w[..., 1, 1] * b
                y = jnp.stack([na, nb2], axis=-2).reshape(*lead, dim)
            return y
        h = jnp.einsum('bsd,dh->bsh', x, W_exp) + b_exp
        h = butterfly(h, up_weights, D_HIDDEN)
        h = jax.nn.gelu(h + up_bias, approximate=False)
        h = butterfly(h, down_weights, D_HIDDEN)
        y = jnp.einsum('bsh,hd->bsd', h, W_con) + b_con
        return y + down_bias

    def _L1_attn_ref(x, wq, w_kv_down, w_k_up, w_v_up, wo):
        import jax, jax.numpy as jnp
        import numpy as np
        N_HEADS = 16
        HEAD_DIM = 64
        ROPE_THETA = 10000.0

        def _rope_cos_sin(seq_len, dim, theta):
            inv_freq = 1.0 / theta ** (jnp.arange(0, dim, 2, dtype=jnp.float32) / dim)
            pos = jnp.arange(seq_len, dtype=jnp.float32)
            freqs = pos[:, None] * inv_freq[None, :]
            emb = jnp.concatenate([freqs, freqs], axis=-1)
            return (jnp.cos(emb), jnp.sin(emb))

        def _rotate_half(x):
            d = x.shape[-1] // 2
            return jnp.concatenate([-x[..., d:], x[..., :d]], axis=-1)
        B, S, _ = x.shape
        H, D = (N_HEADS, HEAD_DIM)
        q = jnp.einsum('bsd,qd->bsq', x, wq).reshape(B, S, H, D).transpose(0, 2, 1, 3)
        kv_latent = jnp.einsum('bsd,ld->bsl', x, w_kv_down)
        k = jnp.einsum('bsl,ql->bsq', kv_latent, w_k_up).reshape(B, S, H, D).transpose(0, 2, 1, 3)
        v = jnp.einsum('bsl,ql->bsq', kv_latent, w_v_up).reshape(B, S, H, D).transpose(0, 2, 1, 3)
        cos, sin = _rope_cos_sin(S, D, ROPE_THETA)
        cos = cos[None, None]
        sin = sin[None, None]
        q = q * cos + _rotate_half(q) * sin
        k = k * cos + _rotate_half(k) * sin
        scores = jnp.einsum('bhsd,bhtd->bhst', q, k) / jnp.sqrt(jnp.float32(D))
        causal = jnp.triu(jnp.full((S, S), -jnp.inf, dtype=jnp.float32), k=1)
        scores = scores + causal[None, None]
        probs = jax.nn.softmax(scores.astype(jnp.float32), axis=-1).astype(q.dtype)
        out = jnp.einsum('bhst,bhtd->bhsd', probs, v)
        out = out.transpose(0, 2, 1, 3).reshape(B, S, H * D)
        return jnp.einsum('bsq,dq->bsd', out, wo)

    def _L1_xattn_ref(x1, x2, Wq1, Wk1, Wv1, Wk2, Wv2, Wo, bo):
        import jax, jax.numpy as jnp
        import numpy as np
        HEADS = 8
        DIM_HEAD = 64
        h, d = (HEADS, DIM_HEAD)
        scale = d ** (-0.5)
        B, N1, _ = x1.shape
        N2 = x2.shape[1]

        def split_heads(t, n):
            return t.reshape(B, n, h, d)
        q1 = split_heads(x1 @ Wq1, N1)
        k1 = split_heads(x1 @ Wk1, N1)
        v1 = split_heads(x1 @ Wv1, N1)
        k2 = split_heads(x2 @ Wk2, N2)
        v2 = split_heads(x2 @ Wv2, N2)
        k = jnp.concatenate([k1, k2], axis=1)
        v = jnp.concatenate([v1, v2], axis=1)
        sim = jnp.einsum('bihd,bjhd->bhij', q1.astype(jnp.float32), k.astype(jnp.float32)) * scale
        attn = jax.nn.softmax(sim, axis=-1)
        out = jnp.einsum('bhij,bjhd->bihd', attn, v)
        out = out.reshape(B, N1, h * d)
        return out @ Wo + bo

    def _L1_ffn_ref(x, gamma, beta, router_w, W1, W2):
        import jax, jax.numpy as jnp
        import numpy as np
        E = 8
        K = 2
        D = 256
        H = 4 * D
        EPS = 1e-05
        TEMP = 1.5
        res = x
        mu = jnp.mean(x, axis=-1, keepdims=True)
        var = jnp.mean(jnp.square(x - mu), axis=-1, keepdims=True)
        xn = (x - mu) * jax.lax.rsqrt(var + EPS) * gamma + beta
        logits = jnp.einsum('btd,ed->bte', xn, router_w)
        probs = jax.nn.softmax(logits / TEMP, axis=-1)
        w, idx = jax.lax.top_k(probs, K)
        wdense = jnp.sum(jax.nn.one_hot(idx, E, dtype=w.dtype) * w[..., None], axis=-2)
        h = jax.nn.silu(jnp.einsum('btd,edf->betf', xn, W1))
        y = jnp.einsum('betf,efd->betd', h, W2)
        out = jnp.einsum('bte,betd->btd', wdense, y)
        return out + res
    x = _layernorm(x + _L0_attn_ref(x, L0_attn_W_q, L0_attn_W_k, L0_attn_W_v, L0_attn_W_o, L0_attn_W_down_kv, L0_attn_W_up_k, L0_attn_W_up_v), axis=-1)
    x = _layernorm(x + _L0_xattn_ref(x, ctx_1024, ctx_1024, mask_BxSxS2_ik1), axis=-1)
    x = _layernorm(x + _L0_ffn_ref(x, L0_ffn_W_exp, L0_ffn_b_exp, L0_ffn_up_weights, L0_ffn_up_bias, L0_ffn_down_weights, L0_ffn_W_con, L0_ffn_b_con, L0_ffn_down_bias), axis=-1)
    x = _layernorm(x + _L1_attn_ref(x, L1_attn_wq, L1_attn_w_kv_down, L1_attn_w_k_up, L1_attn_w_v_up, L1_attn_wo), axis=-1)
    x = _layernorm(x + _L1_xattn_ref(x, ctx_1024, L1_xattn_Wq1, L1_xattn_Wk1, L1_xattn_Wv1, L1_xattn_Wk2, L1_xattn_Wv2, L1_xattn_Wo, L1_xattn_bo), axis=-1)
    x = _layernorm(x + _L1_ffn_ref(x, L1_ffn_gamma, L1_ffn_beta, L1_ffn_router_w, L1_ffn_W1, L1_ffn_W2), axis=-1)
    return x

_drawn_inputs = setup_inputs


def setup_inputs(seed=0):
    import zlib

    import numpy as np

    out = dict(_drawn_inputs(seed))
    spreads = {'L0_ffn_b_exp': (0.0, 0.1),
     'L0_ffn_up_bias': (0.0, 0.1),
     'L0_ffn_b_con': (0.0, 0.1),
     'L0_ffn_down_bias': (0.0, 0.1),
     'L1_xattn_bo': (0.0, 0.1),
     'L1_ffn_gamma': (1.0, 0.6),
     'L1_ffn_beta': (0.0, 0.8)}
    factors = {'L0_attn_W_q': 2.703,
     'L0_attn_W_up_k': 2.688,
     'L1_ffn_router_w': 5.345,
     'L1_ffn_W1': 4.534,
     'L1_ffn_W2': 4.486}
    for name, (base, spread) in spreads.items():
        noise = np.random.default_rng([zlib.crc32(name.encode()), seed]).standard_normal(out[name].shape)
        drawn = base * np.exp(spread * noise) if base else spread * noise
        out[name] = jnp.asarray(drawn.astype(out[name].dtype))
    for name, factor in factors.items():
        out[name] = (out[name] * factor).astype(out[name].dtype)
    return out
```

```python
from contextlib import ExitStack

import numpy as np

import concourse.bass as bass
from concourse import mybir

F32 = mybir.dt.float32
F32R = mybir.dt.float32r
I32 = mybir.dt.int32
U32 = mybir.dt.uint32
ALU = mybir.AluOpType
ACT = mybir.ActivationFunctionType
AX_X = mybir.AxisListType.X

P = 128
B, S, D = 8, 512, 256
SC = 64
QT = S // P
DT = D // P
FH = 4 * D
FT = FH // P
STAGES = 10
NE = 8
EPS = 1e-5
LOWEST = -3.0e38
A_BANKS = 4


class Env:

    def __init__(self, nc, ctx, prefix):
        self.nc, self.ctx, self.prefix = nc, ctx, prefix

    def sb(self, name, shape, dt=F32):
        return self.ctx.enter_context(self.nc.sbuf_tensor(f"{self.prefix}_{name}", shape, dt))

    def ps(self, name, shape, dt=F32):
        return self.ctx.enter_context(self.nc.psum_tensor(f"{self.prefix}_{name}", shape, dt))

    def sem(self, name):
        return self.ctx.enter_context(self.nc.semaphore(f"{self.prefix}_{name}"))


def wait_apart(eng, met, *waits):
    waits = [(sem, value if isinstance(value, int) else eng.to_reg(value)) for sem, value in waits]
    eng.wait_ge(*met)
    for sem, value in waits:
        eng.wait_ge(sem, value)


class Chain:

    def __init__(self, eng, sem, base, met):
        self.eng, self.sem, self.base, self.n, self.met = eng, sem, base, 0, met

    def link(self, ins):
        self.n += 1
        ins.then_inc(self.sem, 1)
        wait_apart(self.eng, self.met, (self.sem, self.base + self.n))


class Segment:

    def __init__(self, jobs, sems, base, last, n=A_BANKS):
        self.n, self.sems, self.base = n, sems, dict(base)
        self.number = {name: i for i, (name, _) in enumerate(jobs)}
        self.reader = dict(jobs)
        assert len(self.number) == len(jobs)
        self.per = {r: sum(x == r for _, x in jobs) for r in sems}
        self.per["full"] = len(jobs)
        self.count, self.before, last, seen = {}, {}, list(last), dict.fromkeys(sems, 0)
        for k, (name, r) in enumerate(jobs):
            seen[r] += 1
            self.count[name] = seen[r]
            self.before[name] = last[k % n]
            last[k % n] = (r, seen[r])
        self.end = {r: self.base[r] + self.per[r] for r in self.base}
        self.last = [(r, k - self.per[r]) for r, k in last]

    def bank(self, name):
        return self.number[name] % self.n

    def _at(self, r, turn, k):
        return self.sems[r], turn * self.per[r] + (self.base[r] + k)

    def full(self, turn, name):
        return self._at("full", turn, self.number[name] + 1)

    def empty(self, turn, name):
        return self._at(self.before[name][0], turn, self.before[name][1])

    def emptied(self, turn, name):
        return self._at(self.reader[name], turn, self.count[name])


def layer_norm_rows(nv, steps, row, stats, mv, scratch, to=None):
    to = to or row
    for qt in range(QT):
        ins = nv.bn_stats(stats[:, qt, :], row(qt))
    steps.link(ins)
    for qt in range(QT):
        ins = nv.bn_aggr(mv[:, qt, :], stats[:, qt, :])
    steps.link(ins)
    rsqrt_columns(nv, steps, mv[:, :, 1], scratch)
    for qt in range(QT):
        ins = nv.tensor_scalar(to(qt), row(qt), mv[:, qt, 0:1], scratch[:, 1, qt:qt + 1],
                               ALU.subtract, ALU.mult)
    steps.link(ins)


def rsqrt_columns(nv, steps, var, scratch):
    v, y, t = scratch[:, 0, :], scratch[:, 1, :], scratch[:, 2, :]
    steps.link(nv.tensor_scalar(v, var, EPS, None, ALU.add))
    steps.link(nv.tensor_scalar(t.bitcast(I32), v.bitcast(I32), 1, None, ALU.arith_shift_right))
    steps.link(nv.tensor_scalar(y.bitcast(I32), t.bitcast(I32), -1, 0x5F3759DF, ALU.mult, ALU.add))
    for _ in range(3):
        steps.link(nv.tensor_tensor(t, y, y, ALU.mult))
        steps.link(nv.scalar_tensor_tensor(out=t, in0=t, scalar=-0.5, in1=v, op0=ALU.mult, op1=ALU.mult))
        steps.link(nv.scalar_tensor_tensor(out=y, in0=t, scalar=1.5, in1=y, op0=ALU.add, op1=ALU.mult))


LN_LINKS = 3 + 3 + 3 * 3


class Shared:

    def __init__(self, nc, ctx):
        self.x_all = ctx.enter_context(nc.sbuf_tensor("x_all", [P, B * QT, D], F32))
        self.ident = ctx.enter_context(nc.sbuf_tensor("ident", [P, P], F32))


def load_block(nc, sh, x, ident):
    with ExitStack() as ctx:
        env = Env(nc, ctx, "load")
        loaded = env.sem("loaded")
        block = ctx.enter_context(nc.Block())

        @block.sync
        def _(sp):
            sp.dma_start(sh.ident[:], ident).then_inc(loaded, 16)
            sp.dma_start(sh.x_all[:, :, :], x.rearrange("b (q p) d -> p (b q) d", p=P)).then_inc(loaded, 16)
            sp.wait_ge(loaded, 32)


def attention(nc, sh, kind, w):
    a0, a1, x1 = kind == "a0", kind == "a1", kind == "x1"
    G = {"a0": 4, "a1": 4, "x1": 2}[kind]
    ITEMS = {"a0": 2, "a1": 4, "x1": 5}[kind]
    U = G * QT
    NK = S + SC if x1 else S
    PAIRS = 2 * G
    SCALE = 1.0 / 16.0 if a0 else 0.125
    LAG_E, LAG_N, LAG_T, LAG_V = 1, 2, 3, 4
    V_STEP, Y_STEP = 3, 5
    IN = FH if a1 else 512
    N_V = {"a0": 2, "a1": 2 * QT, "x1": QT + 1}[kind]

    def keys(u):
        return (u % QT + 1) * P if a1 else S

    def work_at(s):
        g, at = divmod(s, QT)
        spread = {"a0": ([0], [1], [], []), "a1": ([0], [1], [2, 3], []), "x1": ([0, 1], [2, 3], [4], [])}[kind]
        if g + 1 < G:
            return [("item", g + 1, i) for i in spread[at]]
        first = {"a0": ([], [0], [1], []), "a1": ([], [0], [1, 2], [3]), "x1": ([], [0, 1], [2, 3], [4])}[kind]
        return ([("xT",)] + ([("lat",)] if not x1 else []) if at == 0 else []) + \
            [("item", 0, i) for i in first[at]]

    START = [("xT",)] + ([("lat",)] if not x1 else []) + [("item", 0, i) for i in range(ITEMS)]

    def work_jobs(work):
        if work[0] == "xT":
            return [(("xT", dt), "xt") for dt in range(DT)]
        if work[0] == "lat":
            return [("lat", "act")]
        if a1:
            return [((*work, 0), "dve"), ((*work, 1), "rot")]
        if x1:
            return [(work, "ql")]
        return [(work, ("dve", "kl")[work[2]])]

    def segment_jobs(prev, own, nxt):
        jobs = []
        for s in range(U if own else Y_STEP + 1):
            if own:
                jobs += [(("score", s, j), "dve") for j in range(5 if x1 else 4)]
            if s == V_STEP and own:
                jobs += [(("v", i), "dve" if a0 else "v") for i in range(N_V)]
            if s == Y_STEP and prev:
                jobs += [(("y", qt), "dve") for qt in range(QT)]
            if own and (nxt or s < U - QT):
                for work in work_at(s):
                    jobs += work_jobs(work)
        return jobs

    T_UNIT = 5 if x1 else 4
    T_JOBS = U * T_UNIT
    T_CREDIT = 4 * T_UNIT
    N_O = 2 if a0 else 2 * G
    HI_GROUP = {"a0": 2, "a1": 6, "x1": 10}[kind]
    LOW_GROUP = {"a0": 4, "a1": 6, "x1": 0}[kind]
    LOW_ITEM = {"a1": (1, 3, 4, 6)}.get(kind)
    HI_ITEM = {"a0": (1, 2), "a1": (1, 3, 4, 6), "x1": (1, 2, 4, 6, 10)}[kind]

    with ExitStack() as ctx:
        env = Env(nc, ctx, kind)
        sb, sem = env.sb, env.sem
        xin = sb("xin", [P, QT, D])
        xT = sb("xT", [P, DT, S])
        widths = [4 * keys(u) if a1 else 4 * NK for u in range(4)]
        tiles = [12, 16] if a1 else [20 if x1 else 16] * 2
        t_buf = sb("t", [P, sum(widths)])
        p_T = sb("pT", [P, sum(tiles), P])
        mx = sb("mx", [P, 4, 4])
        mx1 = sb("mx1", [P, 4, 4])
        neg = sb("neg", [P, 4, 4])
        total = sb("total", [P, 4, 4])
        inv = sb("inv", [P, 4, 4])
        stats = sb("stats", [P, QT, 6])
        mv = sb("mv", [P, QT, 2])
        scratch = sb("scratch", [P, 3, QT])
        oT = sb("oT", [P, 2 if a0 else PAIRS, S])
        wo = sb("wo", [P, 2 if a0 else PAIRS, D])
        kpad = sb("kpad", [P, 2, 2, 4, NK], F32R)
        if a0:
            qs = sb("qs", [P, 2, S], F32R)
            kh = sb("kh", [P, S], F32R)
            kl = sb("kl", [P, S], F32R)
            lat = sb("lat", [64, S])
            v_sb = sb("v", [P, QT, 16, 32])
            wq = sb("wq", [P, DT, G, P])
            wkd = sb("wkd", [P, DT, 64])
            wupk = sb("wupk", [64, G, P])
            wupv = sb("wupv", [64, D])
            wkT = sb("wkT", [P, DT, D])
            wvT = sb("wvT", [P, DT, D])
            wdn = sb("wdn", [P, DT, 64])
            table = sb("decay", [P, 2 * S - P])
            hmask = sb("hmask", [P, 4])
        else:
            q_hl = sb("qhl", [P, 2, 2, 2, S], F32R)
            v_sb = sb("v", [P, QT, IN])
            wq = sb("wq", [P, DT, IN])
            table = sb("table", [P, S])
        if a1:
            wqs = sb("wqs", [P, DT, IN])
            lat = sb("lat", [P, S])
            wdn = sb("wdn", [P, DT, P])
            wupk = sb("wupk", [P, 2, IN])
            wupv = sb("wupv", [P, IN])
            cos = sb("cos", [P, S])
            sin = sb("sin", [P, S])
            rsum = sb("rsum", [P, 2, S])
            rsin = sb("rsin", [P, S])
        if x1:
            v2 = sb("v2", [SC, IN])
            ctxT = sb("ctxT", [P, DT, SC])
            wk1 = sb("wk1", [P, DT, IN])
            wv1 = sb("wv1", [P, DT, IN])
            wk2 = sb("wk2", [P, DT, IN])
            wv2 = sb("wv2", [P, DT, IN])
            bo = sb("bo", [1, D])
            ones = sb("ones", [1, P])

        A = [env.ps(f"A{i}", [P, 512]) for i in range(A_BANKS)]
        T = [env.ps(f"T{i}", [P, 4, P]) for i in range(2)]
        O = [env.ps(f"O{i}", [P, S]) for i in range(2)]

        weights = sem("weights")
        ready = sem("ready")
        folded = sem("folded")
        xin_in = sem("xin_in")
        ctx_in = sem("ctx_in")
        a_full = sem("a_full")
        a_act = sem("a_act")
        xt_done = sem("xt_done")
        v_done = sem("v_done")
        a_dve = sem("a_dve")
        hi = sem("hi")
        rot_sum = sem("rot_sum")
        kl_done = sem("kl_done")
        rot_done = sem("rot_done")
        low = sem("low")
        kp = sem("kp")
        negated = sem("negated")
        exped = sem("exped")
        normed = sem("normed")
        t_full = sem("t_full")
        t_empty = sem("t_empty")
        pv = sem("pv")
        o_empty = sem("o_empty")
        inverted = sem("inverted")
        q_low = sem("q_low")
        chain = sem("chain")
        sems = {"full": a_full, "act": a_act, "dve": a_dve, "xt": xt_done, "v": v_done,
                "kl": kl_done, "rot": rot_done, "ql": q_low}
        zero = dict.fromkeys(sems, 0) | {"dve": A_BANKS}
        start = Segment([j for work in START for j in work_jobs(work)], sems, zero,
                        [("dve", 0)] * A_BANKS)
        first = Segment(segment_jobs(False, True, True), sems, start.end, start.last)
        steady = Segment(segment_jobs(True, True, True), sems, first.end, first.last)
        assert steady.last == first.last
        looped = {r: steady.base[r] + (B - 2) * steady.per[r] for r in steady.base}
        final = Segment(segment_jobs(True, True, False), sems, looped, steady.last)
        tail = Segment(segment_jobs(True, False, False), sems, final.end, final.last)

        def batches(eng, begin, body):
            begin()
            body(first, 0, 0, prev=False, own=True, nxt=True)
            with eng.Fori(1, B - 1) as b:
                body(steady, b - 1, b, prev=True, own=True, nxt=True)
            body(final, 0, B - 1, prev=True, own=True, nxt=False)
            body(tail, 0, B, prev=True, own=False, nxt=False)

        def t_of(u, j, lo, hi):
            at = sum(widths[:u % 4]) + j * widths[u % 4] // 4
            return t_buf[:, at + lo:at + hi]

        def p_tile(u, j, kt, n=1):
            at = (u % 2) * tiles[0] + j * tiles[u % 2] // 4 + kt
            return p_T[:, at:at + n, :] if n > 1 else p_T[:, at, :]

        block = ctx.enter_context(nc.Block())

        def tiled(x):
            return x.rearrange("(t p) n -> p t n", p=P)

        loads = [(wo[:], tiled(w["w_o"]))]
        if a0:
            w_q = w["w_q"].rearrange("(t p) g c -> p t g c", p=P)
            for t in range(DT):
                loads += [(wq[:, t, :, 0:64], w_q[:, t]), (wq[:, t, :, 64:128], w_q[:, t])]
            loads += [(wkT[:], tiled(w["w_kT"])), (wvT[:], tiled(w["w_vT"])), (wdn[:], tiled(w["w_down"])),
                      (wupk[:, :, 0:64], w["w_up_k"]), (wupk[:, :, 64:128], w["w_up_k"]),
                      (wupv[:], w["w_up_v"]), (table[:], w["decay"]), (hmask[:], w["head_mask"])]
        if a1:
            loads += [(wq[:], tiled(w["w_q"])), (wqs[:], tiled(w["w_q_swapped"])), (wdn[:], tiled(w["w_down"])),
                      (wupk[:, 0, :], w["w_up_k"]), (wupk[:, 1, :], w["w_up_k_swapped"]),
                      (wupv[:], w["w_up_v"]), (table[:], w["causal"]), (cos[:], w["cos"]), (sin[:], w["sin"])]
        if x1:
            loads += [(wq[:], tiled(w["w_q"])), (wk1[:], tiled(w["w_k1"])), (wv1[:], tiled(w["w_v1"])),
                      (wk2[:], tiled(w["w_k2"])), (wv2[:], tiled(w["w_v2"])), (bo[:], w["b_o"])]
        N_READY = {"a0": 3, "a1": 1, "x1": 3}[kind]

        @block.sync
        def _(sp):
            sp.dma_start(xin[:], sh.x_all[:, 0:QT, :]).then_inc(xin_in, 16)
            for to, src in loads:
                sp.dma_start(to, src).then_inc(weights, 16)
            if x1:
                sp.dma_start(ctxT[:], tiled(w["ctxT"][0])).then_inc(ctx_in, 16)
            with sp.Fori(1, B) as b:
                sp.wait_ge(xt_done, b * DT)
                sp.dma_start(xin[:], sh.x_all[:, bass.ds(b * QT, QT), :]).then_inc(xin_in, 16)
                if x1:
                    sp.wait_ge(v_done, b * N_V)
                    sp.dma_start(ctxT[:], w["ctxT"][bass.ds(b, 1)].rearrange("a (t p) n -> p (a t) n", p=P))\
                      .then_inc(ctx_in, 16)

        @block.tensor
        def _(pe):
            pe.sem_inc(t_full, T_CREDIT)
            pe.sem_inc(pv, 2)
            pe.wait_ge(weights, 16 * len(loads))
            if a0:
                pe.wait_ge(ready, 1)
                for dt in range(DT):
                    for t in range(DT):
                        mm = pe.matmul(A[0][:, 64 * dt:64 * dt + 64], wkT[:, t, dt * P:(dt + 1) * P], wdn[:, t, :],
                                       start=(t == 0), stop=(t == DT - 1))
                mm.then_inc(folded, 1)
            pe.wait_ge(ready, N_READY)

            def project(seg, turn, b, work):
                if work[0] == "xT":
                    pe.wait_ge(xin_in, b * 16 + 16)
                    for dt in range(DT):
                        name = ("xT", dt)
                        pe.wait_ge(*seg.empty(turn, name))
                        bank = A[seg.bank(name)]
                        for qt in range(QT):
                            mm = pe.transpose(bank[:, qt * P:(qt + 1) * P], xin[:, qt, dt * P:(dt + 1) * P],
                                              sh.ident[:])
                        mm.then_inc(a_full, 1)
                    pe.wait_ge(xt_done, b * DT + DT)
                    return
                if work[0] == "lat":
                    pe.wait_ge(*seg.empty(turn, "lat"))
                    bank = A[seg.bank("lat")]
                    wl, rows_l = (wkd, 64) if a0 else (wdn, P)
                    for t in range(DT):
                        mm = pe.matmul(bank[0:rows_l, :], wl[:, t, :], xT[:, t, :], start=(t == 0), stop=(t == DT - 1))
                    mm.then_inc(a_full, 1)
                    return
                _, g, i = work
                if a1:
                    pair = 2 * g + i // 2
                    col = slice(pair * P, (pair + 1) * P)
                    if g == 0 and i == 1:
                        pe.wait_ge(a_act, b + 1)
                    for sw in range(2):
                        name = (*work, sw)
                        pe.wait_ge(*seg.empty(turn, name))
                        bank = A[seg.bank(name)]
                        if i % 2 == 0:
                            for t in range(DT):
                                mm = pe.matmul(bank[:], (wq, wqs)[sw][:, t, col], xT[:, t, :],
                                               start=(t == 0), stop=(t == DT - 1))
                        else:
                            mm = pe.matmul(bank[:], wupk[:, sw, col], lat[:], start=True, stop=True)
                        mm.then_inc(a_full, 1)
                    return
                pe.wait_ge(*seg.empty(turn, work))
                bank = A[seg.bank(work)]
                if a0 and i == 0:
                    for t in range(DT):
                        mm = pe.matmul(bank[:], wq[:, t, g, :], xT[:, t, :], start=(t == 0), stop=(t == DT - 1))
                elif a0:
                    if g == 0:
                        pe.wait_ge(a_act, b + 1)
                    mm = pe.matmul(bank[:], wupk[:, g, :], lat[:], start=True, stop=True)
                elif i < 4:
                    pair = 2 * g + i % 2
                    for t in range(DT):
                        mm = pe.matmul(bank[:], (wq, wk1)[i // 2][:, t, pair * P:(pair + 1) * P], xT[:, t, :],
                                       start=(t == 0), stop=(t == DT - 1))
                else:
                    pe.wait_ge(ctx_in, b * 16 + 16)
                    for pr in range(2):
                        pair = 2 * g + pr
                        for t in range(DT):
                            mm = pe.matmul(bank[:, pr * SC:(pr + 1) * SC], wk2[:, t, pair * P:(pair + 1) * P],
                                           ctxT[:, t, :], start=(t == 0), stop=(t == DT - 1))
                mm.then_inc(a_full, 1)

            def values(seg, turn, b):
                for i in range(N_V):
                    name = ("v", i)
                    pe.wait_ge(*seg.empty(turn, name))
                    bank = A[seg.bank(name)]
                    if a0:
                        for k in range(2):
                            kt = 2 * i + k
                            mm = pe.matmul(bank[:, k * D:(k + 1) * D], lat[:, kt * P:(kt + 1) * P], wupv[:],
                                           start=True, stop=True)
                    elif a1:
                        kt, half = divmod(i, 2)
                        mm = pe.matmul(bank[:], lat[:, kt * P:(kt + 1) * P], wupv[:, half * 512:(half + 1) * 512],
                                       start=True, stop=True)
                    elif i < QT:
                        for t in range(DT):
                            mm = pe.matmul(bank[:], xT[:, t, i * P:(i + 1) * P], wv1[:, t, :],
                                           start=(t == 0), stop=(t == DT - 1))
                    else:
                        for t in range(DT):
                            mm = pe.matmul(bank[0:SC, :], ctxT[:, t, :], wv2[:, t, :],
                                           start=(t == 0), stop=(t == DT - 1))
                    mm.then_inc(a_full, 1)

            def score_head(seg, turn, b, u, j):
                g, qt = divmod(u, QT)
                gp = g % 2
                q = slice(qt * P, (qt + 1) * P)
                if qt == 0 and j == 0:
                    if a0:
                        pe.wait_ge(kp, b * 4 * G + 4 * (g + 1))
                        pe.wait_ge(low, b * 4 * G + 4 * (g + 1) + 4)
                    elif a1:
                        pe.wait_ge(low, b * LOW_GROUP * G + LOW_GROUP * (g + 2))
                    else:
                        pe.wait_ge(q_low, b * ITEMS * G + ITEMS * (g + 1))
                name = ("score", u, j)
                pe.wait_ge(*seg.empty(turn, name))
                bank = A[seg.bank(name)]
                parts = [(bank[:, 0:keys(u)], j, slice(0, keys(u)))] if j < 4 else \
                    [(bank[:, h * SC:(h + 1) * SC], h, slice(S, NK)) for h in range(4)]
                for out, h, ks in parts:
                    if a0:
                        terms = [(qs[:, gp, q], 1), (qs[:, gp, q], 0)]
                    else:
                        pr = h // 2
                        terms = [(q_hl[:, gp, 0, pr, q], 1), (q_hl[:, gp, 1, pr, q], 0), (q_hl[:, gp, 0, pr, q], 0)]
                    for n, (lhs, hl) in enumerate(terms):
                        mm = pe.matmul(out, lhs, kpad[:, gp, hl, h, ks], start=(n == 0), stop=(n == len(terms) - 1))
                mm.then_inc(a_full, 1)

            def transpose_head(b, ug, u, j):
                job = ug * T_UNIT + j
                waits = [(normed, ug * 4 + min(j + 1, 4)), (t_empty, job + 1)]
                if j < 4:
                    for sem, value in waits:
                        pe.wait_ge(sem, value)
                else:
                    wait_apart(pe, (ready, N_READY), *waits)
                bank = T[(u * T_UNIT + j) % 2]
                if j < 4:
                    for kt in range(keys(u) // P):
                        mm = pe.transpose(bank[:, kt, :], t_of(u, j, kt * P, (kt + 1) * P), sh.ident[:])
                else:
                    for h in range(4):
                        mm = pe.transpose(bank[0:SC, h, :], t_of(u, h, S, NK), sh.ident[:])
                mm.then_inc(t_full, 1)

            def times_values(ug, u, kt):
                g, qt = divmod(u, QT)
                q = slice(qt * P, (qt + 1) * P)
                last = kt == (4 if x1 else keys(u) // P - 1)
                for j in range(4):
                    pr, half = divmod(j, 2)
                    col = slice((2 * g + pr) * P + 64 * half, (2 * g + pr) * P + 64 * half + 64)
                    if a0:
                        hh, par = divmod(g, 2)
                        mm = pe.matmul(O[hh][32 * j:32 * j + 32, q], v_sb[:, kt, 8 * hh + 2 * j + par, :],
                                       p_tile(u, j, kt), start=(par == 0 and qt == 0 and kt == 0),
                                       stop=(par == 1 and last), skip_group_check=True)
                    elif kt < 4:
                        mm = pe.matmul(O[pr][64 * half:64 * half + 64, q], v_sb[:, kt, col],
                                       p_tile(u, j, kt), start=(kt == 0), stop=last, skip_group_check=True)
                    else:
                        mm = pe.matmul(O[pr][64 * half:64 * half + 64, q], v2[:, col],
                                       p_tile(u, j, 4)[0:SC], start=False, stop=True, skip_group_check=True)
                if last:
                    mm.then_inc(pv, 1)

            def step(seg, turn, b, s, prev, own, nxt):
                u_t, u_v = s - LAG_T, s - LAG_V
                do_t = s < U and (own if u_t >= 0 else prev)
                do_v = s < U and (own if u_v >= 0 else prev)
                if do_v:
                    pe.wait_ge(t_empty, (b * U + u_v + 1) * T_UNIT + 2)
                    g, qt = divmod(u_v % U, QT)
                    if u_v == 0:
                        pe.wait_ge(*(seg.emptied(turn, ("v", N_V - 1)) if a0 else (v_done, b * N_V + N_V)))
                    if qt == 0 and not a0:
                        pe.wait_ge(o_empty, b * N_O + (2 * g + 2 - (N_O if u_v < 0 else 0)))
                    elif qt == 0 and g % 2 == 0:
                        pe.wait_ge(o_empty, b * N_O + (g // 2 + 1))
                for j in range(5):
                    if own and j < (5 if x1 else 4):
                        score_head(seg, turn, b, s, j)
                    if do_t and j < T_UNIT:
                        transpose_head(b, b * U + u_t, u_t % U, j)
                    if do_v and (j < keys(u_v % U) // P or (x1 and j == 4)):
                        times_values(b * U + u_v, u_v % U, j)
                if s == V_STEP and own:
                    values(seg, turn, b)
                if s == Y_STEP and prev:
                    pe.wait_ge(o_empty, b * N_O + 2)
                    for qt in range(QT):
                        name = ("y", qt)
                        pe.wait_ge(*seg.empty(turn, name))
                        bank = A[seg.bank(name)]
                        n_o = 2 if a0 else PAIRS
                        for t in range(n_o):
                            mm = pe.matmul(bank[:, 0:D], oT[:, t, qt * P:(qt + 1) * P], wo[:, t, :], start=(t == 0),
                                           stop=(t == n_o - 1 and not x1))
                        if x1:
                            mm = pe.matmul(bank[:, 0:D], ones[:], bo[:], start=False, stop=True)
                        mm.then_inc(a_full, 1)
                if own and (nxt or s < U - QT):
                    for work in work_at(s):
                        project(seg, turn, b if s < U - QT else b + 1, work)

            def begin():
                for work in START:
                    project(start, 0, 0, work)

            def body(seg, turn, b, prev, own, nxt):
                for s in range(U if own else Y_STEP + 1):
                    step(seg, turn, b, s, prev, own, nxt)

            batches(pe, begin, body)

        @block.scalar
        def _(act):
            act.sem_inc(t_empty, 2)
            act.sem_inc(o_empty, 2)
            act.wait_ge(ready, N_READY)

            def high_parts(seg, turn, b, g, i):
                gp = g % 2
                if a0:
                    name = ("item", g, i)
                    act.wait_ge(*seg.full(turn, name))
                    nc.scalar.activation((qs[:, gp, :], kh[:])[i], A[seg.bank(name)][:], ACT.Copy).then_inc(hi, 1)
                elif a1:
                    act.wait_ge(rot_sum, b * 4 * G + (4 * g + i + 1 + 2))
                    if i % 2 == 0:
                        nc.scalar.activation(q_hl[:, gp, 0, i // 2, :], rsum[:, i % 2, :], ACT.Copy).then_inc(hi, 1)
                    else:
                        for half in range(2):
                            r = slice(64 * half, 64 * half + 64)
                            nc.scalar.activation(kpad[r, gp, 0, 2 * (i // 2) + half, :], rsum[r, i % 2, :],
                                                 ACT.Copy).then_inc(hi, 1)
                else:
                    name = ("item", g, i)
                    bank = A[seg.bank(name)]
                    act.wait_ge(*seg.full(turn, name))
                    if i < 2:
                        nc.scalar.activation(q_hl[:, gp, 0, i, :], bank[:], ACT.Copy).then_inc(hi, 1)
                    elif i < 4:
                        for half in range(2):
                            r = slice(64 * half, 64 * half + 64)
                            nc.scalar.activation(kpad[r, gp, 0, 2 * (i - 2) + half, 0:S], bank[r, :],
                                                 ACT.Copy).then_inc(hi, 1)
                    else:
                        for pr in range(2):
                            for half in range(2):
                                r = slice(64 * half, 64 * half + 64)
                                nc.scalar.activation(kpad[r, gp, 0, 2 * pr + half, S:NK],
                                                     bank[r, pr * SC:(pr + 1) * SC], ACT.Copy).then_inc(hi, 1)

            def project(seg, turn, b, work):
                if work[0] == "xT":
                    for dt in range(DT):
                        name = ("xT", dt)
                        act.wait_ge(*seg.full(turn, name))
                        nc.scalar.activation(xT[:, dt, :], A[seg.bank(name)][:], ACT.Copy).then_inc(xt_done, 1)
                elif work[0] == "lat":
                    act.wait_ge(*seg.full(turn, "lat"))
                    nc.scalar.activation(lat[:], A[seg.bank("lat")][0:64 if a0 else P, :], ACT.Copy).then_inc(a_act, 1)
                else:
                    high_parts(seg, turn, b, work[1], work[2])

            def step(seg, turn, b, s, prev, own, nxt):
                u_e, u_t, u_v = s - LAG_E, s - LAG_T, s - LAG_V
                do_e = s < U and (own if u_e >= 0 else prev)
                do_t = s < U and (own if u_t >= 0 else prev)
                do_v = s < U and (own if u_v >= 0 else prev)
                if do_e:
                    act.wait_ge(negated, b * U + (u_e + 1))
                if do_t:
                    act.wait_ge(pv, b * U + (u_t + 1))
                for j in range(5):
                    if do_t and j < T_UNIT:
                        u = u_t % U
                        act.wait_ge(t_full, (b * U + u_t) * T_UNIT + (j + 1 + T_CREDIT))
                        bank = T[(u * T_UNIT + j) % 2]
                        kts = keys(u) // P
                        to, of = (p_tile(u, j, 0, kts), bank[:, 0:kts, :] if kts > 1 else bank[:, 0, :]) if j < 4 else \
                            (p_T[0:SC, (u % 2) * tiles[0] + 4:(u % 2) * tiles[0] + tiles[0]:5, :], bank[0:SC, :, :])
                        nc.scalar.activation(to, of, ACT.Copy).then_inc(t_empty, 1)
                    if do_e and j < 4:
                        slot, n = u_e % 4, (NK if x1 else keys(u_e % U))
                        nc.scalar.activation(t_of(u_e % U, j, 0, n), t_of(u_e % U, j, 0, n), ACT.Exp,
                                             bias=neg[:, slot, j:j + 1], scale=SCALE,
                                             accum_out=total[:, slot, j:j + 1]).then_inc(exped, 1)
                if s == V_STEP and own and not a0:
                    for i in range(N_V):
                        name = ("v", i)
                        act.wait_ge(*seg.full(turn, name))
                        bank = A[seg.bank(name)]
                        if a1:
                            kt, half = divmod(i, 2)
                            to, of = v_sb[:, kt, half * 512:(half + 1) * 512], bank[:]
                        elif i < QT:
                            to, of = v_sb[:, i, :], bank[:]
                        else:
                            to, of = v2[:], bank[0:SC, :]
                        nc.scalar.activation(to, of, ACT.Copy).then_inc(v_done, 1)
                if do_v:
                    g, qt = divmod(u_v % U, QT)
                    if qt == QT - 1 and (not a0 or g % 2 == 1):
                        act.wait_ge(pv, b * U + (u_v + 1 + 2))
                        for o in ([g // 2] if a0 else [0, 1]):
                            nc.scalar.activation(oT[:, o if a0 else 2 * g + o, :], O[o][:],
                                                 ACT.Copy).then_inc(o_empty, 1)
                if own and (nxt or s < U - QT):
                    for work in work_at(s):
                        project(seg, turn, b if s < U - QT else b + 1, work)

            def begin():
                for work in START:
                    project(start, 0, 0, work)

            def body(seg, turn, b, prev, own, nxt):
                for s in range(U if own else Y_STEP + 1):
                    step(seg, turn, b, s, prev, own, nxt)

            batches(act, begin, body)

        @block.gpsimd
        def _(pool):
            if a0:
                pool.sem_inc(low, 4)
                pool.wait_ge(ready, N_READY)
                with pool.Fori(0, B) as b:
                    for g in range(G):
                        pool.wait_ge(kl_done, b * G + (g + 1))
                        for j in range(4):
                            nc.gpsimd.tensor_tensor(kpad[:, g % 2, 1, j, :], kl[:],
                                                    hmask[:, j:j + 1].to_broadcast([P, S]), ALU.mult).then_inc(low, 1)
            if a1:
                pool.sem_inc(rot_sum, 2)
                pool.sem_inc(low, LOW_GROUP)
                pool.wait_ge(ready, N_READY)
                with pool.Fori(0, B) as b:
                    for g in range(G):
                        for i in range(4):
                            gp = g % 2
                            pool.wait_ge(rot_done, b * 4 * G + (4 * g + i + 1))
                            nc.gpsimd.tensor_tensor(rsum[:, i % 2, :], rsum[:, i % 2, :], rsin[:],
                                                    ALU.add).then_inc(rot_sum, 1)
                            pool.wait_ge(hi, b * HI_GROUP * G + (HI_GROUP * g + HI_ITEM[i]))
                            if i % 2 == 0:
                                nc.gpsimd.tensor_tensor(q_hl[:, gp, 1, i // 2, :], rsum[:, i % 2, :],
                                                        q_hl[:, gp, 0, i // 2, :], ALU.subtract).then_inc(low, 1)
                            else:
                                for half in range(2):
                                    r = slice(64 * half, 64 * half + 64)
                                    h = 2 * (i // 2) + half
                                    nc.gpsimd.tensor_tensor(kpad[r, gp, 1, h, :], rsum[r, i % 2, :],
                                                            kpad[r, gp, 0, h, :], ALU.subtract).then_inc(low, 1)
                                    pool.wait_ge(low, b * LOW_GROUP * G + (LOW_GROUP * (g + 1) + LOW_ITEM[i] - 1 + half))

        @block.vector
        def _(dve):
            if a0:
                dve.wait_ge(weights, 16 * len(loads))
                nc.vector.tensor_tensor(wkT[:], wkT[:], wvT[:], ALU.add).then_inc(ready, 1)
                nc.vector.memset(v_sb[:], 0.0).then_inc(ready, 1)
                dve.wait_ge(folded, 1)
                nc.vector.tensor_copy(wkd[:], A[0][:, 0:DT * 64].rearrange("p (t n) -> p t n", t=DT)).then_inc(ready, 1)
                dve.wait_ge(ready, 3)
            else:
                nc.vector.memset(kpad[:].bitcast(F32), 0.0).then_inc(ready, 1)
                if x1:
                    nc.vector.memset(ones[:], 1.0).then_inc(ready, 1)
                    nc.vector.memset(table[:], 0.0).then_inc(ready, 1)
                dve.wait_ge(ready, N_READY)
                dve.wait_ge(weights, 16 * len(loads))
            dve.sem_inc(a_dve, A_BANKS)

            def low_parts(seg, turn, b, g, i):
                gp = g % 2
                if a0:
                    name = ("item", g, i)
                    bank = A[seg.bank(name)]
                    dve.wait_ge(*seg.full(turn, name))
                    dve.wait_ge(hi, b * HI_GROUP * G + (HI_GROUP * g + HI_ITEM[i]))
                    if i == 0:
                        nc.vector.tensor_tensor(qs[64:128, gp, :], bank[64:128, :], qs[64:128, gp, :],
                                                ALU.subtract).then_inc(a_dve, 1)
                    else:
                        dve.wait_ge(low, b * 4 * G + 4 * (g + 1))
                        nc.vector.tensor_tensor(kl[:], bank[:], kh[:], ALU.subtract).then_inc(kl_done, 1)
                        for j in range(4):
                            nc.vector.tensor_scalar(kpad[:, gp, 0, j, :], kh[:], hmask[:, j:j + 1], None,
                                                    ALU.mult).then_inc(kp, 1)
                elif a1:
                    dve.wait_ge(low, b * LOW_GROUP * G + (LOW_GROUP * g + (LOW_ITEM[i + 2] if i < 2 else LOW_GROUP + LOW_ITEM[i - 2])))
                    for sw in range(2):
                        name = ("item", g, i, sw)
                        if sw:
                            dve.wait_ge(rot_sum, b * 4 * G + (4 * g + i + 2))
                        dve.wait_ge(*seg.full(turn, name))
                        nc.vector.tensor_tensor((rsum[:, i % 2, :], rsin[:])[sw], A[seg.bank(name)][:], (cos, sin)[sw][:],
                                                ALU.mult).then_inc((a_dve, rot_done)[sw], 1)
                else:
                    name = ("item", g, i)
                    bank = A[seg.bank(name)]
                    dve.wait_ge(*seg.full(turn, name))
                    dve.wait_ge(hi, b * HI_GROUP * G + (HI_GROUP * g + HI_ITEM[i]))
                    if i < 2:
                        ins = nc.vector.tensor_tensor(q_hl[:, gp, 1, i, :], bank[:], q_hl[:, gp, 0, i, :], ALU.subtract)
                    elif i < 4:
                        for half in range(2):
                            r = slice(64 * half, 64 * half + 64)
                            h = 2 * (i - 2) + half
                            ins = nc.vector.tensor_tensor(kpad[r, gp, 1, h, 0:S], bank[r, :], kpad[r, gp, 0, h, 0:S],
                                                          ALU.subtract)
                    else:
                        for pr in range(2):
                            for half in range(2):
                                r = slice(64 * half, 64 * half + 64)
                                h = 2 * pr + half
                                ins = nc.vector.tensor_tensor(kpad[r, gp, 1, h, S:NK], bank[r, pr * SC:(pr + 1) * SC],
                                                              kpad[r, gp, 0, h, S:NK], ALU.subtract)
                    ins.then_inc(q_low, 1)

            def step(seg, turn, b, s, prev, own, nxt):
                u_n = s - LAG_N
                do_n = s < U and (own if u_n >= 0 else prev)
                if own:
                    dve.wait_ge(t_full, (b * U + s + 1) * T_UNIT)
                if do_n:
                    dve.wait_ge(exped, (b * U + u_n + 1) * 4)
                    nc.vector.reciprocal(inv[:, u_n % 4, :], total[:, u_n % 4, :]).then_inc(inverted, 1)
                slot, qt, n = s % 4, s % QT, keys(s)
                at = S - P - qt * P if (a0 or a1) else 0
                for j in range(4):
                    if own:
                        name = ("score", s, j)
                        wait_apart(dve, (ready, N_READY), seg.full(turn, name))
                        nc.vector.tensor_tensor_reduce(
                            t_of(s, j, 0, n), A[seg.bank(name)][:, 0:n], table[:, at:at + n], 1.0, LOWEST,
                            ALU.mult if a0 else ALU.add, ALU.max,
                            (mx1 if x1 else mx)[:, slot, j:j + 1]).then_inc(a_dve, 1)
                    if do_n:
                        if j == 0:
                            dve.wait_ge(inverted, b * U + (u_n + 1))
                        m = NK if x1 else keys(u_n % U)
                        nc.vector.tensor_scalar(t_of(u_n % U, j, 0, m), t_of(u_n % U, j, 0, m),
                                                inv[:, u_n % 4, j:j + 1], None, ALU.mult).then_inc(normed, 1)
                if x1 and own:
                    name = ("score", s, 4)
                    wait_apart(dve, (ready, N_READY), seg.full(turn, name), seg.emptied(turn, ("score", s, 3)))
                    for j in range(4):
                        ins = nc.vector.tensor_tensor_reduce(
                            t_of(s, j, S, NK), A[seg.bank(name)][:, j * SC:(j + 1) * SC],
                            table[:, 0:SC], 1.0, mx1[:, slot, j:j + 1], ALU.add, ALU.max, mx[:, slot, j:j + 1])
                    ins.then_inc(a_dve, 1)
                if own:
                    dve.wait_ge(*seg.emptied(turn, ("score", s, 4 if x1 else 3)))
                    nc.vector.tensor_scalar(neg[:, slot, :], mx[:, slot, :], -SCALE, None,
                                            ALU.mult).then_inc(negated, 1)
                if s == V_STEP and own and a0:
                    for i in range(N_V):
                        name = ("v", i)
                        dve.wait_ge(*seg.full(turn, name))
                        bank = A[seg.bank(name)][:].rearrange("p (k h r c) -> p k h r c", k=2, r=2, c=16)
                        for par in range(2):
                            ins = nc.vector.tensor_copy(v_sb[:, 2 * i:2 * i + 2, par:16:2, 16 * par:16 * par + 16],
                                                        bank[:, :, :, par, :])
                        ins.then_inc(a_dve, 1)
                if s == Y_STEP and prev:
                    for qt in range(QT):
                        name = ("y", qt)
                        dve.wait_ge(*seg.full(turn, name))
                        row = sh.x_all[:, b * QT - QT + qt, :]
                        nc.vector.tensor_tensor(row, A[seg.bank(name)][:, 0:D], row, ALU.add).then_inc(a_dve, 1)
                if own and (nxt or s < U - QT):
                    for work in work_at(s):
                        if work[0] == "item":
                            low_parts(seg, turn, b if s < U - QT else b + 1, work[1], work[2])
                if s == Y_STEP and prev:
                    wait_apart(dve, (ready, N_READY), seg.emptied(turn, ("y", QT - 1)))
                    steps = Chain(dve, chain, (b - 1) * LN_LINKS, (ready, N_READY))
                    layer_norm_rows(nc.vector, steps, lambda qt: sh.x_all[:, b * QT - QT + qt, :], stats, mv,
                                    scratch)
                    assert steps.n == LN_LINKS, steps.n

            def begin():
                for work in START:
                    if work[0] == "item":
                        low_parts(start, 0, 0, work[1], work[2])

            def body(seg, turn, b, prev, own, nxt):
                for s in range(U if own else Y_STEP + 1):
                    step(seg, turn, b, s, prev, own, nxt)

            batches(dve, begin, body)


def cross_attention_heads(nc, sh, w):
    H, HD = 16, 16
    HH = H // DT
    PR = H // 2
    VC = HD + 1
    LAG_T, LAG_V, LN_STEP = 2, 3, 2
    OPS = 2 * DT
    T_DONE = (4, 6, 10, 12)

    with ExitStack() as ctx:
        env = Env(nc, ctx, "x0")
        sb, sem = env.sb, env.sem
        xin = sb("xin", [P, QT, D])
        x_hl = sb("xhl", [P, 2, DT, S], F32R)
        ctxT = sb("ctxT", [P, DT, B, SC])
        ctx_hl = sb("ctxhl", [P, 2, DT, B * SC], F32R)
        keys = sb("keys", [P, 2, DT, B, HH, SC], F32R)
        v_nat = sb("vnat", [P, B, D])
        v_all = sb("v", [P, B, PR * 2 * VC])
        hmask = sb("hmask", [P, HH])
        mask = sb("mask", [P, B * QT, SC], I32)
        bias = sb("bias", [P, B * QT, SC])
        t_buf = sb("t", [P, QT, H, SC])
        p_T = sb("pT", [P, 2, PR, P])
        mx = sb("mx", [P, QT, H])
        inv = sb("inv", [P, 2, H])
        res = sb("res", [P, 2, D])
        stats = sb("stats", [P, QT, 6])
        mv = sb("mv", [P, QT, 2])
        scratch = sb("scratch", [P, 3, QT])
        SB = [env.ps(f"S{i}", [P, HH, SC]) for i in range(2 * DT)]
        T = [env.ps(f"T{i}", [P, 4, P]) for i in range(2)]
        O = [env.ps(f"O{i}", [P, H * VC]) for i in range(2)]

        loaded = sem("loaded")
        xin_in = sem("xin_in")
        ready = sem("ready")
        ctx_hi = sem("ctx_hi")
        keyed = sem("keyed")
        t_full = sem("t_full")
        t_act = sem("t_act")
        x_low = sem("x_low")
        x_hi = sem("x_hi")
        s_full = sem("s_full")
        s_read = sem("s_read")
        maxed = sem("maxed")
        shifted = sem("shifted")
        exped = sem("exped")
        pv = sem("pv")
        inverted = sem("inverted")
        scaled = sem("scaled")
        added = sem("added")
        chain = sem("chain")
        sems = {"full": t_full, "act": t_act, "dve": x_low}

        def xt_jobs():
            return [(("xT", dt), "dve") for dt in range(DT)]

        def seg_jobs(prev, own, nxt):
            jobs = []
            for s in range(QT if own else LAG_V):
                if s >= LAG_T if own and not prev else (s < LAG_T if not own else True):
                    jobs += [(("T", s, j), "act") for j in range(2)]
                if own and nxt and s == QT - 1:
                    jobs += xt_jobs()
            return jobs

        start = Segment(xt_jobs(), sems, {"full": 0, "act": 0, "dve": 2}, [("dve", 0)] * 2, n=2)
        first = Segment(seg_jobs(False, True, True), sems, start.end, start.last, n=2)
        steady = Segment(seg_jobs(True, True, True), sems, first.end, first.last, n=2)
        assert steady.last == first.last
        looped = {r: steady.base[r] + (B - 2) * steady.per[r] for r in steady.base}
        final = Segment(seg_jobs(True, True, False), sems, looped, steady.last, n=2)
        tail = Segment(seg_jobs(True, False, False), sems, final.end, final.last, n=2)

        def batches(eng, body):
            body(first, 0, 0, prev=False, own=True, nxt=True)
            with eng.Fori(1, B - 1) as b:
                body(steady, b - 1, b, prev=True, own=True, nxt=True)
            body(final, 0, B - 1, prev=True, own=True, nxt=False)
            body(tail, 0, B, prev=True, own=False, nxt=False)

        def lagged(s, lag, prev, own):
            return own if s >= lag else prev

        block = ctx.enter_context(nc.Block())
        LOADS = DT + 2 + 2

        @block.sync
        def _(sp):
            sp.dma_start(xin[:], sh.x_all[:, 0:QT, :]).then_inc(xin_in, 16)
            for t in range(DT):
                sp.dma_start(ctxT[:, t], w["ctxT"][:, t * P:(t + 1) * P, :].rearrange("b p n -> p b n"))\
                  .then_inc(loaded, 16)
            for half in range(2):
                sp.dma_start(v_nat[half * SC:(half + 1) * SC], w["ctx"].rearrange("b n d -> n b d")).then_inc(loaded, 16)
            sp.dma_start(hmask[:], w["head_mask8"]).then_inc(loaded, 16)
            sp.dma_start(mask[:], w["mask"].rearrange("b (q p) n -> p (b q) n", p=P)).then_inc(loaded, 16)
            with sp.Fori(1, B) as b:
                sp.wait_ge(x_low, b * DT + 2)
                sp.dma_start(xin[:], sh.x_all[:, bass.ds(b * QT, QT), :]).then_inc(xin_in, 16)

        @block.tensor
        def _(pe):
            def transpose_x(seg, turn, b):
                pe.wait_ge(xin_in, b * 16 + 16)
                for dt in range(DT):
                    name = ("xT", dt)
                    pe.wait_ge(*seg.empty(turn, name))
                    for qt in range(QT):
                        mm = pe.transpose(T[seg.bank(name)][:, qt, :], xin[:, qt, dt * P:(dt + 1) * P], sh.ident[:])
                    mm.then_inc(t_full, 1)

            def body(seg, turn, b, prev, own, nxt):
                for s in range(QT if own else LAG_V):
                    if lagged(s, LAG_T, prev, own):
                        u = (s - LAG_T) % QT
                        pe.wait_ge(exped, b * QT + (s - LAG_T + 1))
                        for j in range(2):
                            name = ("T", s, j)
                            pe.wait_ge(*seg.empty(turn, name))
                            for i in range(4):
                                pr = 4 * j + i
                                mm = pe.transpose(T[seg.bank(name)][:, i, :],
                                                  t_buf[:, u, 2 * pr:2 * pr + 2, :].rearrange("p h k -> p (h k)"),
                                                  sh.ident[:])
                            mm.then_inc(t_full, 1)
                    if own:
                        if s == 0:
                            pe.wait_ge(x_low, b * DT + (DT + 2))
                            pe.wait_ge(keyed, b * OPS + OPS)
                        pe.wait_ge(s_read, b * QT * DT + DT * (s + 1))
                        q = slice(s * P, (s + 1) * P)
                        for dt in range(DT):
                            for n, (a, k) in enumerate(((0, 1), (1, 0), (0, 0))):
                                mm = pe.matmul(SB[DT * (s % 2) + dt][:], x_hl[:, a, dt, q], keys[:, k, dt, b],
                                               start=(n == 0), stop=(n == 2))
                            mm.then_inc(s_full, 1)
                    if lagged(s, LAG_V, prev, own):
                        u, back = (s - LAG_V) % QT, s - LAG_V
                        pe.wait_ge(t_act, (b * QT + back + 1) * 2)
                        pe.wait_ge(scaled, b * QT + (back + 1))
                        vb = b if back >= 0 else b - 1
                        for pr in range(PR):
                            mm = pe.matmul(O[u % 2][:, pr * 2 * VC:(pr + 1) * 2 * VC], p_T[:, u % 2, pr, :],
                                           v_all[:, vb, pr * 2 * VC:(pr + 1) * 2 * VC],
                                           start=True, stop=True)
                        mm.then_inc(pv, 1)
                    if nxt and s == QT - 1:
                        transpose_x(seg, turn, b + 1)

            pe.wait_ge(ready, 4)
            transpose_x(start, 0, 0)
            batches(pe, body)

        @block.scalar
        def _(act):
            act.wait_ge(loaded, 16 * LOADS)
            nc.scalar.activation(ctx_hl[:, 0], ctxT[:].rearrange("p t b n -> p t (b n)"), ACT.Copy).then_inc(ctx_hi, 1)
            act.sem_inc(pv, 2)

            def split_x(seg, turn, b):
                if not (isinstance(b, int) and b == 0):
                    act.wait_ge(s_full, b * QT * DT)
                for dt in range(DT):
                    name = ("xT", dt)
                    act.wait_ge(*seg.full(turn, name))
                    nc.scalar.activation(x_hl[:, 0, dt, :], T[seg.bank(name)][:].rearrange("p a b -> p (a b)"),
                                         ACT.Copy).then_inc(x_hi, 1)

            def body(seg, turn, b, prev, own, nxt):
                for s in range(QT if own else LAG_V):
                    if lagged(s, LAG_T, prev, own):
                        u, back = (s - LAG_T) % QT, s - LAG_T
                        act.wait_ge(pv, b * QT + (back + 1))
                        for j in range(2):
                            name = ("T", s, j)
                            act.wait_ge(*seg.full(turn, name))
                            nc.scalar.activation(p_T[:, u % 2, 4 * j:4 * j + 4, :], T[seg.bank(name)][:],
                                                 ACT.Copy).then_inc(t_act, 1)
                    if lagged(s, 1, prev, own):
                        u = (s - 1) % QT
                        act.wait_ge(shifted, b * QT + s)
                        nc.scalar.activation(t_buf[:, u], t_buf[:, u], ACT.Exp).then_inc(exped, 1)
                    if nxt and s == QT - 1:
                        split_x(seg, turn, b + 1)

            split_x(start, 0, 0)
            batches(act, body)

        @block.gpsimd
        def _(pool):
            def make_keys(b):
                for hl in range(2):
                    for dt in range(DT):
                        k = ctx_hl[:, hl, dt, bass.ds(b * SC, SC)].unsqueeze(1).to_broadcast([P, HH, SC])
                        nc.gpsimd.tensor_tensor(keys[:, hl, dt, b], k,
                                                hmask[:].unsqueeze(2).to_broadcast([P, HH, SC]),
                                                ALU.mult).then_inc(keyed, 1)

            def body(seg, turn, b, prev, own, nxt):
                for s in range(QT if own else 0):
                    pool.wait_ge(maxed, b * QT + (s + 1))
                    nc.gpsimd.tensor_tensor(t_buf[:, s], t_buf[:, s],
                                            mx[:, s, :].unsqueeze(2).to_broadcast([P, H, SC]),
                                            ALU.subtract).then_inc(shifted, 1)
                    if nxt and s == 1:
                        make_keys(b + 1)

            pool.wait_ge(ready, 4)
            make_keys(0)
            batches(pool, body)

        @block.vector
        def _(dve):
            nc.vector.memset(v_all[:], 0.0).then_inc(ready, 1)
            dve.sem_inc(s_read, 2 * DT)
            dve.sem_inc(scaled, 2)
            dve.sem_inc(x_low, 2)
            dve.wait_ge(loaded, 16 * LOADS)
            dve.wait_ge(ready, 1)
            for half in range(2):
                r = slice(half * SC, (half + 1) * SC)
                of = v_nat[r].rearrange("p b (r h c) -> p b r h c", h=2, c=HD)[:, :, :, half, :]
                to = v_all[r].rearrange("p b (r h c) -> p (b r) h c", h=2, c=VC)[:, :, half, :]
                nc.vector.tensor_copy(to[:, :, 0:HD], of.rearrange("p b r c -> p (b r) c"))
                nc.vector.memset(to[:, :, HD:VC], 1.0)
            nc.vector.tensor_scalar(bias[:], mask[:], 1.0e9, -1.0e9, ALU.mult, ALU.add).then_inc(ready, 1)
            dve.wait_ge(ctx_hi, 1)
            for dt in range(DT):
                nc.vector.tensor_tensor(ctx_hl[:, 1, dt], ctxT[:, dt].rearrange("p b n -> p (b n)"), ctx_hl[:, 0, dt],
                                        ALU.subtract).then_inc(ready, 1)
            dve.wait_ge(ready, 4)

            def split_x(seg, turn, b):
                for dt in range(DT):
                    dve.wait_ge(x_hi, b * DT + (dt + 1))
                    nc.vector.tensor_tensor(x_hl[:, 1, dt, :],
                                            T[seg.bank(("xT", dt))][:].rearrange("p a b -> p (a b)"),
                                            x_hl[:, 0, dt, :], ALU.subtract).then_inc(x_low, 1)

            def body(seg, turn, b, prev, own, nxt):
                for s in range(QT if own else LAG_V):
                    if own:
                        if prev:
                            dve.wait_ge(t_full, b * 10 + (T_DONE[s] - 10))
                        for dt in range(DT):
                            dve.wait_ge(s_full, b * QT * DT + (DT * s + dt + 1))
                            nc.vector.scalar_tensor_tensor(
                                out=t_buf[:, s, HH * dt:HH * (dt + 1), :], in0=SB[DT * (s % 2) + dt][:], scalar=0.25,
                                in1=bias[:, bass.ds(b * QT + s, 1), :].to_broadcast([P, HH, SC]),
                                op0=ALU.mult, op1=ALU.add).then_inc(s_read, 1)
                        dve.wait_ge(s_read, b * QT * DT + (DT * (s + 1) + 2 * DT))
                        nc.vector.tensor_reduce(mx[:, s, :], t_buf[:, s], AX_X, ALU.max).then_inc(maxed, 1)
                    if nxt and s == QT - 1:
                        split_x(seg, turn, b + 1)
                    if lagged(s, LAG_V, prev, own):
                        u, back = (s - LAG_V) % QT, s - LAG_V
                        rb = b if back >= 0 else b - 1
                        heads = O[u % 2][:].rearrange("p (h c) -> p h c", c=VC)
                        dve.wait_ge(pv, b * QT + (back + 1 + 2))
                        nc.vector.reciprocal(inv[:, u % 2, :], heads[:, :, HD:VC].rearrange("p h c -> p (h c)"))\
                          .then_inc(inverted, 1)
                        dve.wait_ge(inverted, b * QT + (back + 1))
                        nc.vector.tensor_tensor(res[:, u % 2].rearrange("p (h c) -> p h c", c=HD), heads[:, :, 0:HD],
                                                inv[:, u % 2, :].unsqueeze(2).to_broadcast([P, H, HD]),
                                                ALU.mult).then_inc(scaled, 1)
                        dve.wait_ge(scaled, b * QT + (back + 1 + 2))
                        row = sh.x_all[:, rb * QT + u, :]
                        nc.vector.tensor_tensor(row, res[:, u % 2], row, ALU.add).then_inc(added, 1)
                    if s == LN_STEP and prev:
                        wait_apart(dve, (ready, 4), (added, b * QT))
                        steps = Chain(dve, chain, (b - 1) * LN_LINKS, (ready, 4))
                        layer_norm_rows(nc.vector, steps, lambda qt: sh.x_all[:, b * QT - QT + qt, :], stats, mv,
                                        scratch)

            split_x(start, 0, 0)
            batches(dve, body)


def butterfly_stage(engine, dst, tmp, src, weights, stage, transposed):
    s = 2 ** stage
    w = weights.rearrange("p (n s o i) -> p n o i s", n=FH // (2 * s), s=s, o=2, i=2)
    if transposed:
        w = w.rearrange("p n o i s -> p n i o s")
    x = src.rearrange("p (n k s) -> p n k s", k=2, s=s)
    full = [src.shape[0], FH // (2 * s), 2, s]
    view = [a.rearrange("p (n k s) -> p n k s", k=2, s=s) for a in (tmp, dst)]
    for k in range(2):
        yield engine.tensor_tensor(view[k], w[:, :, :, k, :], x[:, :, k:k + 1, :].to_broadcast(full), ALU.mult)
    yield engine.tensor_tensor(dst, dst, tmp, ALU.add)


def fold_butterflies(nc, w, w_up, w_down, bias_h, bias_y, sh):
    with ExitStack() as ctx:
        env = Env(nc, ctx, "fold")
        sb, sem = env.sb, env.sem
        up = sb("up", [P, 2, DT + 1, FH])
        down = sb("down", [P, 2, DT, FH])
        tmp_up = sb("tmpup", [P, DT + 1, FH])
        tmp_down = sb("tmpdown", [P, DT, FH])
        w_stage = sb("wstage", [P, 2, 2, 2 * FH])
        rows = sb("rows", [1, FH])
        b2 = sb("b2", [1, D])
        one = sb("one", [1, 1])
        BH = env.ps("BH", [P, FT])
        TB = [env.ps(f"T{i}", [P, 2, D]) for i in range(4)]
        loaded = sem("loaded")
        staged = [[sem(f"staged_{side}{parity}") for parity in range(2)] for side in ("up", "down")]
        v_step = sem("v_step")
        p_step = sem("p_step")
        biased = sem("biased")
        turned = sem("turned")
        done = sem("done")
        block = ctx.enter_context(nc.Block())
        order = [list(range(STAGES)), list(range(STAGES - 1, -1, -1))]
        source = [w["up_weights"], w["down_weights"]]
        OPS = [3 * (DT + 1), 3 * DT]

        @block.sync
        def _(sp):
            sp.dma_start(up[:, 0, 0:DT, :], w["w_exp"].rearrange("(t p) n -> p t n", p=P)).then_inc(loaded, 16)
            sp.dma_start(up[0:1, 0, DT, :], w["b_exp"]).then_inc(loaded, 16)
            sp.dma_start(down[:, 0], w["w_conT"].rearrange("(t p) n -> p t n", p=P)).then_inc(loaded, 16)
            sp.dma_start(rows[:], w["up_bias"]).then_inc(loaded, 16)
            sp.dma_start(bias_y, w["b_con"]).then_inc(loaded, 16)
            sp.dma_start(b2[:], w["down_bias"]).then_inc(loaded, 16)
            for k in range(STAGES):
                for side, step in ((0, v_step), (1, p_step)):
                    if k >= 2:
                        sp.wait_ge(step, OPS[side] * (k - 1) + (1 if side == 0 else 0))
                    sp.dma_start(w_stage[:, side, k % 2], source[side][order[side][k]].to_broadcast([P, 2 * FH]))\
                      .then_inc(staged[side][k % 2], 16)

        def fold(engine, eng, buf, tmp, side, step, base, parts):
            n = base
            for k in range(STAGES):
                eng.wait_ge(staged[side][k % 2], 16 * (k // 2 + 1))
                runs = [butterfly_stage(engine, buf[p, (k + 1) % 2, t, :], tmp[p, t, :], buf[p, k % 2, t, :],
                                        w_stage[p, side, k % 2], order[side][k], side == 1) for t, p in parts]
                for _ in range(2):
                    for run in runs:
                        next(run).then_inc(step, 1)
                        n += 1
                eng.wait_ge(step, n)
                for run in runs:
                    next(run).then_inc(step, 1)
                    n += 1
                eng.wait_ge(step, n)
            return n

        @block.vector
        def _(dve):
            nc.vector.memset(one[:], 1.0).then_inc(v_step, 1)
            dve.wait_ge(loaded, 16 * 6)
            full = slice(0, P)
            n = fold(nc.vector, dve, up, tmp_up, 0, v_step, 1, [(t, full) for t in range(DT)] + [(DT, slice(0, 1))])
            nc.vector.tensor_tensor(rows[:], rows[:], up[0:1, 0, DT, :], ALU.add).then_inc(biased, 1)
            nc.vector.tensor_tensor(bias_y, bias_y, b2[:], ALU.add).then_inc(biased, 1)
            nc.vector.tensor_copy(w_up, up[:, 0, 0:DT, :]).then_inc(biased, 1)
            assert STAGES % 2 == 0 and n == OPS[0] * STAGES + 1
            dve.wait_ge(biased, 3)

        @block.gpsimd
        def _(pool):
            pool.wait_ge(loaded, 16 * 6)
            fold(nc.gpsimd, pool, down, tmp_down, 1, p_step, 0, [(t, slice(0, P)) for t in range(DT)])

        @block.tensor
        def _(pe):
            pe.wait_ge(biased, 2)
            for f in range(FT):
                mm = pe.matmul(BH[:, f:f + 1], rows[0:1, f * P:(f + 1) * P], one[:], start=True, stop=True)
            mm.then_inc(turned, 1)
            pe.wait_ge(p_step, OPS[1] * STAGES)
            for i in range(4):
                for j in range(2):
                    f = 2 * i + j
                    for t in range(DT):
                        mm = pe.transpose(TB[i][:, j, t * P:(t + 1) * P], down[:, 0, t, f * P:(f + 1) * P],
                                          sh.ident[:])
                mm.then_inc(turned, 1)

        @block.scalar
        def _(act):
            act.wait_ge(turned, 1)
            nc.scalar.activation(bias_h, BH[:], ACT.Copy).then_inc(done, 1)
            for i in range(4):
                act.wait_ge(turned, i + 2)
                nc.scalar.activation(w_down[:, 2 * i:2 * i + 2, :], TB[i][:], ACT.Copy).then_inc(done, 1)
            act.wait_ge(done, 5)


def butterfly_ffn(nc, sh, w):
    with ExitStack() as ctx:
        env = Env(nc, ctx, "ffn")
        sb, sem = env.sb, env.sem
        w_up = sb("wup", [P, DT, FH])
        w_down = sb("wdown", [P, FT, D])
        bias_h = sb("biash", [P, FT])
        bias_y = sb("biasy", [1, D])
        fold_butterflies(nc, w, w_up[:], w_down[:], bias_h[:], bias_y[:], sh)
        ones = sb("ones", [1, P])
        xin = sb("xin", [P, QT, D])
        xT = sb("xT", [P, DT, S])
        hT = sb("hT", [P, FT, S])
        stats = sb("stats", [P, QT, 6])
        mv = sb("mv", [P, QT, 2])
        scratch = sb("scratch", [P, 3, QT])
        X = [env.ps(f"X{i}", [P, S]) for i in range(DT)]
        H = [env.ps(f"H{i}", [P, S]) for i in range(2)]
        Y = [env.ps(f"Y{i}", [P, D]) for i in range(QT)]
        ready = sem("ready")
        xin_in = sem("xin_in")
        xt_full = sem("xt_full")
        xt_done = sem("xt_done")
        h_full = sem("h_full")
        h_done = sem("h_done")
        y_full = sem("y_full")
        y_read = sem("y_read")
        chain = sem("chain")
        block = ctx.enter_context(nc.Block())

        @block.sync
        def _(sp):
            sp.dma_start(xin[:], sh.x_all[:, 0:QT, :]).then_inc(xin_in, 16)
            with sp.Fori(1, B) as b:
                sp.wait_ge(xt_full, b * DT)
                sp.dma_start(xin[:], sh.x_all[:, bass.ds(b * QT, QT), :]).then_inc(xin_in, 16)

        @block.tensor
        def _(pe):
            def transpose_x(b):
                pe.wait_ge(xin_in, b * 16 + 16)
                for dt in range(DT):
                    for qt in range(QT):
                        mm = pe.transpose(X[dt][:, qt * P:(qt + 1) * P], xin[:, qt, dt * P:(dt + 1) * P], sh.ident[:])
                    mm.then_inc(xt_full, 1)

            def body(b, nxt):
                pe.wait_ge(xt_done, b * DT + DT)
                for f in range(FT):
                    pe.wait_ge(h_done, b * FT + (f + 1))
                    for t in range(DT):
                        mm = pe.matmul(H[f % 2][:], w_up[:, t, f * P:(f + 1) * P], xT[:, t, :], start=(t == 0),
                                       stop=(t == DT - 1))
                    mm.then_inc(h_full, 1)
                if nxt:
                    transpose_x(b + 1)
                for qt in range(QT):
                    pe.wait_ge(y_read, b * QT + (qt + 1))
                    for f in range(FT):
                        if qt == 0:
                            pe.wait_ge(h_done, b * FT + (f + 1 + 2))
                        mm = pe.matmul(Y[qt][:], hT[:, f, qt * P:(qt + 1) * P], w_down[:, f, :], start=(f == 0),
                                       stop=False)
                    mm = pe.matmul(Y[qt][:], ones[:], bias_y[:], start=False, stop=True)
                    mm.then_inc(y_full, 1)

            pe.wait_ge(ready, 1)
            transpose_x(0)
            with pe.Fori(0, B - 1) as b:
                body(b, True)
            body(B - 1, False)

        @block.scalar
        def _(act):
            act.sem_inc(h_done, 2)

            def copy_x(b):
                for dt in range(DT):
                    act.wait_ge(xt_full, b * DT + (dt + 1))
                    nc.scalar.activation(xT[:, dt, :], X[dt][:], ACT.Copy).then_inc(xt_done, 1)

            def body(b, nxt):
                for f in range(FT):
                    act.wait_ge(h_full, b * FT + (f + 1))
                    nc.scalar.activation(hT[:, f, :], H[f % 2][:], ACT.Gelu, bias=bias_h[:, f:f + 1]).then_inc(h_done, 1)
                if nxt:
                    copy_x(b + 1)

            copy_x(0)
            with act.Fori(0, B - 1) as b:
                body(b, True)
            body(B - 1, False)

        @block.vector
        def _(dve):
            nc.vector.memset(ones[:], 1.0).then_inc(ready, 1)
            dve.sem_inc(y_read, QT)
            with dve.Fori(0, B) as b:
                for qt in range(QT):
                    dve.wait_ge(y_full, b * QT + (qt + 1))
                    row = sh.x_all[:, b * QT + qt, :]
                    nc.vector.tensor_tensor(row, Y[qt][:], row, ALU.add).then_inc(y_read, 1)
                wait_apart(dve, (ready, 1), (y_read, b * QT + 2 * QT))
                steps = Chain(dve, chain, b * LN_LINKS, (ready, 1))
                layer_norm_rows(nc.vector, steps, lambda qt: sh.x_all[:, b * QT + qt, :], stats, mv, scratch)


def moe(nc, sh, w, out):
    TEMP = 1.5
    TOP = 2
    with ExitStack() as ctx:
        env = Env(nc, ctx, "moe")
        sb, sem = env.sb, env.sem
        xnT = sb("xnT", [P, DT, B * S])
        gates = sb("gates", [P, B * QT, NE])
        route(nc, sh, w, xnT, gates)
        w1 = sb("w1", [P, 2, DT, FH])
        w2 = sb("w2", [P, 2, FT, D])
        hT = sb("hT", [P, FT, S])
        stats = sb("stats", [P, QT, 6])
        mv = sb("mv", [P, QT, 2])
        scratch = sb("scratch", [P, 3, QT])
        H = [env.ps(f"H{i}", [P, S]) for i in range(2)]
        Y = [env.ps(f"Y{i}", [P, D]) for i in range(QT)]
        w_in = [sem(f"w_in{parity}") for parity in range(2)]
        h_full = sem("h_full")
        h_done = sem("h_done")
        y_full = sem("y_full")
        y_read = sem("y_read")
        chain = sem("chain")
        ready = sem("ready")
        stored = sem("stored")
        block = ctx.enter_context(nc.Block())
        BY, BH = B * QT, B * FT

        def load(sp, e, parity):
            sp.dma_start(w1[:, parity], w["w1"][e].rearrange("(t p) f -> p t f", p=P)).then_inc(w_in[parity], 16)
            sp.dma_start(w2[:, parity], w["w2"][e].rearrange("(t p) d -> p t d", p=P)).then_inc(w_in[parity], 16)

        @block.sync
        def _(sp):
            load(sp, 0, 0)
            load(sp, 1, 1)
            with sp.Fori(1, NE // 2) as pair:
                for parity in range(2):
                    sp.wait_ge(y_full, pair * 2 * BY + (parity - 1) * BY)
                    e = bass.ds(pair * 2 + parity, 1)
                    sp.dma_start(w1[:, parity], w["w1"][e].rearrange("e (t p) f -> p (e t) f", p=P)).then_inc(w_in[parity], 16)
                    sp.dma_start(w2[:, parity], w["w2"][e].rearrange("e (t p) d -> p (e t) d", p=P)).then_inc(w_in[parity], 16)
            with sp.Fori(0, B) as b:
                sp.wait_ge(chain, (b + 1) * LN_LINKS)
                sp.dma_start(out[bass.ds(b, 1)].rearrange("b (q p) d -> p (b q) d", p=P),
                             sh.x_all[:, bass.ds(b * QT, QT), :]).then_inc(stored, 16)
            sp.wait_ge(stored, 16 * B)

        @block.tensor
        def _(pe):
            with pe.Fori(0, NE // 2) as pair:
                for parity in range(2):
                    with pe.Fori(0, B) as b:
                        pe.wait_ge(w_in[parity], pair * 32 + 32)
                        for f in range(FT):
                            pe.wait_ge(h_done, pair * 2 * BH + b * FT + (parity * BH + f + 1))
                            for t in range(DT):
                                mm = pe.matmul(H[f % 2][:], w1[:, parity, t, f * P:(f + 1) * P],
                                               xnT[:, t, bass.ds(b * S, S)], start=(t == 0), stop=(t == DT - 1))
                            mm.then_inc(h_full, 1)
                        for qt in range(QT):
                            pe.wait_ge(y_read, pair * 2 * BY + b * QT + (parity * BY + qt + 1))
                            for f in range(FT):
                                if qt == 0:
                                    pe.wait_ge(h_done, pair * 2 * BH + b * FT + (parity * BH + f + 1 + 2))
                                mm = pe.matmul(Y[qt][:], hT[:, f, qt * P:(qt + 1) * P], w2[:, parity, f, :],
                                               start=(f == 0), stop=(f == FT - 1))
                            mm.then_inc(y_full, 1)

        @block.scalar
        def _(act):
            act.sem_inc(h_done, 2)
            with act.Fori(0, NE * B) as eb:
                for f in range(FT):
                    act.wait_ge(h_full, eb * FT + (f + 1))
                    nc.scalar.activation(hT[:, f, :], H[f % 2][:], ACT.Silu).then_inc(h_done, 1)

        @block.vector
        def _(dve):
            nc.vector.tensor_scalar(sh.x_all[:], sh.x_all[:], 2.0, None, ALU.mult).then_inc(ready, 1)
            dve.sem_inc(y_read, QT)
            dve.wait_ge(ready, 1)
            for e in range(NE):
                with dve.Fori(0, B) as b:
                    for qt in range(QT):
                        dve.wait_ge(y_full, b * QT + (e * BY + qt + 1))
                        row = sh.x_all[:, b * QT + qt, :]
                        nc.vector.scalar_tensor_tensor(out=row, in0=Y[qt][:],
                                                       scalar=gates[:, b * QT + qt, e:e + 1],
                                                       in1=row, op0=ALU.mult, op1=ALU.add).then_inc(y_read, 1)
                dve.wait_ge(y_read, (e + 1) * BY + QT)
            with dve.Fori(0, B) as b:
                steps = Chain(dve, chain, b * LN_LINKS, (ready, 1))
                layer_norm_rows(nc.vector, steps, lambda qt: sh.x_all[:, b * QT + qt, :], stats, mv, scratch)


def route(nc, sh, w, xnT, gates):
    TEMP, TOP = 1.5, 2
    with ExitStack() as ctx:
        env = Env(nc, ctx, "route")
        sb, sem = env.sb, env.sem
        xhat = sb("xhat", [P, QT, D])
        xn_b = sb("xnb", [P, DT, S])
        gamma = sb("gamma", [P, DT])
        beta = sb("beta", [P, DT])
        router = sb("router", [P, DT, NE])
        iota = sb("iota", [P, NE])
        stats = sb("stats", [P, QT, 6])
        mv = sb("mv", [P, QT, 2])
        scratch = sb("scratch", [P, 3, QT])
        logit = sb("logit", [P, QT, NE])
        top = sb("top", [P, QT, 1])
        total = sb("total", [P, QT, 1])
        best = sb("best", [P, QT, 8])
        index = sb("index", [P, QT, 8], U32)
        index_f = sb("indexf", [P, QT, 8])
        pick = sb("pick", [P, QT, TOP, NE])
        X = [env.ps(f"X{i}", [P, QT, P]) for i in range(DT)]
        R = env.ps("R", [P, QT, NE])
        loaded = sem("loaded")
        ready = sem("ready")
        chain = sem("chain")
        xt_full = sem("xt_full")
        xt_done = sem("xt_done")
        routed = sem("routed")
        exped = sem("exped")
        saved = sem("saved")
        block = ctx.enter_context(nc.Block())
        LOGIT_LINKS = 11
        PER = LN_LINKS + LOGIT_LINKS
        SHIFTED = LN_LINKS + 3

        @block.sync
        def _(sp):
            sp.dma_start(gamma[:], w["gamma"]).then_inc(loaded, 16)
            sp.dma_start(beta[:], w["beta"]).then_inc(loaded, 16)
            sp.dma_start(router[:], w["router_wT"].rearrange("(t p) e -> p t e", p=P)).then_inc(loaded, 16)
            sp.dma_start(iota[:], w["iota"]).then_inc(loaded, 16)

        @block.tensor
        def _(pe):
            pe.wait_ge(loaded, 64)
            with pe.Fori(0, B) as b:
                pe.wait_ge(chain, b * PER + LN_LINKS)
                for dt in range(DT):
                    pe.wait_ge(xt_done, b * DT + (dt + 1))
                    for qt in range(QT):
                        mm = pe.transpose(X[dt][:, qt, :], xhat[:, qt, dt * P:(dt + 1) * P], sh.ident[:])
                    mm.then_inc(xt_full, 1)
                pe.wait_ge(xt_done, b * DT + 2 * DT)
                for qt in range(QT):
                    for dt in range(DT):
                        mm = pe.matmul(R[:, qt, :], xn_b[:, dt, qt * P:(qt + 1) * P], router[:, dt, :],
                                       start=(dt == 0), stop=(dt == DT - 1))
                mm.then_inc(routed, 1)

        @block.scalar
        def _(act):
            act.sem_inc(xt_done, DT)
            act.sem_inc(saved, DT)
            act.wait_ge(loaded, 64)
            with act.Fori(0, B) as b:
                for dt in range(DT):
                    act.wait_ge(saved, b * DT + (dt + 1))
                    act.wait_ge(xt_full, b * DT + (dt + 1))
                    nc.scalar.activation(xn_b[:, dt, :], X[dt][:].rearrange("p a b -> p (a b)"), ACT.Identity,
                                         bias=beta[:, dt:dt + 1], scale=gamma[:, dt:dt + 1]).then_inc(xt_done, 1)
                act.wait_ge(chain, b * PER + SHIFTED)
                nc.scalar.activation(logit[:], logit[:], ACT.Exp).then_inc(exped, 1)

        @block.gpsimd
        def _(pool):
            with pool.Fori(0, B) as b:
                for dt in range(DT):
                    pool.wait_ge(xt_done, b * DT + (dt + 1 + DT))
                    nc.gpsimd.tensor_copy(xnT[:, dt, bass.ds(b * S, S)], xn_b[:, dt, :]).then_inc(saved, 1)

        @block.vector
        def _(dve):
            nc.vector.memset(top[:], 0.0).then_inc(ready, 1)
            dve.wait_ge(loaded, 64)
            dve.wait_ge(ready, 1)
            with dve.Fori(0, B) as b:
                nv = nc.vector
                steps = Chain(dve, chain, b * PER, (ready, 1))
                layer_norm_rows(nv, steps, lambda qt: sh.x_all[:, b * QT + qt, :], stats, mv, scratch,
                                lambda qt: xhat[:, qt, :])
                wait_apart(dve, (ready, 1), (routed, b + 1))
                steps.link(nv.tensor_scalar(logit[:], R[:], 1.0 / TEMP, None, ALU.mult))
                steps.link(nv.tensor_reduce(top[:, :, 0], logit[:], AX_X, ALU.max))
                steps.link(nv.tensor_tensor(logit[:], logit[:], top[:].to_broadcast([P, QT, NE]), ALU.subtract))
                wait_apart(dve, (ready, 1), (exped, b + 1))
                steps.link(nv.tensor_reduce(total[:, :, 0], logit[:], AX_X, ALU.add))
                steps.link(nv.reciprocal(total[:], total[:]))
                steps.link(nv.tensor_tensor(logit[:], logit[:], total[:].to_broadcast([P, QT, NE]), ALU.mult))
                for qt in range(QT):
                    ins = nv.max(best[:, qt, :], logit[:, qt, :])
                steps.link(ins)
                for qt in range(QT):
                    ins = nv.max_index(index[:, qt, :], best[:, qt, :], logit[:, qt, :])
                steps.link(ins)
                steps.link(nv.tensor_copy(index_f[:], index[:]))
                for qt in range(QT):
                    for k in range(TOP):
                        ins = nv.tensor_scalar(pick[:, qt, k, :], iota[:], index_f[:, qt, k:k + 1],
                                               best[:, qt, k:k + 1], ALU.is_equal, ALU.mult)
                steps.link(ins)
                steps.link(nv.tensor_tensor(gates[:, bass.ds(b * QT, QT), :], pick[:, :, 0, :], pick[:, :, 1, :],
                                            ALU.add))
                assert steps.n == PER, steps.n


_INS = ("x", "ident", "decay", "causal", "cos", "sin", "head_mask4", "head_mask8", "iota", "ctx", "ctxT", "mask",
        "a0_w_q", "a0_w_kT", "a0_w_vT", "a0_w_down", "a0_w_up_k", "a0_w_up_v", "a0_w_o",
        "f0_w_exp", "f0_b_exp", "f0_up_weights", "f0_up_bias", "f0_down_weights", "f0_w_conT", "f0_b_con",
        "f0_down_bias",
        "a1_w_q", "a1_w_q_swapped", "a1_w_down", "a1_w_up_k", "a1_w_up_k_swapped", "a1_w_up_v", "a1_w_o",
        "x1_w_q", "x1_w_k1", "x1_w_v1", "x1_w_k2", "x1_w_v2", "x1_w_o", "x1_b_o",
        "f1_gamma", "f1_beta", "f1_router_wT", "f1_w1", "f1_w2")


def decoder(nc, *args):
    w, out = dict(zip(_INS, args)), args[-1]

    def part(prefix, **more):
        return {n[len(prefix):]: a for n, a in w.items() if n.startswith(prefix)} | more

    with ExitStack() as ctx:
        sh = Shared(nc, ctx)
        load_block(nc, sh, w["x"], w["ident"])
        attention(nc, sh, "a0", part("a0_", decay=w["decay"], head_mask=w["head_mask4"]))
        cross_attention_heads(nc, sh, {n: w[n] for n in ("ctx", "ctxT", "mask", "head_mask8")})
        butterfly_ffn(nc, sh, part("f0_"))
        attention(nc, sh, "a1", part("a1_", causal=w["causal"], cos=w["cos"], sin=w["sin"]))
        attention(nc, sh, "x1", part("x1_", ctxT=w["ctxT"]))
        moe(nc, sh, part("f1_", iota=w["iota"]), out)


def shape_constants():
    f = np.float32
    p = np.arange(P)
    far = np.abs(p[:, None] - (np.arange(2 * S - P)[None, :] - (S - P))).astype(f)
    key = np.arange(S)[None, :] - (S - P)
    inv_freq = f(1) / f(10000.0) ** (np.arange(0, 64, 2, dtype=f) / f(64))
    angle = np.arange(S, dtype=f)[:, None] * inv_freq[None, :]
    angle = np.concatenate([angle, angle], 1)
    cos, sin = np.cos(angle).T, np.sin(angle).T.copy()
    sin[:32] *= -1
    return {"ident": np.eye(P, dtype=f),
            "decay": np.exp(f(-0.01) * far),
            "causal": np.where(key <= p[:, None], f(0), f(-1e30)),
            "cos": np.concatenate([cos, cos]), "sin": np.concatenate([sin, sin]),
            "head_mask4": ((p[:, None] % 64) // 16 == np.arange(4)[None, :]).astype(f),
            "head_mask8": (p[:, None] // 16 == np.arange(8)[None, :]).astype(f),
            "iota": np.tile(np.arange(NE, dtype=f), (P, 1))}


def laid_out(a):
    def split_pairs(wt):
        n = wt.shape[0]
        return wt.reshape(n, 2, 4, 2, 16).transpose(0, 1, 3, 2, 4).reshape(n, 4, 64)

    def swapped(wt):
        n = wt.shape[0]
        return wt.reshape(n, -1, 2, 32)[:, :, ::-1].reshape(n, -1)

    row = (1, -1)
    wq1, wku1 = a["L1_attn_wq"].T, a["L1_attn_w_k_up"].T
    return {"x": a["x"], "ctx": a["ctx_1024"], "ctxT": a["ctx_1024"].transpose(0, 2, 1), "mask": a["mask_BxSxS2_ik1"],
            "a0_w_q": split_pairs(a["L0_attn_W_q"]), "a0_w_kT": a["L0_attn_W_k"].T, "a0_w_vT": a["L0_attn_W_v"].T,
            "a0_w_down": a["L0_attn_W_down_kv"], "a0_w_up_k": split_pairs(a["L0_attn_W_up_k"]),
            "a0_w_up_v": a["L0_attn_W_up_v"], "a0_w_o": a["L0_attn_W_o"],
            "f0_w_exp": a["L0_ffn_W_exp"], "f0_b_exp": a["L0_ffn_b_exp"].reshape(row),
            "f0_up_weights": a["L0_ffn_up_weights"].reshape(STAGES, 1, 2 * FH),
            "f0_up_bias": a["L0_ffn_up_bias"].reshape(row),
            "f0_down_weights": a["L0_ffn_down_weights"].reshape(STAGES, 1, 2 * FH),
            "f0_w_conT": a["L0_ffn_W_con"].T, "f0_b_con": a["L0_ffn_b_con"].reshape(row),
            "f0_down_bias": a["L0_ffn_down_bias"].reshape(row),
            "a1_w_q": wq1, "a1_w_q_swapped": swapped(wq1), "a1_w_down": a["L1_attn_w_kv_down"].T,
            "a1_w_up_k": wku1, "a1_w_up_k_swapped": swapped(wku1), "a1_w_up_v": a["L1_attn_w_v_up"].T,
            "a1_w_o": a["L1_attn_wo"].T,
            "x1_w_q": a["L1_xattn_Wq1"], "x1_w_k1": a["L1_xattn_Wk1"], "x1_w_v1": a["L1_xattn_Wv1"],
            "x1_w_k2": a["L1_xattn_Wk2"], "x1_w_v2": a["L1_xattn_Wv2"], "x1_w_o": a["L1_xattn_Wo"],
            "x1_b_o": a["L1_xattn_bo"].reshape(row),
            "f1_gamma": a["L1_ffn_gamma"].reshape(DT, P).T, "f1_beta": a["L1_ffn_beta"].reshape(DT, P).T,
            "f1_router_wT": a["L1_ffn_router_w"].T, "f1_w1": a["L1_ffn_W1"], "f1_w2": a["L1_ffn_W2"]}


def kernel(**inputs):
    import concourse.bacc as bacc
    from concourse.bass_utils import run_bass_kernel_spmd

    host = laid_out({n: np.asarray(a) for n, a in inputs.items()}) | shape_constants()
    nc = bacc.Bacc("TRN2", target_bir_lowering=False, num_devices=1)
    arrays, args = {}, []
    for name in _INS:
        a = np.ascontiguousarray(host[name])
        arrays[f"in_{name}_dram"] = a
        args.append(nc.dram_tensor(f"in_{name}_dram", a.shape, mybir.dt.from_np(a.dtype), kind="ExternalInput").ap())
    args.append(nc.dram_tensor("out_dram", (B, S, D), F32, kind="ExternalOutput").ap())
    decoder(nc, *args)
    r = run_bass_kernel_spmd(nc, [arrays], core_ids=[0])
    return r.results[0]["out_dram"]
```

```python
from contextlib import ExitStack

import numpy as np

import concourse.bass as bass
from concourse import mybir

F32 = mybir.dt.float32
F32R = mybir.dt.float32r
I32 = mybir.dt.int32
U32 = mybir.dt.uint32
ALU = mybir.AluOpType
ACT = mybir.ActivationFunctionType
AX_X = mybir.AxisListType.X

P = 128
B, S, D = 8, 512, 256
SC = 64
QT = S // P
DT = D // P
FH = 4 * D
FT = FH // P
STAGES = 10
NE = 8
EPS = 1e-5
LOWEST = -3.0e38
A_BANKS = 4


class Env:

    def __init__(self, nc, ctx, prefix):
        self.nc, self.ctx, self.prefix = nc, ctx, prefix

    def sb(self, name, shape, dt=F32):
        return self.ctx.enter_context(self.nc.sbuf_tensor(f"{self.prefix}_{name}", shape, dt))

    def ps(self, name, shape, dt=F32):
        return self.ctx.enter_context(self.nc.psum_tensor(f"{self.prefix}_{name}", shape, dt))

    def sem(self, name):
        return self.ctx.enter_context(self.nc.semaphore(f"{self.prefix}_{name}"))


def wait_apart(eng, met, *waits):
    waits = [(sem, value if isinstance(value, int) else eng.to_reg(value)) for sem, value in waits]
    eng.wait_ge(*met)
    for sem, value in waits:
        eng.wait_ge(sem, value)


class Chain:

    def __init__(self, eng, sem, base, met):
        self.eng, self.sem, self.base, self.n, self.met = eng, sem, base, 0, met

    def mark(self, ins):
        self.n += 1
        ins.then_inc(self.sem, 1)

    def settle(self):
        wait_apart(self.eng, self.met, (self.sem, self.base + self.n))

    def link(self, ins):
        self.mark(ins)
        self.settle()


class Segment:

    def __init__(self, jobs, sems, base, last, n=A_BANKS):
        self.n, self.sems, self.base = n, sems, dict(base)
        self.number = {name: i for i, (name, _) in enumerate(jobs)}
        self.reader = dict(jobs)
        assert len(self.number) == len(jobs)
        self.per = {r: sum(x == r for _, x in jobs) for r in sems}
        self.per["full"] = len(jobs)
        self.count, self.before, last, seen = {}, {}, list(last), dict.fromkeys(sems, 0)
        for k, (name, r) in enumerate(jobs):
            seen[r] += 1
            self.count[name] = seen[r]
            self.before[name] = last[k % n]
            last[k % n] = (r, seen[r])
        self.end = {r: self.base[r] + self.per[r] for r in self.base}
        self.last = [(r, k - self.per[r]) for r, k in last]

    def bank(self, name):
        return self.number[name] % self.n

    def _at(self, r, turn, k):
        return self.sems[r], turn * self.per[r] + (self.base[r] + k)

    def full(self, turn, name):
        return self._at("full", turn, self.number[name] + 1)

    def empty(self, turn, name):
        return self._at(self.before[name][0], turn, self.before[name][1])

    def emptied(self, turn, name):
        return self._at(self.reader[name], turn, self.count[name])


def layer_norm_rows(nv, steps, row, stats, mv, scratch, to=None):
    to = to or row
    for qt in range(QT):
        ins = nv.bn_stats(stats[:, qt, :], row(qt))
    steps.mark(ins)
    yield
    steps.settle()
    for qt in range(QT):
        ins = nv.bn_aggr(mv[:, qt, :], stats[:, qt, :])
    steps.mark(ins)
    for _ in rsqrt_columns(nv, steps, mv[:, :, 1], scratch):
        yield
    steps.settle()
    for qt in range(QT):
        ins = nv.tensor_scalar(to(qt), row(qt), mv[:, qt, 0:1], scratch[:, 1, qt:qt + 1],
                               ALU.subtract, ALU.mult)
    steps.mark(ins)
    yield
    steps.settle()


def rsqrt_columns(nv, steps, var, scratch):
    v, y, t = scratch[:, 0, :], scratch[:, 1, :], scratch[:, 2, :]
    yield
    steps.settle()
    steps.mark(nv.tensor_scalar(v, var, EPS, None, ALU.add))
    yield
    steps.settle()
    steps.mark(nv.tensor_scalar(t.bitcast(I32), v.bitcast(I32), 1, None, ALU.arith_shift_right))
    yield
    steps.settle()
    steps.mark(nv.tensor_scalar(y.bitcast(I32), t.bitcast(I32), -1, 0x5F3759DF, ALU.mult, ALU.add))
    for _ in range(3):
        yield
        steps.settle()
        steps.mark(nv.tensor_tensor(t, y, y, ALU.mult))
        yield
        steps.settle()
        steps.mark(nv.scalar_tensor_tensor(out=t, in0=t, scalar=-0.5, in1=v, op0=ALU.mult, op1=ALU.mult))
        yield
        steps.settle()
        steps.mark(nv.scalar_tensor_tensor(out=y, in0=t, scalar=1.5, in1=y, op0=ALU.add, op1=ALU.mult))
    yield


DONE = object()


def advance(work, n=None):
    while n is None or n > 0:
        if next(work, DONE) is DONE:
            return
        n = n - 1 if n is not None else None


LN_LINKS = 3 + 3 + 3 * 3


class Shared:

    def __init__(self, nc, ctx):
        self.x_all = ctx.enter_context(nc.sbuf_tensor("x_all", [P, B * QT, D], F32))
        self.ident = ctx.enter_context(nc.sbuf_tensor("ident", [P, P], F32))


def load_block(nc, sh, x, ident):
    with ExitStack() as ctx:
        env = Env(nc, ctx, "load")
        loaded = env.sem("loaded")
        block = ctx.enter_context(nc.Block())

        @block.sync
        def _(sp):
            sp.dma_start(sh.ident[:], ident).then_inc(loaded, 16)
            sp.dma_start(sh.x_all[:, :, :], x.rearrange("b (q p) d -> p (b q) d", p=P)).then_inc(loaded, 16)
            sp.wait_ge(loaded, 32)


def attention(nc, sh, kind, w):
    a0, a1, x1 = kind == "a0", kind == "a1", kind == "x1"
    G = {"a0": 4, "a1": 4, "x1": 2}[kind]
    ITEMS = {"a0": 2, "a1": 4, "x1": 5}[kind]
    U = G * QT
    NK = S + SC if x1 else S
    PAIRS = 2 * G
    SCALE = 1.0 / 16.0 if a0 else 0.125
    LAG_E, LAG_N, LAG_T, LAG_V = 1, 2, 3, 4
    Y_AT = [(LAG_V, 0), (LAG_V, 2), (LAG_V + 1, 0), (LAG_V + 1, 2)] if x1 else [(LAG_V + i, 0) for i in range(QT)]
    LN_STEP = Y_AT[-1][0] + 1
    POOL_HEADS = () if a1 else (2, 3)
    DVE_HEADS = 4 - len(POOL_HEADS)
    V_CUT = 256
    IN = FH if a1 else 512
    N_V = {"a0": 2, "a1": 2 * G, "x1": 3 * G}[kind]

    def keys(u):
        return (u % QT + 1) * P if a1 else S

    V_OF = {g: [("v", g, i) for i in range(N_V // G)] for g in range(G)} if not a0 else {}

    def tasks(s, prev, own, nxt):
        found = [(j, ("y", qt)) for qt, (at, j) in enumerate(Y_AT) if prev and at == s]
        if not own:
            return found
        g, at = divmod(s, QT)
        if a0 and s == LAG_V - 1:
            found += [(4, ("v", 0, i)) for i in range(N_V)]
        if g + 1 < G:
            items = {"a0": ([0], [1], [], []), "a1": ([0, 1], [2, 3], [], []), "x1": ([0, 1], [2, 3], [4], [])}[kind]
            works = [("item", g + 1, i) for i in items[at]]
            values = {"a0": [], "a1": V_OF and V_OF[g + 1][at - 2:at - 1] if at >= 2 else [],
                      "x1": V_OF and V_OF[g + 1] if at == 3 else []}[kind]
        elif nxt:
            items = {"a0": ([], [0], [1], []), "a1": ([], [0, 1], [2, 3], []), "x1": ([], [0, 1], [2, 3], [4])}[kind]
            works = ([("xT",)] + ([("lat",)] if not x1 else []) if at == 0 else []) + \
                [("item", 0, i) for i in items[at]]
            values = V_OF[0] if at == 3 and not a0 else []
        else:
            return found
        found += [(1 + 2 * k if len(works) > 1 else 1, work) for k, work in enumerate(works)]
        return found + [(4 if x1 or at == 3 else 3, work) for work in values]

    START = [("xT",)] + ([("lat",)] if not x1 else []) + [("item", 0, i) for i in range(ITEMS)] + \
        (V_OF[0] if not a0 else [])

    def work_jobs(work):
        if work[0] == "xT":
            return [(("xT", dt), "xt") for dt in range(DT)]
        if work[0] == "lat":
            return [("lat", "act")]
        if work[0] == "v":
            return [(work, "dve" if a0 else "v")]
        if work[0] == "y":
            return [(work, "dve")]
        if a1:
            return [((*work, 0), "dve"), ((*work, 1), "rot")]
        if x1:
            return [(work, "ql")]
        return [(work, ("dve", "kl")[work[2]])]

    def segment_jobs(prev, own, nxt):
        jobs = []
        for s in range(U if own else LN_STEP):
            found = tasks(s, prev, own, nxt)
            for j in range(5):
                if own and j < (5 if x1 else 4):
                    jobs += [(("score", s, j), "dve")]
                jobs += [job for at, work in found if at == j for job in work_jobs(work)]
        return jobs

    NEXT = START

    T_UNIT = 5 if x1 else 4
    T_JOBS = U * T_UNIT
    T_CREDIT = 4 * T_UNIT
    N_O = 2 if a0 else 2 * G
    HI_GROUP = {"a0": 2, "a1": 6, "x1": 10}[kind]
    LOW_GROUP = {"a0": 4, "a1": 6, "x1": 0}[kind]
    LOW_ITEM = {"a1": (1, 3, 4, 6)}.get(kind)
    HI_ITEM = {"a0": (1, 2), "a1": (1, 3, 4, 6), "x1": (1, 2, 4, 6, 10)}[kind]

    with ExitStack() as ctx:
        env = Env(nc, ctx, kind)
        sb, sem = env.sb, env.sem
        xin = sb("xin", [P, QT, D])
        xT = sb("xT", [P, DT, S])
        widths = [4 * keys(u) if a1 else 4 * NK for u in range(4)]
        tiles = [12, 16] if a1 else [20 if x1 else 16] * 2
        t_buf = sb("t", [P, sum(widths)])
        p_T = sb("pT", [P, sum(tiles), P])
        mx = sb("mx", [P, 4, 4])
        mx1 = sb("mx1", [P, 4, 4])
        neg = sb("neg", [P, 4, 4])
        total = sb("total", [P, 4, 4])
        inv = sb("inv", [P, 4, 4])
        stats = sb("stats", [P, QT, 6])
        mv = sb("mv", [P, QT, 2])
        scratch = sb("scratch", [P, 3, QT])
        oT = sb("oT", [P, 2 if a0 else PAIRS, S])
        wo = sb("wo", [P, 2 if a0 else PAIRS, D])
        kpad = sb("kpad", [P, 2, 2, 4, NK], F32R)
        if a0:
            qs = sb("qs", [P, 2, S], F32R)
            kh = sb("kh", [P, S], F32R)
            kl = sb("kl", [P, S], F32R)
            lat = sb("lat", [64, S])
            v_sb = sb("v", [P, QT, 16, 32])
            wq = sb("wq", [P, DT, G, P])
            wkd = sb("wkd", [P, DT, 64])
            wupk = sb("wupk", [64, G, P])
            wupv = sb("wupv", [64, D])
            wkT = sb("wkT", [P, DT, D])
            wvT = sb("wvT", [P, DT, D])
            wdn = sb("wdn", [P, DT, 64])
            table = sb("decay", [P, 2 * S - P])
            hmask = sb("hmask", [P, 4])
        else:
            q_hl = sb("qhl", [P, 2, 2, 2, S], F32R)
            v_sb = sb("v", [P, QT, IN])
            wq = sb("wq", [P, DT, IN])
            table = sb("table", [P, S])
        if a1:
            wqs = sb("wqs", [P, DT, IN])
            lat = sb("lat", [P, S])
            wdn = sb("wdn", [P, DT, P])
            wupk = sb("wupk", [P, 2, IN])
            wupv = sb("wupv", [P, IN])
            cos = sb("cos", [P, S])
            sin = sb("sin", [P, S])
            rsum = sb("rsum", [P, 2, S])
            rsin = sb("rsin", [P, S])
        if x1:
            v2 = sb("v2", [SC, IN])
            ctxT = sb("ctxT", [P, DT, SC])
            wk1 = sb("wk1", [P, DT, IN])
            wv1 = sb("wv1", [P, DT, IN])
            wk2 = sb("wk2", [P, DT, IN])
            wv2 = sb("wv2", [P, DT, IN])
            bo = sb("bo", [1, D])
            ones = sb("ones", [1, P])

        A = [env.ps(f"A{i}", [P, 512]) for i in range(A_BANKS)]
        T = [env.ps(f"T{i}", [P, 4, P]) for i in range(2)]
        O = [env.ps(f"O{i}", [P, S]) for i in range(2)]

        weights = sem("weights")
        ready = sem("ready")
        folded = sem("folded")
        xin_in = sem("xin_in")
        ctx_in = sem("ctx_in")
        a_full = sem("a_full")
        a_act = sem("a_act")
        xt_done = sem("xt_done")
        v_done = sem("v_done")
        a_dve = sem("a_dve")
        hi = sem("hi")
        rot_sum = sem("rot_sum")
        kl_done = sem("kl_done")
        rot_done = sem("rot_done")
        low = sem("low")
        kp = sem("kp")
        negated = sem("negated")
        exped = sem("exped")
        normed = sem("normed")
        normed_pool = sem("normed_pool")
        t_full = sem("t_full")
        t_empty = sem("t_empty")
        pv = sem("pv")
        o_empty = sem("o_empty")
        inverted = sem("inverted")
        q_low = sem("q_low")
        chain = sem("chain")
        sems = {"full": a_full, "act": a_act, "dve": a_dve, "xt": xt_done, "v": v_done,
                "kl": kl_done, "rot": rot_done, "ql": q_low}
        zero = dict.fromkeys(sems, 0) | {"dve": A_BANKS}
        start = Segment([j for work in START for j in work_jobs(work)], sems, zero,
                        [("dve", 0)] * A_BANKS)
        first = Segment(segment_jobs(False, True, True), sems, start.end, start.last)
        steady = Segment(segment_jobs(True, True, True), sems, first.end, first.last)
        assert steady.last == first.last
        looped = {r: steady.base[r] + (B - 2) * steady.per[r] for r in steady.base}
        final = Segment(segment_jobs(True, True, False), sems, looped, steady.last)
        tail = Segment(segment_jobs(True, False, False), sems, final.end, final.last)

        def batches(eng, begin, body):
            begin()
            body(first, 0, 0, prev=False, own=True, nxt=True)
            with eng.Fori(1, B - 1) as b:
                body(steady, b - 1, b, prev=True, own=True, nxt=True)
            body(final, 0, B - 1, prev=True, own=True, nxt=False)
            body(tail, 0, B, prev=True, own=False, nxt=False)

        def t_of(u, j, lo, hi):
            at = sum(widths[:u % 4]) + j * widths[u % 4] // 4
            return t_buf[:, at + lo:at + hi]

        def p_tile(u, j, kt, n=1):
            at = (u % 2) * tiles[0] + j * tiles[u % 2] // 4 + kt
            return p_T[:, at:at + n, :] if n > 1 else p_T[:, at, :]

        block = ctx.enter_context(nc.Block())

        def tiled(x):
            return x.rearrange("(t p) n -> p t n", p=P)

        loads = [(wo[:], tiled(w["w_o"]))]
        if a0:
            w_q = w["w_q"].rearrange("(t p) g c -> p t g c", p=P)
            for t in range(DT):
                loads += [(wq[:, t, :, 0:64], w_q[:, t]), (wq[:, t, :, 64:128], w_q[:, t])]
            loads += [(wkT[:], tiled(w["w_kT"])), (wvT[:], tiled(w["w_vT"])), (wdn[:], tiled(w["w_down"])),
                      (wupk[:, :, 0:64], w["w_up_k"]), (wupk[:, :, 64:128], w["w_up_k"]),
                      (wupv[:], w["w_up_v"]), (table[:], w["decay"]), (hmask[:], w["head_mask"])]
        if a1:
            loads += [(wq[:], tiled(w["w_q"])), (wqs[:], tiled(w["w_q_swapped"])), (wdn[:], tiled(w["w_down"])),
                      (wupk[:, 0, :], w["w_up_k"]), (wupk[:, 1, :], w["w_up_k_swapped"]),
                      (wupv[:], w["w_up_v"]), (table[:], w["causal"]), (cos[:], w["cos"]), (sin[:], w["sin"])]
        if x1:
            loads += [(wq[:], tiled(w["w_q"])), (wk1[:], tiled(w["w_k1"])), (wv1[:], tiled(w["w_v1"])),
                      (wk2[:], tiled(w["w_k2"])), (wv2[:], tiled(w["w_v2"])), (bo[:], w["b_o"])]
        N_READY = {"a0": 3, "a1": 1, "x1": 3}[kind]

        @block.sync
        def _(sp):
            sp.dma_start(xin[:], sh.x_all[:, 0:QT, :]).then_inc(xin_in, 16)
            for to, src in loads:
                sp.dma_start(to, src).then_inc(weights, 16)
            if x1:
                sp.dma_start(ctxT[:], tiled(w["ctxT"][0])).then_inc(ctx_in, 16)
            with sp.Fori(1, B) as b:
                sp.wait_ge(xt_done, b * DT)
                sp.dma_start(xin[:], sh.x_all[:, bass.ds(b * QT, QT), :]).then_inc(xin_in, 16)
                if x1:
                    sp.wait_ge(v_done, b * N_V)
                    sp.dma_start(ctxT[:], w["ctxT"][bass.ds(b, 1)].rearrange("a (t p) n -> p (a t) n", p=P))\
                      .then_inc(ctx_in, 16)

        @block.tensor
        def _(pe):
            pe.sem_inc(t_full, T_CREDIT)
            pe.sem_inc(pv, 2)
            pe.wait_ge(weights, 16 * len(loads))
            if a0:
                pe.wait_ge(ready, 1)
                for dt in range(DT):
                    for t in range(DT):
                        mm = pe.matmul(A[0][:, 64 * dt:64 * dt + 64], wkT[:, t, dt * P:(dt + 1) * P], wdn[:, t, :],
                                       start=(t == 0), stop=(t == DT - 1))
                mm.then_inc(folded, 1)
            pe.wait_ge(ready, N_READY)

            def project(seg, turn, b, work):
                if work[0] == "xT":
                    pe.wait_ge(xin_in, b * 16 + 16)
                    for dt in range(DT):
                        name = ("xT", dt)
                        pe.wait_ge(*seg.empty(turn, name))
                        bank = A[seg.bank(name)]
                        for qt in range(QT):
                            mm = pe.transpose(bank[:, qt * P:(qt + 1) * P], xin[:, qt, dt * P:(dt + 1) * P],
                                              sh.ident[:])
                        mm.then_inc(a_full, 1)
                    pe.wait_ge(xt_done, b * DT + DT)
                    return
                if work[0] == "lat":
                    pe.wait_ge(*seg.empty(turn, "lat"))
                    bank = A[seg.bank("lat")]
                    wl, rows_l = (wkd, 64) if a0 else (wdn, P)
                    for t in range(DT):
                        mm = pe.matmul(bank[0:rows_l, :], wl[:, t, :], xT[:, t, :], start=(t == 0), stop=(t == DT - 1))
                    mm.then_inc(a_full, 1)
                    return
                _, g, i = work
                if a1:
                    pair = 2 * g + i // 2
                    col = slice(pair * P, (pair + 1) * P)
                    if g == 0 and i == 1:
                        pe.wait_ge(a_act, b + 1)
                    for sw in range(2):
                        name = (*work, sw)
                        pe.wait_ge(*seg.empty(turn, name))
                        bank = A[seg.bank(name)]
                        if i % 2 == 0:
                            for t in range(DT):
                                mm = pe.matmul(bank[:], (wq, wqs)[sw][:, t, col], xT[:, t, :],
                                               start=(t == 0), stop=(t == DT - 1))
                        else:
                            mm = pe.matmul(bank[:], wupk[:, sw, col], lat[:], start=True, stop=True)
                        mm.then_inc(a_full, 1)
                    return
                pe.wait_ge(*seg.empty(turn, work))
                bank = A[seg.bank(work)]
                if a0 and i == 0:
                    for t in range(DT):
                        mm = pe.matmul(bank[:], wq[:, t, g, :], xT[:, t, :], start=(t == 0), stop=(t == DT - 1))
                elif a0:
                    if g == 0:
                        pe.wait_ge(a_act, b + 1)
                    mm = pe.matmul(bank[:], wupk[:, g, :], lat[:], start=True, stop=True)
                elif i < 4:
                    pair = 2 * g + i % 2
                    for t in range(DT):
                        mm = pe.matmul(bank[:], (wq, wk1)[i // 2][:, t, pair * P:(pair + 1) * P], xT[:, t, :],
                                       start=(t == 0), stop=(t == DT - 1))
                else:
                    pe.wait_ge(ctx_in, b * 16 + 16)
                    for pr in range(2):
                        pair = 2 * g + pr
                        for t in range(DT):
                            mm = pe.matmul(bank[:, pr * SC:(pr + 1) * SC], wk2[:, t, pair * P:(pair + 1) * P],
                                           ctxT[:, t, :], start=(t == 0), stop=(t == DT - 1))
                mm.then_inc(a_full, 1)

            def values(seg, turn, b, work):
                _, g, i = work
                pe.wait_ge(*seg.empty(turn, work))
                bank = A[seg.bank(work)]
                col = slice(g * V_CUT, (g + 1) * V_CUT)
                if x1 and i == 2:
                    pe.wait_ge(ctx_in, b * 16 + 16)
                    for t in range(DT):
                        mm = pe.matmul(bank[0:SC, 0:V_CUT], ctxT[:, t, :], wv2[:, t, col],
                                       start=(t == 0), stop=(t == DT - 1))
                else:
                    if not x1 and g == 0:
                        pe.wait_ge(a_act, b + 1)
                    for k in range(2):
                        out, kt = bank[:, k * V_CUT:(k + 1) * V_CUT], slice((2 * i + k) * P, (2 * i + k + 1) * P)
                        if x1:
                            for t in range(DT):
                                mm = pe.matmul(out, xT[:, t, kt], wv1[:, t, col], start=(t == 0), stop=(t == DT - 1))
                        else:
                            mm = pe.matmul(out, lat[:, kt], wupv[:, col], start=True, stop=True)
                mm.then_inc(a_full, 1)

            def finish(seg, turn, b, work):
                qt = work[1]
                pe.wait_ge(o_empty, b * N_O + 2)
                pe.wait_ge(*seg.empty(turn, work))
                bank = A[seg.bank(work)]
                n_o = 2 if a0 else PAIRS
                for t in range(n_o):
                    mm = pe.matmul(bank[:, 0:D], oT[:, t, qt * P:(qt + 1) * P], wo[:, t, :], start=(t == 0),
                                   stop=(t == n_o - 1 and not x1))
                if x1:
                    mm = pe.matmul(bank[:, 0:D], ones[:], bo[:], start=False, stop=True)
                mm.then_inc(a_full, 1)

            def score_head(seg, turn, b, u, j):
                g, qt = divmod(u, QT)
                gp = g % 2
                q = slice(qt * P, (qt + 1) * P)
                if qt == 0 and j == 0:
                    if a0:
                        pe.wait_ge(kp, b * 4 * G + 4 * (g + 1))
                        pe.wait_ge(low, b * 4 * G + 4 * (g + 1) + 4)
                    elif a1:
                        pe.wait_ge(low, b * LOW_GROUP * G + LOW_GROUP * (g + 2))
                    else:
                        pe.wait_ge(q_low, b * ITEMS * G + ITEMS * (g + 1))
                name = ("score", u, j)
                pe.wait_ge(*seg.empty(turn, name))
                bank = A[seg.bank(name)]
                parts = [(bank[:, 0:keys(u)], j, j, slice(0, keys(u)))] if j < 4 else \
                    [(bank[:, h * SC:(h + 2) * SC], h, slice(h, h + 2), slice(S, NK)) for h in (0, 2)]
                for out, h, heads, ks in parts:
                    if a0:
                        terms = [(qs[:, gp, q], 1), (qs[:, gp, q], 0)]
                    else:
                        pr = h // 2
                        terms = [(q_hl[:, gp, 0, pr, q], 1), (q_hl[:, gp, 1, pr, q], 0), (q_hl[:, gp, 0, pr, q], 0)]
                    for n, (lhs, hl) in enumerate(terms):
                        mm = pe.matmul(out, lhs, kpad[:, gp, hl, heads, ks], start=(n == 0),
                                       stop=(n == len(terms) - 1))
                mm.then_inc(a_full, 1)

            def transpose_head(b, ug, u, j):
                job = ug * T_UNIT + j
                by_dve, by_pool = min(j + 1, DVE_HEADS), min(j + 1, 4) - DVE_HEADS
                waits = [(normed, ug * DVE_HEADS + by_dve)] + \
                    ([(normed_pool, ug * len(POOL_HEADS) + by_pool)] if by_pool > 0 else []) + [(t_empty, job + 1)]
                if j < 4:
                    for sem, value in waits:
                        pe.wait_ge(sem, value)
                else:
                    wait_apart(pe, (ready, N_READY), *waits)
                bank = T[(u * T_UNIT + j) % 2]
                if j < 4:
                    for kt in range(keys(u) // P):
                        mm = pe.transpose(bank[:, kt, :], t_of(u, j, kt * P, (kt + 1) * P), sh.ident[:])
                else:
                    for h in range(4):
                        mm = pe.transpose(bank[0:SC, h, :], t_of(u, h, S, NK), sh.ident[:])
                mm.then_inc(t_full, 1)

            def times_values(ug, u, kt):
                g, qt = divmod(u, QT)
                q = slice(qt * P, (qt + 1) * P)
                last = kt == (4 if x1 else keys(u) // P - 1)
                for j in range(4):
                    pr, half = divmod(j, 2)
                    col = slice((2 * g + pr) * P + 64 * half, (2 * g + pr) * P + 64 * half + 64)
                    if a0:
                        hh, par = divmod(g, 2)
                        mm = pe.matmul(O[hh][32 * j:32 * j + 32, q], v_sb[:, kt, 8 * hh + 2 * j + par, :],
                                       p_tile(u, j, kt), start=(par == 0 and qt == 0 and kt == 0),
                                       stop=(par == 1 and last), skip_group_check=True)
                    elif kt < 4:
                        mm = pe.matmul(O[pr][64 * half:64 * half + 64, q], v_sb[:, kt, col],
                                       p_tile(u, j, kt), start=(kt == 0), stop=last, skip_group_check=True)
                    else:
                        mm = pe.matmul(O[pr][64 * half:64 * half + 64, q], v2[:, col],
                                       p_tile(u, j, 4)[0:SC], start=False, stop=True, skip_group_check=True)
                if last:
                    mm.then_inc(pv, 1)

            def run(seg, turn, b, work):
                {"v": values, "y": finish}.get(work[0], project)(seg, turn, b, work)

            def step(seg, turn, b, s, prev, own, nxt):
                found = tasks(s, prev, own, nxt)
                u_t, u_v = s - LAG_T, s - LAG_V
                do_t = s < U and (own if u_t >= 0 else prev)
                do_v = s < U and (own if u_v >= 0 else prev)
                for j in range(5):
                    if own and j < (5 if x1 else 4):
                        score_head(seg, turn, b, s, j)
                    if do_t and j < T_UNIT:
                        transpose_head(b, b * U + u_t, u_t % U, j)
                    if do_v and j == 0:
                        pe.wait_ge(t_empty, (b * U + u_v + 1) * T_UNIT + 2)
                        g, qt = divmod(u_v % U, QT)
                        if u_v >= 0 and qt == 0 and (not a0 or g == 0):
                            pe.wait_ge(*(seg.emptied(turn, ("v", 0, N_V - 1)) if a0 else (v_done, b * N_V + (g + 1) * N_V // G)))
                        if qt == 0 and not a0:
                            pe.wait_ge(o_empty, b * N_O + (2 * g + 2 - (N_O if u_v < 0 else 0)))
                        elif qt == 0 and g % 2 == 0:
                            pe.wait_ge(o_empty, b * N_O + (g // 2 + 1))
                    if do_v and (j < keys(u_v % U) // P or (x1 and j == 4)):
                        times_values(b * U + u_v, u_v % U, j)
                    for at, work in found:
                        if at == j:
                            run(seg, turn, b + (work in NEXT and s >= U - QT), work)

            def begin():
                for work in START:
                    run(start, 0, 0, work)

            def body(seg, turn, b, prev, own, nxt):
                for s in range(U if own else LN_STEP):
                    step(seg, turn, b, s, prev, own, nxt)

            batches(pe, begin, body)

        @block.scalar
        def _(act):
            act.sem_inc(t_empty, 2)
            act.sem_inc(o_empty, 2)
            act.wait_ge(ready, N_READY)

            def high_parts(seg, turn, b, g, i):
                gp = g % 2
                if a0:
                    name = ("item", g, i)
                    act.wait_ge(*seg.full(turn, name))
                    nc.scalar.activation((qs[:, gp, :], kh[:])[i], A[seg.bank(name)][:], ACT.Copy).then_inc(hi, 1)
                elif a1:
                    act.wait_ge(rot_sum, b * 4 * G + (4 * g + i + 1 + 2))
                    if i % 2 == 0:
                        nc.scalar.activation(q_hl[:, gp, 0, i // 2, :], rsum[:, i % 2, :], ACT.Copy).then_inc(hi, 1)
                    else:
                        for half in range(2):
                            r = slice(64 * half, 64 * half + 64)
                            nc.scalar.activation(kpad[r, gp, 0, 2 * (i // 2) + half, :], rsum[r, i % 2, :],
                                                 ACT.Copy).then_inc(hi, 1)
                else:
                    name = ("item", g, i)
                    bank = A[seg.bank(name)]
                    act.wait_ge(*seg.full(turn, name))
                    if i < 2:
                        nc.scalar.activation(q_hl[:, gp, 0, i, :], bank[:], ACT.Copy).then_inc(hi, 1)
                    elif i < 4:
                        for half in range(2):
                            r = slice(64 * half, 64 * half + 64)
                            nc.scalar.activation(kpad[r, gp, 0, 2 * (i - 2) + half, 0:S], bank[r, :],
                                                 ACT.Copy).then_inc(hi, 1)
                    else:
                        for pr in range(2):
                            for half in range(2):
                                r = slice(64 * half, 64 * half + 64)
                                nc.scalar.activation(kpad[r, gp, 0, 2 * pr + half, S:NK],
                                                     bank[r, pr * SC:(pr + 1) * SC], ACT.Copy).then_inc(hi, 1)

            def project(seg, turn, b, work):
                if work[0] == "xT":
                    for dt in range(DT):
                        name = ("xT", dt)
                        act.wait_ge(*seg.full(turn, name))
                        nc.scalar.activation(xT[:, dt, :], A[seg.bank(name)][:], ACT.Copy).then_inc(xt_done, 1)
                elif work[0] == "lat":
                    act.wait_ge(*seg.full(turn, "lat"))
                    nc.scalar.activation(lat[:], A[seg.bank("lat")][0:64 if a0 else P, :], ACT.Copy).then_inc(a_act, 1)
                elif work[0] == "v" and not a0:
                    _, g, i = work
                    act.wait_ge(*seg.full(turn, work))
                    bank, col = A[seg.bank(work)], slice(g * V_CUT, (g + 1) * V_CUT)
                    to, of = (v2[:, col], bank[0:SC, 0:V_CUT]) if x1 and i == 2 else \
                        (v_sb[:, 2 * i:2 * i + 2, col], bank[:].rearrange("p (k n) -> p k n", k=2))
                    nc.scalar.activation(to, of, ACT.Copy).then_inc(v_done, 1)
                elif work[0] == "item":
                    high_parts(seg, turn, b, work[1], work[2])

            def step(seg, turn, b, s, prev, own, nxt):
                found = tasks(s, prev, own, nxt)
                u_e, u_t, u_v = s - LAG_E, s - LAG_T, s - LAG_V
                do_e = s < U and (own if u_e >= 0 else prev)
                do_t = s < U and (own if u_t >= 0 else prev)
                do_v = s < U and (own if u_v >= 0 else prev)
                if do_t:
                    act.wait_ge(pv, b * U + (u_t + 1))
                for j in range(5):
                    if do_t and j < T_UNIT:
                        u = u_t % U
                        act.wait_ge(t_full, (b * U + u_t) * T_UNIT + (j + 1 + T_CREDIT))
                        bank = T[(u * T_UNIT + j) % 2]
                        kts = keys(u) // P
                        to, of = (p_tile(u, j, 0, kts), bank[:, 0:kts, :] if kts > 1 else bank[:, 0, :]) if j < 4 else \
                            (p_T[0:SC, (u % 2) * tiles[0] + 4:(u % 2) * tiles[0] + tiles[0]:5, :], bank[0:SC, :, :])
                        nc.scalar.activation(to, of, ACT.Copy).then_inc(t_empty, 1)
                    if do_e and j == 0:
                        act.wait_ge(negated, b * U + (u_e + 1))
                    if do_e and j < 4:
                        slot, n = u_e % 4, (NK if x1 else keys(u_e % U))
                        nc.scalar.activation(t_of(u_e % U, j, 0, n), t_of(u_e % U, j, 0, n), ACT.Exp,
                                             bias=neg[:, slot, j:j + 1], scale=SCALE,
                                             accum_out=total[:, slot, j:j + 1]).then_inc(exped, 1)
                    for at, work in found:
                        if at == j and not (a1 and work[0] == "item"):
                            project(seg, turn, b + (work in NEXT and s >= U - QT), work)
                if do_v:
                    g, qt = divmod(u_v % U, QT)
                    if qt == QT - 1 and (not a0 or g % 2 == 1):
                        act.wait_ge(pv, b * U + (u_v + 1 + 2))
                        for o in ([g // 2] if a0 else [0, 1]):
                            nc.scalar.activation(oT[:, o if a0 else 2 * g + o, :], O[o][:],
                                                 ACT.Copy).then_inc(o_empty, 1)
                for _, work in found:
                    if a1 and work[0] == "item":
                        project(seg, turn, b + (work in NEXT and s >= U - QT), work)

            def begin():
                for work in START:
                    project(start, 0, 0, work)

            def body(seg, turn, b, prev, own, nxt):
                for s in range(U if own else LN_STEP):
                    step(seg, turn, b, s, prev, own, nxt)

            batches(act, begin, body)

        @block.gpsimd
        def _(pool):
            def low_keys(b, g):
                pool.wait_ge(kl_done, b * G + (g + 1))
                for j in range(4):
                    nc.gpsimd.tensor_tensor(kpad[:, g % 2, 1, j, :], kl[:],
                                            hmask[:, j:j + 1].to_broadcast([P, S]), ALU.mult).then_inc(low, 1)

            def step(b, s, prev, own, nxt):
                u_n = s - LAG_N
                if s < U and (own if u_n >= 0 else prev):
                    pool.wait_ge(inverted, b * U + (u_n + 1))
                    for j in POOL_HEADS:
                        nc.gpsimd.tensor_tensor(t_of(u_n % U, j, 0, NK), t_of(u_n % U, j, 0, NK),
                                                inv[:, u_n % 4, j:j + 1].to_broadcast([P, NK]),
                                                ALU.mult).then_inc(normed_pool, 1)
                for _, work in tasks(s, prev, own, nxt):
                    if a0 and work[0] == "item" and work[2] == 1:
                        low_keys(b + (s >= U - QT), work[1])

            def begin():
                if a0:
                    pool.sem_inc(low, 4)
                pool.wait_ge(ready, N_READY)
                if a0:
                    low_keys(0, 0)

            def body(seg, turn, b, prev, own, nxt):
                for s in range(U if own else LN_STEP):
                    step(b, s, prev, own, nxt)

            if not a1:
                batches(pool, begin, body)
            if a1:
                pool.sem_inc(rot_sum, 2)
                pool.sem_inc(low, LOW_GROUP)
                pool.wait_ge(ready, N_READY)
                with pool.Fori(0, B) as b:
                    for g in range(G):
                        for i in range(4):
                            gp = g % 2
                            pool.wait_ge(rot_done, b * 4 * G + (4 * g + i + 1))
                            nc.gpsimd.tensor_tensor(rsum[:, i % 2, :], rsum[:, i % 2, :], rsin[:],
                                                    ALU.add).then_inc(rot_sum, 1)
                            pool.wait_ge(hi, b * HI_GROUP * G + (HI_GROUP * g + HI_ITEM[i]))
                            if i % 2 == 0:
                                nc.gpsimd.tensor_tensor(q_hl[:, gp, 1, i // 2, :], rsum[:, i % 2, :],
                                                        q_hl[:, gp, 0, i // 2, :], ALU.subtract).then_inc(low, 1)
                            else:
                                for half in range(2):
                                    r = slice(64 * half, 64 * half + 64)
                                    h = 2 * (i // 2) + half
                                    nc.gpsimd.tensor_tensor(kpad[r, gp, 1, h, :], rsum[r, i % 2, :],
                                                            kpad[r, gp, 0, h, :], ALU.subtract).then_inc(low, 1)
                                    pool.wait_ge(low, b * LOW_GROUP * G + (LOW_GROUP * (g + 1) + LOW_ITEM[i] - 1 + half))

        @block.vector
        def _(dve):
            if a0:
                dve.wait_ge(weights, 16 * len(loads))
                nc.vector.tensor_tensor(wkT[:], wkT[:], wvT[:], ALU.add).then_inc(ready, 1)
                nc.vector.memset(v_sb[:], 0.0).then_inc(ready, 1)
                dve.wait_ge(folded, 1)
                nc.vector.tensor_copy(wkd[:], A[0][:, 0:DT * 64].rearrange("p (t n) -> p t n", t=DT)).then_inc(ready, 1)
                dve.wait_ge(ready, 3)
            else:
                nc.vector.memset(kpad[:].bitcast(F32), 0.0).then_inc(ready, 1)
                if x1:
                    nc.vector.memset(ones[:], 1.0).then_inc(ready, 1)
                    nc.vector.memset(table[:], 0.0).then_inc(ready, 1)
                dve.wait_ge(ready, N_READY)
                dve.wait_ge(weights, 16 * len(loads))
            dve.sem_inc(a_dve, A_BANKS)

            def low_parts(seg, turn, b, g, i):
                gp = g % 2
                if a0:
                    name = ("item", g, i)
                    bank = A[seg.bank(name)]
                    dve.wait_ge(*seg.full(turn, name))
                    dve.wait_ge(hi, b * HI_GROUP * G + (HI_GROUP * g + HI_ITEM[i]))
                    if i == 0:
                        nc.vector.tensor_tensor(qs[64:128, gp, :], bank[64:128, :], qs[64:128, gp, :],
                                                ALU.subtract).then_inc(a_dve, 1)
                    else:
                        dve.wait_ge(low, b * 4 * G + 4 * (g + 1))
                        nc.vector.tensor_tensor(kl[:], bank[:], kh[:], ALU.subtract).then_inc(kl_done, 1)
                        for j in range(4):
                            nc.vector.tensor_scalar(kpad[:, gp, 0, j, :], kh[:], hmask[:, j:j + 1], None,
                                                    ALU.mult).then_inc(kp, 1)
                elif a1:
                    dve.wait_ge(low, b * LOW_GROUP * G + (LOW_GROUP * g + (LOW_ITEM[i + 2] if i < 2 else LOW_GROUP + LOW_ITEM[i - 2])))
                    for sw in range(2):
                        name = ("item", g, i, sw)
                        if sw:
                            dve.wait_ge(rot_sum, b * 4 * G + (4 * g + i + 2))
                        dve.wait_ge(*seg.full(turn, name))
                        nc.vector.tensor_tensor((rsum[:, i % 2, :], rsin[:])[sw], A[seg.bank(name)][:], (cos, sin)[sw][:],
                                                ALU.mult).then_inc((a_dve, rot_done)[sw], 1)
                else:
                    name = ("item", g, i)
                    bank = A[seg.bank(name)]
                    dve.wait_ge(*seg.full(turn, name))
                    dve.wait_ge(hi, b * HI_GROUP * G + (HI_GROUP * g + HI_ITEM[i]))
                    if i < 2:
                        ins = nc.vector.tensor_tensor(q_hl[:, gp, 1, i, :], bank[:], q_hl[:, gp, 0, i, :], ALU.subtract)
                    elif i < 4:
                        for half in range(2):
                            r = slice(64 * half, 64 * half + 64)
                            h = 2 * (i - 2) + half
                            ins = nc.vector.tensor_tensor(kpad[r, gp, 1, h, 0:S], bank[r, :], kpad[r, gp, 0, h, 0:S],
                                                          ALU.subtract)
                    else:
                        for pr in range(2):
                            for half in range(2):
                                r = slice(64 * half, 64 * half + 64)
                                h = 2 * pr + half
                                ins = nc.vector.tensor_tensor(kpad[r, gp, 1, h, S:NK], bank[r, pr * SC:(pr + 1) * SC],
                                                              kpad[r, gp, 0, h, S:NK], ALU.subtract)
                    ins.then_inc(q_low, 1)

            def run(seg, turn, b, work):
                if work[0] == "item":
                    low_parts(seg, turn, b, work[1], work[2])
                elif work[0] == "y":
                    dve.wait_ge(*seg.full(turn, work))
                    row = sh.x_all[:, b * QT - QT + work[1], :]
                    nc.vector.tensor_tensor(row, A[seg.bank(work)][:, 0:D], row, ALU.add).then_inc(a_dve, 1)
                elif work[0] == "v" and a0:
                    i = work[2]
                    dve.wait_ge(*seg.full(turn, work))
                    bank = A[seg.bank(work)][:].rearrange("p (k h r c) -> p k h r c", k=2, r=2, c=16)
                    for par in range(2):
                        ins = nc.vector.tensor_copy(v_sb[:, 2 * i:2 * i + 2, par:16:2, 16 * par:16 * par + 16],
                                                    bank[:, :, :, par, :])
                    ins.then_inc(a_dve, 1)

            def step(seg, turn, b, s, prev, own, nxt):
                found = tasks(s, prev, own, nxt)
                u_n = s - LAG_N
                do_n = s < U and (own if u_n >= 0 else prev)
                if own:
                    dve.wait_ge(t_full, (b * U + s + 1) * T_UNIT)
                slot, qt, n = s % 4, s % QT, keys(s)
                at = S - P - qt * P if (a0 or a1) else 0
                for j in range(5):
                    if own and j < 4:
                        name = ("score", s, j)
                        wait_apart(dve, (ready, N_READY), seg.full(turn, name))
                        nc.vector.tensor_tensor_reduce(
                            t_of(s, j, 0, n), A[seg.bank(name)][:, 0:n], table[:, at:at + n], 1.0, LOWEST,
                            ALU.mult if a0 else ALU.add, ALU.max,
                            (mx1 if x1 else mx)[:, slot, j:j + 1]).then_inc(a_dve, 1)
                    if own and x1 and j == 4:
                        name = ("score", s, 4)
                        wait_apart(dve, (ready, N_READY), seg.full(turn, name), seg.emptied(turn, ("score", s, 3)))
                        for i in range(4):
                            ins = nc.vector.tensor_tensor_reduce(
                                t_of(s, i, S, NK), A[seg.bank(name)][:, i * SC:(i + 1) * SC],
                                table[:, 0:SC], 1.0, mx1[:, slot, i:i + 1], ALU.add, ALU.max, mx[:, slot, i:i + 1])
                        ins.then_inc(a_dve, 1)
                    if own and j == 4:
                        dve.wait_ge(*seg.emptied(turn, ("score", s, 4 if x1 else 3)))
                        nc.vector.tensor_scalar(neg[:, slot, :], mx[:, slot, :], -SCALE, None,
                                                ALU.mult).then_inc(negated, 1)
                    if do_n and j == 0:
                        dve.wait_ge(exped, (b * U + u_n + 1) * 4)
                        nc.vector.reciprocal(inv[:, u_n % 4, :], total[:, u_n % 4, :]).then_inc(inverted, 1)
                        dve.wait_ge(inverted, b * U + (u_n + 1))
                    if do_n and j < DVE_HEADS:
                        m = NK if x1 else keys(u_n % U)
                        nc.vector.tensor_scalar(t_of(u_n % U, j, 0, m), t_of(u_n % U, j, 0, m),
                                                inv[:, u_n % 4, j:j + 1], None, ALU.mult).then_inc(normed, 1)
                    if own and prev and LN_STEP <= s <= LN_STEP + 1:
                        advance(norm[0], 2)
                    for head, work in found:
                        if head == j:
                            run(seg, turn, b + (work in NEXT and s >= U - QT), work)
                if s == LN_STEP - 1 and prev:
                    wait_apart(dve, (ready, N_READY), seg.emptied(turn, ("y", QT - 1)))
                    steps = Chain(dve, chain, (b - 1) * LN_LINKS, (ready, N_READY))
                    norm[:] = [layer_norm_rows(nc.vector, steps, lambda qt: sh.x_all[:, b * QT - QT + qt, :], stats,
                                               mv, scratch)]
                    advance(norm[0], 1 if own else None)
                if s == LN_STEP + 1 and prev:
                    advance(norm[0])

            norm = []

            def begin():
                for work in START:
                    if work[0] == "item":
                        low_parts(start, 0, 0, work[1], work[2])

            def body(seg, turn, b, prev, own, nxt):
                for s in range(U if own else LN_STEP):
                    step(seg, turn, b, s, prev, own, nxt)

            batches(dve, begin, body)


def cross_attention_heads(nc, sh, w):
    H, HD = 16, 16
    HH = H // DT
    PR = H // 2
    VC = HD + 1
    LAG_T, LAG_V, LN_STEP = 2, 3, 2
    OPS = 2 * DT
    T_DONE = (4, 6, 10, 12)

    with ExitStack() as ctx:
        env = Env(nc, ctx, "x0")
        sb, sem = env.sb, env.sem
        xin = sb("xin", [P, QT, D])
        x_hl = sb("xhl", [P, 2, DT, S], F32R)
        ctxT = sb("ctxT", [P, DT, B, SC])
        ctx_hl = sb("ctxhl", [P, 2, DT, B * SC], F32R)
        keys = sb("keys", [P, 2, DT, B, HH, SC], F32R)
        v_nat = sb("vnat", [P, B, D])
        v_all = sb("v", [P, B, PR * 2 * VC])
        hmask = sb("hmask", [P, HH])
        mask = sb("mask", [P, B * QT, SC], I32)
        bias = sb("bias", [P, B * QT, SC])
        t_buf = sb("t", [P, QT, H, SC])
        p_T = sb("pT", [P, 2, PR, P])
        mx = sb("mx", [P, QT, H])
        inv = sb("inv", [P, 2, H])
        res = sb("res", [P, 2, D])
        stats = sb("stats", [P, QT, 6])
        mv = sb("mv", [P, QT, 2])
        scratch = sb("scratch", [P, 3, QT])
        SB = [env.ps(f"S{i}", [P, HH, SC]) for i in range(2 * DT)]
        T = [env.ps(f"T{i}", [P, 4, P]) for i in range(2)]
        O = [env.ps(f"O{i}", [P, H * VC]) for i in range(2)]

        loaded = sem("loaded")
        xin_in = sem("xin_in")
        ready = sem("ready")
        ctx_hi = sem("ctx_hi")
        keyed = sem("keyed")
        t_full = sem("t_full")
        t_act = sem("t_act")
        x_low = sem("x_low")
        x_hi = sem("x_hi")
        s_full = sem("s_full")
        s_read = sem("s_read")
        maxed = sem("maxed")
        shifted = sem("shifted")
        exped = sem("exped")
        pv = sem("pv")
        inverted = sem("inverted")
        scaled = sem("scaled")
        added = sem("added")
        chain = sem("chain")
        sems = {"full": t_full, "act": t_act, "dve": x_low}

        def xt_jobs():
            return [(("xT", dt), "dve") for dt in range(DT)]

        def seg_jobs(prev, own, nxt):
            jobs = []
            for s in range(QT if own else LAG_V):
                if s >= LAG_T if own and not prev else (s < LAG_T if not own else True):
                    jobs += [(("T", s, j), "act") for j in range(2)]
                if own and nxt and s == QT - 1:
                    jobs += xt_jobs()
            return jobs

        start = Segment(xt_jobs(), sems, {"full": 0, "act": 0, "dve": 2}, [("dve", 0)] * 2, n=2)
        first = Segment(seg_jobs(False, True, True), sems, start.end, start.last, n=2)
        steady = Segment(seg_jobs(True, True, True), sems, first.end, first.last, n=2)
        assert steady.last == first.last
        looped = {r: steady.base[r] + (B - 2) * steady.per[r] for r in steady.base}
        final = Segment(seg_jobs(True, True, False), sems, looped, steady.last, n=2)
        tail = Segment(seg_jobs(True, False, False), sems, final.end, final.last, n=2)

        def batches(eng, body):
            body(first, 0, 0, prev=False, own=True, nxt=True)
            with eng.Fori(1, B - 1) as b:
                body(steady, b - 1, b, prev=True, own=True, nxt=True)
            body(final, 0, B - 1, prev=True, own=True, nxt=False)
            body(tail, 0, B, prev=True, own=False, nxt=False)

        def lagged(s, lag, prev, own):
            return own if s >= lag else prev

        block = ctx.enter_context(nc.Block())
        LOADS = DT + 2 + 2

        @block.sync
        def _(sp):
            sp.dma_start(xin[:], sh.x_all[:, 0:QT, :]).then_inc(xin_in, 16)
            for t in range(DT):
                sp.dma_start(ctxT[:, t], w["ctxT"][:, t * P:(t + 1) * P, :].rearrange("b p n -> p b n"))\
                  .then_inc(loaded, 16)
            for half in range(2):
                sp.dma_start(v_nat[half * SC:(half + 1) * SC], w["ctx"].rearrange("b n d -> n b d")).then_inc(loaded, 16)
            sp.dma_start(hmask[:], w["head_mask8"]).then_inc(loaded, 16)
            sp.dma_start(mask[:], w["mask"].rearrange("b (q p) n -> p (b q) n", p=P)).then_inc(loaded, 16)
            with sp.Fori(1, B) as b:
                sp.wait_ge(x_low, b * DT + 2)
                sp.dma_start(xin[:], sh.x_all[:, bass.ds(b * QT, QT), :]).then_inc(xin_in, 16)

        @block.tensor
        def _(pe):
            def transpose_x(seg, turn, b):
                pe.wait_ge(xin_in, b * 16 + 16)
                for dt in range(DT):
                    name = ("xT", dt)
                    pe.wait_ge(*seg.empty(turn, name))
                    for qt in range(QT):
                        mm = pe.transpose(T[seg.bank(name)][:, qt, :], xin[:, qt, dt * P:(dt + 1) * P], sh.ident[:])
                    mm.then_inc(t_full, 1)

            def body(seg, turn, b, prev, own, nxt):
                for s in range(QT if own else LAG_V):
                    if lagged(s, LAG_T, prev, own):
                        u = (s - LAG_T) % QT
                        pe.wait_ge(exped, b * QT + (s - LAG_T + 1))
                        for j in range(2):
                            name = ("T", s, j)
                            pe.wait_ge(*seg.empty(turn, name))
                            for i in range(4):
                                pr = 4 * j + i
                                mm = pe.transpose(T[seg.bank(name)][:, i, :],
                                                  t_buf[:, u, 2 * pr:2 * pr + 2, :].rearrange("p h k -> p (h k)"),
                                                  sh.ident[:])
                            mm.then_inc(t_full, 1)
                    if own:
                        if s == 0:
                            pe.wait_ge(x_low, b * DT + (DT + 2))
                            pe.wait_ge(keyed, b * OPS + OPS)
                        pe.wait_ge(s_read, b * QT * DT + DT * (s + 1))
                        q = slice(s * P, (s + 1) * P)
                        for dt in range(DT):
                            for n, (a, k) in enumerate(((0, 1), (1, 0), (0, 0))):
                                mm = pe.matmul(SB[DT * (s % 2) + dt][:], x_hl[:, a, dt, q], keys[:, k, dt, b],
                                               start=(n == 0), stop=(n == 2))
                            mm.then_inc(s_full, 1)
                    if lagged(s, LAG_V, prev, own):
                        u, back = (s - LAG_V) % QT, s - LAG_V
                        pe.wait_ge(t_act, (b * QT + back + 1) * 2)
                        pe.wait_ge(scaled, b * QT + (back + 1))
                        vb = b if back >= 0 else b - 1
                        for pr in range(PR):
                            mm = pe.matmul(O[u % 2][:, pr * 2 * VC:(pr + 1) * 2 * VC], p_T[:, u % 2, pr, :],
                                           v_all[:, vb, pr * 2 * VC:(pr + 1) * 2 * VC],
                                           start=True, stop=True)
                        mm.then_inc(pv, 1)
                    if nxt and s == QT - 1:
                        transpose_x(seg, turn, b + 1)

            pe.wait_ge(ready, 4)
            transpose_x(start, 0, 0)
            batches(pe, body)

        @block.scalar
        def _(act):
            act.wait_ge(loaded, 16 * LOADS)
            nc.scalar.activation(ctx_hl[:, 0], ctxT[:].rearrange("p t b n -> p t (b n)"), ACT.Copy).then_inc(ctx_hi, 1)
            act.sem_inc(pv, 2)

            def split_x(seg, turn, b):
                if not (isinstance(b, int) and b == 0):
                    act.wait_ge(s_full, b * QT * DT)
                for dt in range(DT):
                    name = ("xT", dt)
                    act.wait_ge(*seg.full(turn, name))
                    nc.scalar.activation(x_hl[:, 0, dt, :], T[seg.bank(name)][:].rearrange("p a b -> p (a b)"),
                                         ACT.Copy).then_inc(x_hi, 1)

            def body(seg, turn, b, prev, own, nxt):
                for s in range(QT if own else LAG_V):
                    if lagged(s, LAG_T, prev, own):
                        u, back = (s - LAG_T) % QT, s - LAG_T
                        act.wait_ge(pv, b * QT + (back + 1))
                        for j in range(2):
                            name = ("T", s, j)
                            act.wait_ge(*seg.full(turn, name))
                            nc.scalar.activation(p_T[:, u % 2, 4 * j:4 * j + 4, :], T[seg.bank(name)][:],
                                                 ACT.Copy).then_inc(t_act, 1)
                    if lagged(s, 1, prev, own):
                        u = (s - 1) % QT
                        act.wait_ge(shifted, b * QT + s)
                        nc.scalar.activation(t_buf[:, u], t_buf[:, u], ACT.Exp).then_inc(exped, 1)
                    if nxt and s == QT - 1:
                        split_x(seg, turn, b + 1)

            split_x(start, 0, 0)
            batches(act, body)

        @block.gpsimd
        def _(pool):
            def make_keys(b):
                for hl in range(2):
                    for dt in range(DT):
                        k = ctx_hl[:, hl, dt, bass.ds(b * SC, SC)].unsqueeze(1).to_broadcast([P, HH, SC])
                        nc.gpsimd.tensor_tensor(keys[:, hl, dt, b], k,
                                                hmask[:].unsqueeze(2).to_broadcast([P, HH, SC]),
                                                ALU.mult).then_inc(keyed, 1)

            def body(seg, turn, b, prev, own, nxt):
                for s in range(QT if own else 0):
                    pool.wait_ge(maxed, b * QT + (s + 1))
                    nc.gpsimd.tensor_tensor(t_buf[:, s], t_buf[:, s],
                                            mx[:, s, :].unsqueeze(2).to_broadcast([P, H, SC]),
                                            ALU.subtract).then_inc(shifted, 1)
                    if nxt and s == 1:
                        make_keys(b + 1)

            pool.wait_ge(ready, 4)
            make_keys(0)
            batches(pool, body)

        @block.vector
        def _(dve):
            nc.vector.memset(v_all[:], 0.0).then_inc(ready, 1)
            dve.sem_inc(s_read, 2 * DT)
            dve.sem_inc(scaled, 2)
            dve.sem_inc(x_low, 2)
            dve.wait_ge(loaded, 16 * LOADS)
            dve.wait_ge(ready, 1)
            for half in range(2):
                r = slice(half * SC, (half + 1) * SC)
                of = v_nat[r].rearrange("p b (r h c) -> p b r h c", h=2, c=HD)[:, :, :, half, :]
                to = v_all[r].rearrange("p b (r h c) -> p (b r) h c", h=2, c=VC)[:, :, half, :]
                nc.vector.tensor_copy(to[:, :, 0:HD], of.rearrange("p b r c -> p (b r) c"))
                nc.vector.memset(to[:, :, HD:VC], 1.0)
            nc.vector.tensor_scalar(bias[:], mask[:], 1.0e9, -1.0e9, ALU.mult, ALU.add).then_inc(ready, 1)
            dve.wait_ge(ctx_hi, 1)
            for dt in range(DT):
                nc.vector.tensor_tensor(ctx_hl[:, 1, dt], ctxT[:, dt].rearrange("p b n -> p (b n)"), ctx_hl[:, 0, dt],
                                        ALU.subtract).then_inc(ready, 1)
            dve.wait_ge(ready, 4)

            def split_x(seg, turn, b):
                for dt in range(DT):
                    dve.wait_ge(x_hi, b * DT + (dt + 1))
                    nc.vector.tensor_tensor(x_hl[:, 1, dt, :],
                                            T[seg.bank(("xT", dt))][:].rearrange("p a b -> p (a b)"),
                                            x_hl[:, 0, dt, :], ALU.subtract).then_inc(x_low, 1)

            def body(seg, turn, b, prev, own, nxt):
                for s in range(QT if own else LAG_V):
                    if own:
                        if prev:
                            dve.wait_ge(t_full, b * 10 + (T_DONE[s] - 10))
                        for dt in range(DT):
                            dve.wait_ge(s_full, b * QT * DT + (DT * s + dt + 1))
                            nc.vector.scalar_tensor_tensor(
                                out=t_buf[:, s, HH * dt:HH * (dt + 1), :], in0=SB[DT * (s % 2) + dt][:], scalar=0.25,
                                in1=bias[:, bass.ds(b * QT + s, 1), :].to_broadcast([P, HH, SC]),
                                op0=ALU.mult, op1=ALU.add).then_inc(s_read, 1)
                        dve.wait_ge(s_read, b * QT * DT + (DT * (s + 1) + 2 * DT))
                        nc.vector.tensor_reduce(mx[:, s, :], t_buf[:, s], AX_X, ALU.max).then_inc(maxed, 1)
                        if prev and s == LN_STEP + 1:
                            advance(norm[0], 3)
                    if nxt and s == QT - 1:
                        split_x(seg, turn, b + 1)
                    if lagged(s, LAG_V, prev, own):
                        u, back = (s - LAG_V) % QT, s - LAG_V
                        rb = b if back >= 0 else b - 1
                        heads = O[u % 2][:].rearrange("p (h c) -> p h c", c=VC)
                        dve.wait_ge(pv, b * QT + (back + 1 + 2))
                        nc.vector.reciprocal(inv[:, u % 2, :], heads[:, :, HD:VC].rearrange("p h c -> p (h c)"))\
                          .then_inc(inverted, 1)
                        if own and prev and s == LN_STEP + 1:
                            advance(norm[0], 4)
                        dve.wait_ge(inverted, b * QT + (back + 1))
                        nc.vector.tensor_tensor(res[:, u % 2].rearrange("p (h c) -> p h c", c=HD), heads[:, :, 0:HD],
                                                inv[:, u % 2, :].unsqueeze(2).to_broadcast([P, H, HD]),
                                                ALU.mult).then_inc(scaled, 1)
                        dve.wait_ge(scaled, b * QT + (back + 1 + 2))
                        row = sh.x_all[:, rb * QT + u, :]
                        nc.vector.tensor_tensor(row, res[:, u % 2], row, ALU.add).then_inc(added, 1)
                    if s == LN_STEP and prev:
                        wait_apart(dve, (ready, 4), (added, b * QT))
                        steps = Chain(dve, chain, (b - 1) * LN_LINKS, (ready, 4))
                        norm[:] = [layer_norm_rows(nc.vector, steps, lambda qt: sh.x_all[:, b * QT - QT + qt, :],
                                                   stats, mv, scratch)]
                        advance(norm[0], 1 if own else None)

                    if own and prev and s == LN_STEP + 1:
                        advance(norm[0])

            norm = []
            split_x(start, 0, 0)
            batches(dve, body)


def butterfly_stage(engine, dst, tmp, src, weights, stage, transposed):
    s = 2 ** stage
    w = weights.rearrange("p (n s o i) -> p n o i s", n=FH // (2 * s), s=s, o=2, i=2)
    if transposed:
        w = w.rearrange("p n o i s -> p n i o s")
    x = src.rearrange("p (n k s) -> p n k s", k=2, s=s)
    full = [src.shape[0], FH // (2 * s), 2, s]
    view = [a.rearrange("p (n k s) -> p n k s", k=2, s=s) for a in (tmp, dst)]
    for k in range(2):
        yield engine.tensor_tensor(view[k], w[:, :, :, k, :], x[:, :, k:k + 1, :].to_broadcast(full), ALU.mult)
    yield engine.tensor_tensor(dst, dst, tmp, ALU.add)


def fold_butterflies(nc, w, w_up, w_down, bias_h, bias_y, sh):
    with ExitStack() as ctx:
        env = Env(nc, ctx, "fold")
        sb, sem = env.sb, env.sem
        up = sb("up", [P, 2, DT + 1, FH])
        down = sb("down", [P, 2, DT, FH])
        tmp_up = sb("tmpup", [P, DT + 1, FH])
        tmp_down = sb("tmpdown", [P, DT, FH])
        w_stage = sb("wstage", [P, 2, 2, 2 * FH])
        rows = sb("rows", [1, FH])
        b2 = sb("b2", [1, D])
        one = sb("one", [1, 1])
        BH = env.ps("BH", [P, FT])
        TB = [env.ps(f"T{i}", [P, 2, D]) for i in range(4)]
        loaded = sem("loaded")
        staged = [[sem(f"staged_{side}{parity}") for parity in range(2)] for side in ("up", "down")]
        v_step = sem("v_step")
        p_step = sem("p_step")
        biased = sem("biased")
        turned = sem("turned")
        done = sem("done")
        block = ctx.enter_context(nc.Block())
        order = [list(range(STAGES)), list(range(STAGES - 1, -1, -1))]
        source = [w["up_weights"], w["down_weights"]]
        SHARED = 4
        full = slice(0, P)
        dve_tiles = [[(1, DT - 1, full)] * (k < SHARED) + [(0, t, full) for t in range(DT)] + [(0, DT, slice(0, 1))]
                     for k in range(STAGES)]
        pool_tiles = [[(1, t, full) for t in range(DT - 1 if k < SHARED else DT)] for k in range(STAGES)]

        def after(tiles, k):
            return 3 * sum(len(t) for t in tiles[:k + 1])


        @block.sync
        def _(sp):
            sp.dma_start(up[:, 0, 0:DT, :], w["w_exp"].rearrange("(t p) n -> p t n", p=P)).then_inc(loaded, 16)
            sp.dma_start(up[0:1, 0, DT, :], w["b_exp"]).then_inc(loaded, 16)
            sp.dma_start(down[:, 0], w["w_conT"].rearrange("(t p) n -> p t n", p=P)).then_inc(loaded, 16)
            sp.dma_start(rows[:], w["up_bias"]).then_inc(loaded, 16)
            sp.dma_start(bias_y, w["b_con"]).then_inc(loaded, 16)
            sp.dma_start(b2[:], w["down_bias"]).then_inc(loaded, 16)
            for k in range(STAGES):
                for side in range(2):
                    if k >= 2:
                        if side == 0 or k - 2 < SHARED:
                            sp.wait_ge(v_step, 1 + after(dve_tiles, k - 2))
                        if side == 1:
                            sp.wait_ge(p_step, after(pool_tiles, k - 2))
                    sp.dma_start(w_stage[:, side, k % 2], source[side][order[side][k]].to_broadcast([P, 2 * FH]))\
                      .then_inc(staged[side][k % 2], 16)

        def fold(engine, eng, step, base, tiles):
            n = base
            for k in range(STAGES):
                if engine is nc.gpsimd and k == SHARED:
                    eng.wait_ge(v_step, 1 + after(dve_tiles, k - 1))
                runs = []
                for side in sorted({t[0] for t in tiles[k]}):
                    eng.wait_ge(staged[side][k % 2], 16 * (k // 2 + 1))
                for side, t, p in tiles[k]:
                    buf, tmp = (up, tmp_up) if side == 0 else (down, tmp_down)
                    runs.append(butterfly_stage(engine, buf[p, (k + 1) % 2, t, :], tmp[p, t, :], buf[p, k % 2, t, :],
                                                w_stage[p, side, k % 2], order[side][k], side == 1))
                for _ in range(2):
                    for run in runs:
                        next(run).then_inc(step, 1)
                        n += 1
                eng.wait_ge(step, n)
                for run in runs:
                    next(run).then_inc(step, 1)
                    n += 1
                eng.wait_ge(step, n)
            assert n == base + after(tiles, STAGES - 1)

        @block.vector
        def _(dve):
            nc.vector.memset(one[:], 1.0).then_inc(v_step, 1)
            dve.wait_ge(loaded, 16 * 6)
            fold(nc.vector, dve, v_step, 1, dve_tiles)
            nc.vector.tensor_tensor(rows[:], rows[:], up[0:1, 0, DT, :], ALU.add).then_inc(biased, 1)
            nc.vector.tensor_tensor(bias_y, bias_y, b2[:], ALU.add).then_inc(biased, 1)
            nc.vector.tensor_copy(w_up, up[:, 0, 0:DT, :]).then_inc(biased, 1)
            assert STAGES % 2 == 0
            dve.wait_ge(biased, 3)

        @block.gpsimd
        def _(pool):
            pool.wait_ge(loaded, 16 * 6)
            fold(nc.gpsimd, pool, p_step, 0, pool_tiles)

        @block.tensor
        def _(pe):
            pe.wait_ge(biased, 2)
            for f in range(FT):
                mm = pe.matmul(BH[:, f:f + 1], rows[0:1, f * P:(f + 1) * P], one[:], start=True, stop=True)
            mm.then_inc(turned, 1)
            pe.wait_ge(p_step, after(pool_tiles, STAGES - 1))
            for i in range(4):
                for j in range(2):
                    f = 2 * i + j
                    for t in range(DT):
                        mm = pe.transpose(TB[i][:, j, t * P:(t + 1) * P], down[:, 0, t, f * P:(f + 1) * P],
                                          sh.ident[:])
                mm.then_inc(turned, 1)

        @block.scalar
        def _(act):
            act.wait_ge(turned, 1)
            nc.scalar.activation(bias_h, BH[:], ACT.Copy).then_inc(done, 1)
            for i in range(4):
                act.wait_ge(turned, i + 2)
                nc.scalar.activation(w_down[:, 2 * i:2 * i + 2, :], TB[i][:], ACT.Copy).then_inc(done, 1)
            act.wait_ge(done, 5)


def butterfly_ffn(nc, sh, w):
    with ExitStack() as ctx:
        env = Env(nc, ctx, "ffn")
        sb, sem = env.sb, env.sem
        w_up = sb("wup", [P, DT, FH])
        w_down = sb("wdown", [P, FT, D])
        bias_h = sb("biash", [P, FT])
        bias_y = sb("biasy", [1, D])
        fold_butterflies(nc, w, w_up[:], w_down[:], bias_h[:], bias_y[:], sh)
        ones = sb("ones", [1, P])
        xin = sb("xin", [P, QT, D])
        xT = sb("xT", [P, DT, S])
        hT = sb("hT", [P, FT, S])
        stats = sb("stats", [P, QT, 6])
        mv = sb("mv", [P, QT, 2])
        scratch = sb("scratch", [P, 3, QT])
        X = [env.ps(f"X{i}", [P, S]) for i in range(DT)]
        H = [env.ps(f"H{i}", [P, S]) for i in range(2)]
        Y = [env.ps(f"Y{i}", [P, D]) for i in range(QT)]
        ready = sem("ready")
        xin_in = sem("xin_in")
        xt_full = sem("xt_full")
        xt_done = sem("xt_done")
        h_full = sem("h_full")
        h_done = sem("h_done")
        y_full = sem("y_full")
        y_read = sem("y_read")
        chain = sem("chain")
        block = ctx.enter_context(nc.Block())

        @block.sync
        def _(sp):
            sp.dma_start(xin[:], sh.x_all[:, 0:QT, :]).then_inc(xin_in, 16)
            with sp.Fori(1, B) as b:
                sp.wait_ge(xt_full, b * DT)
                sp.dma_start(xin[:], sh.x_all[:, bass.ds(b * QT, QT), :]).then_inc(xin_in, 16)

        @block.tensor
        def _(pe):
            def transpose_x(b):
                pe.wait_ge(xin_in, b * 16 + 16)
                for dt in range(DT):
                    for qt in range(QT):
                        mm = pe.transpose(X[dt][:, qt * P:(qt + 1) * P], xin[:, qt, dt * P:(dt + 1) * P], sh.ident[:])
                    mm.then_inc(xt_full, 1)

            def body(b, nxt):
                pe.wait_ge(xt_done, b * DT + DT)
                for f in range(FT):
                    pe.wait_ge(h_done, b * FT + (f + 1))
                    for t in range(DT):
                        mm = pe.matmul(H[f % 2][:], w_up[:, t, f * P:(f + 1) * P], xT[:, t, :], start=(t == 0),
                                       stop=(t == DT - 1))
                    mm.then_inc(h_full, 1)
                if nxt:
                    transpose_x(b + 1)
                for qt in range(QT):
                    pe.wait_ge(y_read, b * QT + (qt + 1))
                    for f in range(FT):
                        if qt == 0:
                            pe.wait_ge(h_done, b * FT + (f + 1 + 2))
                        mm = pe.matmul(Y[qt][:], hT[:, f, qt * P:(qt + 1) * P], w_down[:, f, :], start=(f == 0),
                                       stop=False)
                    mm = pe.matmul(Y[qt][:], ones[:], bias_y[:], start=False, stop=True)
                    mm.then_inc(y_full, 1)

            pe.wait_ge(ready, 1)
            transpose_x(0)
            with pe.Fori(0, B - 1) as b:
                body(b, True)
            body(B - 1, False)

        @block.scalar
        def _(act):
            act.sem_inc(h_done, 2)

            def copy_x(b):
                for dt in range(DT):
                    act.wait_ge(xt_full, b * DT + (dt + 1))
                    nc.scalar.activation(xT[:, dt, :], X[dt][:], ACT.Copy).then_inc(xt_done, 1)

            def body(b, nxt):
                for f in range(FT):
                    act.wait_ge(h_full, b * FT + (f + 1))
                    nc.scalar.activation(hT[:, f, :], H[f % 2][:], ACT.Gelu, bias=bias_h[:, f:f + 1]).then_inc(h_done, 1)
                if nxt:
                    copy_x(b + 1)

            copy_x(0)
            with act.Fori(0, B - 1) as b:
                body(b, True)
            body(B - 1, False)

        @block.vector
        def _(dve):
            nc.vector.memset(ones[:], 1.0).then_inc(ready, 1)
            dve.sem_inc(y_read, QT)
            with dve.Fori(0, B) as b:
                for qt in range(QT):
                    dve.wait_ge(y_full, b * QT + (qt + 1))
                    row = sh.x_all[:, b * QT + qt, :]
                    nc.vector.tensor_tensor(row, Y[qt][:], row, ALU.add).then_inc(y_read, 1)
                wait_apart(dve, (ready, 1), (y_read, b * QT + 2 * QT))
                steps = Chain(dve, chain, b * LN_LINKS, (ready, 1))
                advance(layer_norm_rows(nc.vector, steps, lambda qt: sh.x_all[:, b * QT + qt, :], stats, mv, scratch))


TOP = 2
GROUPS = B * QT * TOP
TILES = GROUPS + NE


def moe(nc, sh, w, out):
    with ExitStack() as ctx:
        env = Env(nc, ctx, "moe")
        place = env.sb("place", [P, GROUPS], U32)
        gates = env.sb("gates", [P, B * QT, TOP])
        expert_of = env.sb("expertof", [1, TILES], I32)
        sent = nc.dram_tensor("moe_sent", (TILES * P, D), F32).ap()
        results = nc.dram_tensor("moe_results", (TILES * P, D), F32).ap()
        with ExitStack() as inner:
            env2 = Env(nc, inner, "ex")
            w1 = env2.sb("w1", [P, NE, DT, FH])
            w2 = env2.sb("w2", [P, NE, FT, D])
            w_in = env2.sem("w_in")
            route(nc, sh, w, w1, w2, w_in, place, gates, expert_of, sent)
            experts(nc, sh, w1, w2, w_in, expert_of, sent, results)
        combine(nc, sh, place, gates, results, out)


def route(nc, sh, w, w1, w2, w_in, place, gates, expert_of, sent):
    TEMP = 1.5
    with ExitStack() as ctx:
        env = Env(nc, ctx, "route")
        sb, sem = env.sb, env.sem
        xn_all = sb("xnall", [P, B * QT, D])
        xhat = sb("xhat", [P, QT, D])
        xn_b = sb("xnb", [P, DT, S])
        gamma = sb("gamma", [P, DT])
        beta = sb("beta", [P, DT])
        gamma_r = sb("gammar", [P, D])
        beta_r = sb("betar", [P, D])
        router = sb("router", [P, DT, NE])
        tri = sb("tri", [P, P])
        ones = sb("ones", [P, P])
        iota = sb("iota", [P, TILES])
        zeros = sb("zeros", [P, D])
        BQ = B * QT
        mv = sb("mv", [P, BQ, 2])
        scratch = sb("scratch", [P, 3, BQ])
        logit = env.ps("logit", [P, BQ, NE])
        top = sb("top", [P, BQ, 1])
        picked = sb("picked", [P, GROUPS])
        small = sb("small", [P, 5, NE])
        small_i = sb("smalli", [P, 2, NE], I32)
        X = [env.ps(f"X{i}", [P, QT, P]) for i in range(DT)]
        R = env.ps("R", [P, QT, NE])
        BEFORE = env.ps("before", [P, GROUPS, NE])
        TOTAL = env.ps("all", [P, GROUPS, NE])
        loaded = sem("loaded")
        ready = sem("ready")
        chain = sem("chain")
        xt_full = sem("xt_full")
        xt_done = sem("xt_done")
        routed = sem("routed")
        normal = sem("normal")
        read = sem("read")
        exped = sem("exped")
        scaled = sem("scaled")
        rows = sem("rows")
        shifted = sem("shifted")
        counted = sem("counted")
        cleared = sem("cleared")
        arrived = sem("arrived")
        block = ctx.enter_context(nc.Block())
        LOADS = 7

        @block.sync
        def _(sp):
            sp.dma_start(gamma[:], w["gamma"]).then_inc(loaded, 16)
            sp.dma_start(beta[:], w["beta"]).then_inc(loaded, 16)
            sp.dma_start(gamma_r[:], w["gamma_row"].to_broadcast([P, D])).then_inc(loaded, 16)
            sp.dma_start(beta_r[:], w["beta_row"].to_broadcast([P, D])).then_inc(loaded, 16)
            sp.dma_start(router[:], w["router_wT"].rearrange("(t p) e -> p t e", p=P)).then_inc(loaded, 16)
            sp.dma_start(iota[:], w["iota"]).then_inc(loaded, 16)
            sp.dma_start(tri[:], w["tri"]).then_inc(loaded, 16)
            sp.wait_ge(ready, 2)
            sp.dma_start(sent.rearrange("(t p) d -> p t d", p=P),
                         zeros[:].unsqueeze(1).to_broadcast([P, TILES, D])).then_inc(cleared, 16)
            for e in range(NE):
                sp.dma_start(w1[:, e], w["w1"][e].rearrange("(t p) f -> p t f", p=P)).then_inc(w_in, 16)
                sp.dma_start(w2[:, e], w["w2"][e].rearrange("(t p) d -> p t d", p=P)).then_inc(w_in, 16)

        @block.tensor
        def _(pe):
            pe.wait_ge(loaded, 16 * LOADS)
            with pe.Fori(0, B) as b:
                pe.wait_ge(normal, b + 1)
                for dt in range(DT):
                    for qt in range(QT):
                        mm = pe.transpose(X[dt][:, qt, :], xhat[:, qt, dt * P:(dt + 1) * P], sh.ident[:])
                    mm.then_inc(xt_full, 1)
                pe.wait_ge(xt_done, b * DT + DT)
                for qt in range(QT):
                    for dt in range(DT):
                        mm = pe.matmul(R[:, qt, :], xn_b[:, dt, qt * P:(qt + 1) * P], router[:, dt, :],
                                       start=(dt == 0), stop=(dt == DT - 1))
                mm.then_inc(routed, 1)
            pe.wait_ge(ready, 3)
            chosen = xn_b[:, 0, :]
            pe.matmul(BEFORE[:].rearrange("p g e -> p (g e)"), tri[:], chosen, start=True, stop=True)
            mm = pe.matmul(TOTAL[:].rearrange("p g e -> p (g e)"), ones[:], chosen, start=True, stop=True)
            mm.then_inc(counted, 1)

        @block.scalar
        def _(act):
            act.wait_ge(loaded, 16 * LOADS)
            with act.Fori(0, B) as b:
                for dt in range(DT):
                    act.wait_ge(xt_full, b * DT + (dt + 1))
                    nc.scalar.activation(xn_b[:, dt, :], X[dt][:].rearrange("p a b -> p (a b)"), ACT.Identity,
                                         bias=beta[:, dt:dt + 1], scale=gamma[:, dt:dt + 1]).then_inc(xt_done, 1)
            act.wait_ge(shifted, 1)
            nc.scalar.activation(logit[:], logit[:], ACT.Exp).then_inc(exped, 1)

        @block.gpsimd
        def _(pool):
            pool.wait_ge(loaded, 16 * LOADS)
            pool.sem_inc(scaled, 1)
            with pool.Fori(0, B) as b:
                wait_apart(pool, (loaded, 16 * LOADS), (normal, b + 1))
                to = xn_all[:, bass.ds(b * QT, QT), :]
                nc.gpsimd.tensor_tensor(to, xhat[:], gamma_r[:].unsqueeze(1).to_broadcast([P, QT, D]),
                                        ALU.mult).then_inc(scaled, 1)
                wait_apart(pool, (loaded, 16 * LOADS), (scaled, b + 2))
                nc.gpsimd.tensor_tensor(to, to, beta_r[:].unsqueeze(1).to_broadcast([P, QT, D]),
                                        ALU.add).then_inc(rows, 1)
            pool.wait_ge(rows, B)
            pool.wait_ge(cleared, 16)
            pool.wait_ge(ready, 4)
            for g in range(GROUPS):
                pool.indirect_dma_start(sent, bass.IndirectOffsetOnAxis(ap=place[:, g:g + 1], axis=0),
                                        xn_all[:, g // TOP, :], None).then_inc(arrived, 16)
            pool.wait_ge(arrived, 16 * GROUPS)

        @block.vector
        def _(dve):
            nv = nc.vector
            nv.memset(ones[:], 1.0).then_inc(ready, 1)
            nv.memset(zeros[:], 0.0).then_inc(ready, 1)
            dve.wait_ge(loaded, 16 * LOADS)
            dve.wait_ge(ready, 2)
            steps = Chain(dve, chain, 0, (ready, 2))
            stats = xhat[:].rearrange("p a b -> p (a b)")[:, 0:BQ * 6].rearrange("p (t n) -> p t n", n=6)
            for t in range(BQ):
                ins = nv.bn_stats(stats[:, t, :], sh.x_all[:, t, :])
            steps.link(ins)
            for t in range(BQ):
                ins = nv.bn_aggr(mv[:, t, :], stats[:, t, :])
            steps.link(ins)
            advance(rsqrt_columns(nv, steps, mv[:, :, 1], scratch))
            steps.settle()
            with dve.Fori(0, B) as b:
                wait_apart(dve, (ready, 2), (scaled, b + 1))
                for qt in range(QT):
                    at = b * QT + qt
                    ins = nv.tensor_scalar(xhat[:, qt, :], sh.x_all[:, at, :], mv[:, bass.ds(at, 1), 0],
                                           scratch[:, 1, bass.ds(at, 1)], ALU.subtract, ALU.mult)
                ins.then_inc(normal, 1)
                dve.wait_ge(routed, b + 1)
                nv.tensor_scalar(logit[:, bass.ds(b * QT, QT), :], R[:], 1.0 / TEMP, None, ALU.mult).then_inc(read, 1)
            dve.wait_ge(read, B)
            steps.link(nv.tensor_reduce(top[:, :, 0], logit[:], AX_X, ALU.max))
            nv.tensor_tensor(logit[:], logit[:], top[:].to_broadcast([P, BQ, NE]), ALU.subtract).then_inc(shifted, 1)
            dve.wait_ge(exped, 1)
            steps.link(nv.tensor_reduce(top[:, :, 0], logit[:], AX_X, ALU.add))
            steps.link(nv.reciprocal(top[:], top[:]))
            steps.link(nv.tensor_tensor(logit[:], logit[:], top[:].to_broadcast([P, BQ, NE]), ALU.mult))
            best = xhat[:, 0, 0:BQ * 8].rearrange("p (t e) -> p t e", e=8)
            index = xhat[:, 1, 0:BQ * 8].bitcast(U32).rearrange("p (t e) -> p t e", e=8)
            wait_apart(dve, (ready, 2), (scaled, B + 1))
            for t in range(BQ):
                ins = nv.max(best[:, t, :], logit[:, t, :])
            steps.link(ins)
            for t in range(BQ):
                ins = nv.max_index(index[:, t, :], best[:, t, :], logit[:, t, :])
            steps.link(ins)
            steps.link(nv.tensor_copy(gates[:], best[:, :, 0:TOP]))
            steps.link(nv.tensor_copy(picked[:].rearrange("p (t k) -> p t k", k=TOP), index[:, :, 0:TOP]))
            chosen, sums = [xn_b[:, i, :].rearrange("p (g e) -> p g e", e=NE) for i in range(2)]
            scan = [xhat[:, 2 * i:2 * i + 2, :].rearrange("p a (g e) -> p (a g) e", e=NE) for i in range(2)]
            by_group = [P, GROUPS, NE]
            nv.tensor_tensor(chosen, picked[:].unsqueeze(2).to_broadcast(by_group),
                             iota[:, 0:NE].unsqueeze(1).to_broadcast(by_group), ALU.is_equal).then_inc(ready, 1)
            dve.wait_ge(counted, 1)
            steps.link(nv.tensor_copy(scan[0], TOTAL[:]))
            at, d = 0, 1
            while d < GROUPS:
                nv.tensor_tensor(scan[1 - at][:, d:, :], scan[at][:, d:, :], scan[at][:, :GROUPS - d, :], ALU.add)
                steps.link(nv.tensor_copy(scan[1 - at][:, :d, :], scan[at][:, :d, :]))
                at, d = 1 - at, 2 * d
            upto = scan[at]
            n, tiles, ends, other, first = [small[:, i, :] for i in range(5)]
            steps.link(nv.tensor_scalar(n, upto[:, GROUPS - 1, :], float(P - 1), None, ALU.add))
            steps.link(nv.tensor_copy(small_i[:, 0, :], n))
            steps.link(nv.tensor_scalar(small_i[:, 1, :], small_i[:, 0, :], 7, None, ALU.arith_shift_right))
            steps.link(nv.tensor_copy(tiles, small_i[:, 1, :]))
            a, c, d = tiles, ends, 1
            for k in range(3):
                nv.tensor_tensor(c[:, d:], a[:, d:], a[:, :NE - d], ALU.add)
                steps.link(nv.tensor_copy(c[:, :d], a[:, :d]))
                a, c, d = (ends, other, 2) if k == 0 else (other, ends, 4)
            steps.link(nv.tensor_tensor(first, ends, tiles, ALU.subtract))
            steps.link(nv.tensor_scalar(first, first, float(P), None, ALU.mult))
            steps.link(nv.tensor_tensor(sums, upto, TOTAL[:], ALU.subtract))
            steps.link(nv.tensor_tensor(sums, sums, BEFORE[:], ALU.add))
            steps.link(nv.tensor_tensor(sums, sums, first.unsqueeze(1).to_broadcast(by_group), ALU.add))
            steps.link(nv.tensor_tensor(sums, sums, chosen, ALU.mult))
            steps.link(nv.tensor_reduce(picked[:], sums, AX_X, ALU.add))
            nv.tensor_copy(place[:], picked[:]).then_inc(ready, 1)
            shape = [1, TILES, NE - 1]
            past = xn_b[0:1, 0, 0:TILES * (NE - 1)].rearrange("p (t e) -> p t e", e=NE - 1)
            steps.link(nv.tensor_tensor(past, iota[0:1].unsqueeze(2).to_broadcast(shape),
                                        ends[0:1, 0:NE - 1].unsqueeze(1).to_broadcast(shape), ALU.is_ge))
            steps.link(nv.tensor_reduce(iota[0:1], past, AX_X, ALU.add))
            steps.link(nv.tensor_copy(expert_of[:], iota[0:1]))


def experts(nc, sh, w1, w2, w_in, expert_of, sent, results):
    with ExitStack() as ctx:
        env = Env(nc, ctx, "experts")
        sb, sem = env.sb, env.sem
        xg = sb("xg", [P, 2, D])
        xgT = sb("xgT", [P, DT, P])
        h = sb("h", [P, FH])
        hT = sb("hT", [P, FT, P])
        y_sb = sb("y", [P, 2, D])
        X = env.ps("X", [P, DT, P])
        H = [env.ps(f"H{i}", [P, 512]) for i in range(2)]
        HT = [env.ps(f"HT{i}", [P, FT // 2, P]) for i in range(2)]
        Y = [env.ps(f"Y{i}", [P, D]) for i in range(2)]
        xg_in = [sem(f"xg_in{i}") for i in range(2)]
        xt_full = sem("xt_full")
        xt_done = sem("xt_done")
        h_full = sem("h_full")
        h_act = sem("h_act")
        ht_full = sem("ht_full")
        ht_done = sem("ht_done")
        y_full = sem("y_full")
        y_done = sem("y_done")
        stored = [sem(f"stored{i}") for i in range(2)]
        doubled = sem("doubled")
        block = ctx.enter_context(nc.Block())

        def steps(eng, step):
            for parity in range(2):
                step(0, parity, parity == 0, True)
            with eng.Fori(1, TILES // 2 - 1) as pair:
                for parity in range(2):
                    step(pair, parity, False, True)
            for parity in range(2):
                step(TILES // 2 - 1, parity, False, parity == 0)

        def tile_rows(a, i):
            return a[i * P:(i + 1) * P, :] if isinstance(i, int) else a[bass.ds(i * P, P), :]

        @block.sync
        def _(sp):
            sp.dma_start(xg[:, 0, :], tile_rows(sent, 0)).then_inc(xg_in[0], 16)
            sp.dma_start(xg[:, 1, :], tile_rows(sent, 1)).then_inc(xg_in[1], 16)

            def store(i, parity):
                sp.wait_ge(y_done, i + 1 + 2)
                sp.dma_start(tile_rows(results, i), y_sb[:, parity, :]).then_inc(stored[parity], 16)

            def step(pair, parity, first, more):
                i = pair * 2 + parity
                if not first:
                    store(i - 1, 1 - parity)
                if not (isinstance(i, int) and i + 2 >= TILES):
                    sp.wait_ge(xt_full, i + 1)
                    sp.dma_start(xg[:, parity, :], tile_rows(sent, i + 2)).then_inc(xg_in[parity], 16)

            steps(sp, step)
            store(TILES - 1, 1)
            for i in range(2):
                sp.wait_ge(stored[i], 16 * (TILES // 2 + 1))

        @block.tensor
        def _(pe):
            def expert(i):
                return pe.value_load(expert_of[0:1, i:i + 1] if isinstance(i, int) else
                                     expert_of[0:1, bass.ds(i, 1)], min_val=0, max_val=NE - 1)

            def transpose_rows(parity, turn):
                pe.wait_ge(xg_in[parity], turn * 16)
                for dt in range(DT):
                    mm = pe.transpose(X[:, dt, :], xg[:, parity, dt * P:(dt + 1) * P], sh.ident[:])
                mm.then_inc(xt_full, 1)

            def down(i, parity):
                e = expert(i)
                pe.wait_ge(ht_done, i * 2 + 2)
                pe.wait_ge(y_done, i + 1)
                for f in range(FT):
                    mm = pe.matmul(Y[parity][:], hT[:, f, :], w2[:, bass.ds(e, 1), f, :].rearrange("p a d -> p (a d)"),
                                   start=(f == 0), stop=(f == FT - 1))
                mm.then_inc(y_full, 1)

            def step(pair, parity, first, more):
                i = pair * 2 + parity
                e = expert(i)
                pe.wait_ge(xt_done, i + 1)
                pe.wait_ge(h_act, i * 2 + 2)
                for half in range(2):
                    for dt in range(DT):
                        mm = pe.matmul(H[half][:], xgT[:, dt, :],
                                       w1[:, bass.ds(e, 1), dt, half * 512:(half + 1) * 512]
                                       .rearrange("p a f -> p (a f)"), start=(dt == 0), stop=(dt == DT - 1))
                    mm.then_inc(h_full, 1)
                if not first:
                    down(i - 1, 1 - parity)
                for half in range(2):
                    pe.wait_ge(h_act, i * 2 + (half + 1 + 2))
                    for j in range(FT // 2):
                        f = half * (FT // 2) + j
                        mm = pe.transpose(HT[half][:, j, :], h[:, f * P:(f + 1) * P], sh.ident[:])
                    mm.then_inc(ht_full, 1)
                if more:
                    transpose_rows(1 - parity, pair + (parity + 1))

            pe.wait_ge(w_in, 16 * 2 * NE)
            transpose_rows(0, 1)
            steps(pe, step)
            down(TILES - 1, 1)

        @block.scalar
        def _(act):
            act.sem_inc(h_act, 2)

            def copy_rows(i):
                act.wait_ge(xt_full, i + 1)
                nc.scalar.activation(xgT[:], X[:], ACT.Copy).then_inc(xt_done, 1)

            def step(pair, parity, first, more):
                i = pair * 2 + parity
                for half in range(2):
                    act.wait_ge(h_full, i * 2 + (half + 1))
                    nc.scalar.activation(h[:, half * 512:(half + 1) * 512], H[half][:], ACT.Silu).then_inc(h_act, 1)
                if more:
                    copy_rows(i + 1)

            copy_rows(0)
            steps(act, step)

        @block.vector
        def _(dve):
            dve.sem_inc(y_done, 2)
            for parity in range(2):
                dve.sem_inc(stored[parity], 16)
            nc.vector.tensor_scalar(sh.x_all[:], sh.x_all[:], 2.0, None, ALU.mult).then_inc(doubled, 1)

            def result(i, parity, turn):
                dve.wait_ge(stored[parity], turn * 16)
                dve.wait_ge(y_full, i + 1)
                nc.vector.tensor_copy(y_sb[:, parity, :], Y[parity][:]).then_inc(y_done, 1)

            def step(pair, parity, first, more):
                i = pair * 2 + parity
                if not first:
                    result(i - 1, 1 - parity, pair + parity)
                for half in range(2):
                    dve.wait_ge(ht_full, i * 2 + (half + 1))
                    nc.vector.tensor_copy(hT[:, half * (FT // 2):(half + 1) * (FT // 2), :],
                                          HT[half][:]).then_inc(ht_done, 1)

            steps(dve, step)
            result(TILES - 1, 1, TILES // 2)
            dve.wait_ge(doubled, 1)


def combine(nc, sh, place, gates, results, out):
    with ExitStack() as ctx:
        env = Env(nc, ctx, "combine")
        sb, sem = env.sb, env.sem
        got = sb("got", [P, 2, QT * TOP, D])
        stats = sb("stats", [P, QT, 6])
        mv = sb("mv", [P, QT, 2])
        scratch = sb("scratch", [P, 3, QT])
        ready = sem("ready")
        fetched = [sem(f"fetched{i}") for i in range(2)]
        added = sem("added")
        chain = sem("chain")
        stored = sem("stored")
        block = ctx.enter_context(nc.Block())
        G = QT * TOP

        @block.gpsimd
        def _(pool):
            for b in range(B):
                if b >= 2:
                    pool.wait_ge(added, TOP * (b - 1))
                for g in range(G):
                    pool.indirect_dma_start(got[:, b % 2, g, :], None, results,
                                            bass.IndirectOffsetOnAxis(ap=place[:, b * G + g:b * G + g + 1], axis=0))\
                        .then_inc(fetched[b % 2], 16)

        @block.sync
        def _(sp):
            with sp.Fori(0, B) as b:
                sp.wait_ge(chain, (b + 1) * LN_LINKS)
                sp.dma_start(out[bass.ds(b, 1)].rearrange("b (q p) d -> p (b q) d", p=P),
                             sh.x_all[:, bass.ds(b * QT, QT), :]).then_inc(stored, 16)
            sp.wait_ge(stored, 16 * B)

        @block.vector
        def _(dve):
            nc.vector.memset(scratch[:], 0.0).then_inc(ready, 1)
            dve.wait_ge(ready, 1)
            with dve.Fori(0, B // 2) as pair:
                for parity in range(2):
                    b = pair * 2 + parity
                    dve.wait_ge(fetched[parity], pair * 16 * G + 16 * G)
                    for k in range(TOP):
                        for qt in range(QT):
                            row = sh.x_all[:, b * QT + qt, :]
                            ins = nc.vector.scalar_tensor_tensor(out=row, in0=got[:, parity, qt * TOP + k, :],
                                                                 scalar=gates[:, b * QT + qt, k:k + 1], in1=row,
                                                                 op0=ALU.mult, op1=ALU.add)
                        ins.then_inc(added, 1)
                        wait_apart(dve, (ready, 1), (added, pair * 2 * TOP + (parity * TOP + k + 1)))
                    steps = Chain(dve, chain, b * LN_LINKS, (ready, 1))
                    advance(layer_norm_rows(nc.vector, steps, lambda qt: sh.x_all[:, b * QT + qt, :], stats, mv,
                                            scratch))


_INS = ("x", "ident", "decay", "causal", "cos", "sin", "head_mask4", "head_mask8", "iota", "tri", "ctx", "ctxT", "mask",
        "a0_w_q", "a0_w_kT", "a0_w_vT", "a0_w_down", "a0_w_up_k", "a0_w_up_v", "a0_w_o",
        "f0_w_exp", "f0_b_exp", "f0_up_weights", "f0_up_bias", "f0_down_weights", "f0_w_conT", "f0_b_con",
        "f0_down_bias",
        "a1_w_q", "a1_w_q_swapped", "a1_w_down", "a1_w_up_k", "a1_w_up_k_swapped", "a1_w_up_v", "a1_w_o",
        "x1_w_q", "x1_w_k1", "x1_w_v1", "x1_w_k2", "x1_w_v2", "x1_w_o", "x1_b_o",
        "f1_gamma", "f1_beta", "f1_gamma_row", "f1_beta_row", "f1_router_wT", "f1_w1", "f1_w2")


def decoder(nc, *args):
    w, out = dict(zip(_INS, args)), args[-1]

    def part(prefix, **more):
        return {n[len(prefix):]: a for n, a in w.items() if n.startswith(prefix)} | more

    with ExitStack() as ctx:
        sh = Shared(nc, ctx)
        load_block(nc, sh, w["x"], w["ident"])
        attention(nc, sh, "a0", part("a0_", decay=w["decay"], head_mask=w["head_mask4"]))
        cross_attention_heads(nc, sh, {n: w[n] for n in ("ctx", "ctxT", "mask", "head_mask8")})
        butterfly_ffn(nc, sh, part("f0_"))
        attention(nc, sh, "a1", part("a1_", causal=w["causal"], cos=w["cos"], sin=w["sin"]))
        attention(nc, sh, "x1", part("x1_", ctxT=w["ctxT"]))
        moe(nc, sh, part("f1_", iota=w["iota"], tri=w["tri"]), out)


def shape_constants():
    f = np.float32
    p = np.arange(P)
    far = np.abs(p[:, None] - (np.arange(2 * S - P)[None, :] - (S - P))).astype(f)
    key = np.arange(S)[None, :] - (S - P)
    inv_freq = f(1) / f(10000.0) ** (np.arange(0, 64, 2, dtype=f) / f(64))
    angle = np.arange(S, dtype=f)[:, None] * inv_freq[None, :]
    angle = np.concatenate([angle, angle], 1)
    cos, sin = np.cos(angle).T, np.sin(angle).T.copy()
    sin[:32] *= -1
    return {"ident": np.eye(P, dtype=f),
            "decay": np.exp(f(-0.01) * far),
            "causal": np.where(key <= p[:, None], f(0), f(-1e30)),
            "cos": np.concatenate([cos, cos]), "sin": np.concatenate([sin, sin]),
            "head_mask4": ((p[:, None] % 64) // 16 == np.arange(4)[None, :]).astype(f),
            "head_mask8": (p[:, None] // 16 == np.arange(8)[None, :]).astype(f),
            "iota": np.tile(np.arange(TILES, dtype=f), (P, 1)),
            "tri": np.triu(np.ones((P, P), f), 1)}


def laid_out(a):
    def split_pairs(wt):
        n = wt.shape[0]
        return wt.reshape(n, 2, 4, 2, 16).transpose(0, 1, 3, 2, 4).reshape(n, 4, 64)

    def swapped(wt):
        n = wt.shape[0]
        return wt.reshape(n, -1, 2, 32)[:, :, ::-1].reshape(n, -1)

    row = (1, -1)
    wq1, wku1 = a["L1_attn_wq"].T, a["L1_attn_w_k_up"].T
    return {"x": a["x"], "ctx": a["ctx_1024"], "ctxT": a["ctx_1024"].transpose(0, 2, 1), "mask": a["mask_BxSxS2_ik1"],
            "a0_w_q": split_pairs(a["L0_attn_W_q"]), "a0_w_kT": a["L0_attn_W_k"].T, "a0_w_vT": a["L0_attn_W_v"].T,
            "a0_w_down": a["L0_attn_W_down_kv"], "a0_w_up_k": split_pairs(a["L0_attn_W_up_k"]),
            "a0_w_up_v": a["L0_attn_W_up_v"], "a0_w_o": a["L0_attn_W_o"],
            "f0_w_exp": a["L0_ffn_W_exp"], "f0_b_exp": a["L0_ffn_b_exp"].reshape(row),
            "f0_up_weights": a["L0_ffn_up_weights"].reshape(STAGES, 1, 2 * FH),
            "f0_up_bias": a["L0_ffn_up_bias"].reshape(row),
            "f0_down_weights": a["L0_ffn_down_weights"].reshape(STAGES, 1, 2 * FH),
            "f0_w_conT": a["L0_ffn_W_con"].T, "f0_b_con": a["L0_ffn_b_con"].reshape(row),
            "f0_down_bias": a["L0_ffn_down_bias"].reshape(row),
            "a1_w_q": wq1, "a1_w_q_swapped": swapped(wq1), "a1_w_down": a["L1_attn_w_kv_down"].T,
            "a1_w_up_k": wku1, "a1_w_up_k_swapped": swapped(wku1), "a1_w_up_v": a["L1_attn_w_v_up"].T,
            "a1_w_o": a["L1_attn_wo"].T,
            "x1_w_q": a["L1_xattn_Wq1"], "x1_w_k1": a["L1_xattn_Wk1"], "x1_w_v1": a["L1_xattn_Wv1"],
            "x1_w_k2": a["L1_xattn_Wk2"], "x1_w_v2": a["L1_xattn_Wv2"], "x1_w_o": a["L1_xattn_Wo"],
            "x1_b_o": a["L1_xattn_bo"].reshape(row),
            "f1_gamma": a["L1_ffn_gamma"].reshape(DT, P).T, "f1_beta": a["L1_ffn_beta"].reshape(DT, P).T,
            "f1_gamma_row": a["L1_ffn_gamma"].reshape(row), "f1_beta_row": a["L1_ffn_beta"].reshape(row),
            "f1_router_wT": a["L1_ffn_router_w"].T, "f1_w1": a["L1_ffn_W1"], "f1_w2": a["L1_ffn_W2"]}


def kernel(**inputs):
    import concourse.bacc as bacc
    from concourse.bass_utils import run_bass_kernel_spmd

    host = laid_out({n: np.asarray(a) for n, a in inputs.items()}) | shape_constants()
    nc = bacc.Bacc("TRN2", target_bir_lowering=False, num_devices=1)
    arrays, args = {}, []
    for name in _INS:
        a = np.ascontiguousarray(host[name])
        arrays[f"in_{name}_dram"] = a
        args.append(nc.dram_tensor(f"in_{name}_dram", a.shape, mybir.dt.from_np(a.dtype), kind="ExternalInput").ap())
    args.append(nc.dram_tensor("out_dram", (B, S, D), F32, kind="ExternalOutput").ap())
    decoder(nc, *args)
    r = run_bass_kernel_spmd(nc, [arrays], core_ids=[0])
    return r.results[0]["out_dram"]
```
